# Optimizing a Trainium2 kernel written in Bass

```python
import numpy as np
import jax
import jax.numpy as jnp

def _softmax(x, axis=-1):
    return jax.nn.softmax(x, axis=axis)
def _gelu(x):
    return jax.nn.gelu(x, approximate=True)
def _silu(x):
    return jax.nn.silu(x)
def _sigmoid(x):
    return jax.nn.sigmoid(x)
def _layernorm(x, axis=-1, eps=1e-5):
    m = jnp.mean(x, axis=axis, keepdims=True)
    v = jnp.var(x, axis=axis, keepdims=True)
    return (x - m) / jnp.sqrt(v + eps)
def _scatter_add(tgt, idx, src, axis=0):
    return tgt.at[idx].add(src)
def _segment_sum(src, seg, n):
    return jax.ops.segment_sum(src, seg, n)

kernel_name = 'mk_metaformer_d2_conv_nhwc128_4fb9d3'

def setup_inputs(seed: int = 0):
    np.random.seed(seed)
    _w = jnp.asarray
    def _rec_inputs():
        import jax
        import jax.numpy as jnp
        _gk = jax.random.key(seed)
        x = 7.22e-05 + 1 * jax.random.normal(jax.random.fold_in(_gk, 1), (1, 256, 256, 128), jnp.float32)
        return x
    x = _rec_inputs()
    def _L0_conv_setup():
        import jax, jax.numpy as jnp
        import numpy as np
        C_Z = 128
        N_HEADS = 4
        HEAD_DIM = 32
        TOTAL = N_HEADS * HEAD_DIM
        B, N = (1, 256)
        key = jax.random.key(seed)
        ks = jax.random.split(key, 10)
        s = lambda k, sh: jax.random.normal(k, sh, dtype=jnp.float32) * 0.02
        return {'pair_representation': jax.random.normal(ks[0], (B, N, N, C_Z), dtype=jnp.float32), 'ln_gamma': jnp.ones((C_Z,), jnp.float32), 'ln_beta': jnp.zeros((C_Z,), jnp.float32), 'Wq': s(ks[1], (C_Z, TOTAL)), 'Wk': s(ks[2], (C_Z, TOTAL)), 'Wv': s(ks[3], (C_Z, TOTAL)), 'Wb': s(ks[4], (C_Z, N_HEADS)), 'Wg': s(ks[5], (C_Z, TOTAL)), 'bg': jnp.zeros((TOTAL,), jnp.float32), 'Wo': s(ks[6], (TOTAL, C_Z)), 'bo': jnp.zeros((C_Z,), jnp.float32)}
    _L0_conv_all = _L0_conv_setup()
    _L0_conv_in = {k: v for k, v in _L0_conv_all.items() if k in ('ln_gamma', 'ln_beta', 'Wq', 'Wk', 'Wv', 'Wb', 'Wg', 'bg', 'Wo', 'bo', )}
    del _L0_conv_all

    def _L0_ffn_setup():
        import jax, jax.numpy as jnp
        import numpy as np
        B, S, D, E, H, O, K = (512, 2048, 128, 64, 512, 128, 8)
        key = jax.random.key(seed)
        k0, k1, k2, k3 = jax.random.split(key, 4)
        x = jax.random.normal(k0, (B, S, D), dtype=jnp.float32)
        gate_w = jax.random.normal(k1, (E, D), dtype=jnp.float32) * (1.0 / np.sqrt(D))
        gate_b = jnp.zeros((E,), dtype=jnp.float32)
        weight1 = jax.random.uniform(k2, (E, D + 1, H), dtype=jnp.float32, minval=-1.0, maxval=1.0) * (1.0 / np.sqrt(D + 1))
        weight2 = jax.random.uniform(k3, (E, H + 1, O), dtype=jnp.float32, minval=-1.0, maxval=1.0) * (1.0 / np.sqrt(H + 1))
        return {'x': x, 'gate_w': gate_w, 'gate_b': gate_b, 'weight1': weight1, 'weight2': weight2}
    _L0_ffn_all = _L0_ffn_setup()
    _L0_ffn_in = {k: v for k, v in _L0_ffn_all.items() if k in ('gate_w', 'gate_b', 'weight1', 'weight2', )}
    del _L0_ffn_all

    def _L1_conv_setup():
        import jax, jax.numpy as jnp
        import numpy as np
        LN_EPS = 1e-05

        def _layer_norm(h, g, b):
            mu = jnp.mean(h, axis=-1, keepdims=True)
            var = jnp.mean(jnp.square(h - mu), axis=-1, keepdims=True)
            return (h - mu) * jax.lax.rsqrt(var + LN_EPS) * g + b

        def _forward_fourier(x, w1, w2):
            xt = jnp.transpose(x, (0, 3, 1, 2))
            B, I, M, N = xt.shape
            nm = w1.shape[2]
            cw1 = w1[..., 0] + 1j * w1[..., 1]
            cw2 = w2[..., 0] + 1j * w2[..., 1]
            O = cw1.shape[1]
            fty = jnp.fft.rfft(xt, axis=-1, norm='ortho')
            f1 = jnp.einsum('bixy,ioy->boxy', fty[..., :nm], cw1)
            pad_y = jnp.zeros((B, O, M, N // 2 + 1 - nm), dtype=f1.dtype)
            xy = jnp.fft.irfft(jnp.concatenate([f1, pad_y], axis=-1), n=N, axis=-1, norm='ortho')
            ftx = jnp.fft.rfft(xt, axis=-2, norm='ortho')
            f2 = jnp.einsum('bixy,iox->boxy', ftx[:, :, :nm, :], cw2)
            pad_x = jnp.zeros((B, O, M // 2 + 1 - nm, N), dtype=f2.dtype)
            xx = jnp.fft.irfft(jnp.concatenate([f2, pad_x], axis=-2), n=M, axis=-2, norm='ortho')
            return jnp.transpose(xx + xy, (0, 2, 3, 1))
        key = jax.random.key(seed)
        ks = jax.random.split(key, 6)
        B, M, N, D = (16, 128, 128, 128)
        NM, H = (16, 512)
        xav = float(np.sqrt(2.0 / (D + D)))
        return {'x': jax.random.normal(ks[0], (B, M, N, D), jnp.float32), 'w1': jax.random.normal(ks[1], (D, D, NM, 2), jnp.float32) * xav, 'w2': jax.random.normal(ks[2], (D, D, NM, 2), jnp.float32) * xav, 'ff_w0': jax.random.normal(ks[3], (D, H), jnp.float32) * float(1.0 / np.sqrt(D)), 'ff_b0': jnp.zeros((H,), jnp.float32), 'ff_w1': jax.random.normal(ks[4], (H, D), jnp.float32) * float(1.0 / np.sqrt(H)), 'ff_b1': jnp.zeros((D,), jnp.float32), 'ln_g': jnp.ones((D,), jnp.float32), 'ln_b': jnp.zeros((D,), jnp.float32)}
    _L1_conv_all = _L1_conv_setup()
    _L1_conv_in = {k: v for k, v in _L1_conv_all.items() if k in ('w1', 'w2', 'ff_w0', 'ff_b0', 'ff_w1', 'ff_b1', 'ln_g', 'ln_b', )}
    del _L1_conv_all

    def _L1_ffn_setup():
        import jax, jax.numpy as jnp
        import numpy as np
        B, N, D, C, E, K = (8, 8192, 128, 128, 8, 2)
        key = jax.random.key(seed)
        k0, k1, k2 = jax.random.split(key, 3)
        x = jax.random.normal(k0, (B, N, D), dtype=jnp.float32)
        router_w = jax.random.normal(k1, (D, E), dtype=jnp.float32) * 0.05
        router_b = jnp.zeros((E,), dtype=jnp.float32)
        expert_w = jax.random.normal(k2, (E, D, C), dtype=jnp.float32) * (1.0 / np.sqrt(D))
        expert_b = jnp.zeros((E, C), dtype=jnp.float32)
        return {'x': x, 'router_w': router_w, 'router_b': router_b, 'expert_w': expert_w, 'expert_b': expert_b}
    _L1_ffn_all = _L1_ffn_setup()
    _L1_ffn_in = {k: v for k, v in _L1_ffn_all.items() if k in ('router_w', 'router_b', 'expert_w', 'expert_b', )}
    del _L1_ffn_all

    return {
        "x": x,
        "L0_conv_ln_gamma": _L0_conv_in["ln_gamma"],
        "L0_conv_ln_beta": _L0_conv_in["ln_beta"],
        "L0_conv_Wq": _L0_conv_in["Wq"],
        "L0_conv_Wk": _L0_conv_in["Wk"],
        "L0_conv_Wv": _L0_conv_in["Wv"],
        "L0_conv_Wb": _L0_conv_in["Wb"],
        "L0_conv_Wg": _L0_conv_in["Wg"],
        "L0_conv_bg": _L0_conv_in["bg"],
        "L0_conv_Wo": _L0_conv_in["Wo"],
        "L0_conv_bo": _L0_conv_in["bo"],
        "L0_ffn_gate_w": _L0_ffn_in["gate_w"],
        "L0_ffn_gate_b": _L0_ffn_in["gate_b"],
        "L0_ffn_weight1": _L0_ffn_in["weight1"],
        "L0_ffn_weight2": _L0_ffn_in["weight2"],
        "L1_conv_w1": _L1_conv_in["w1"],
        "L1_conv_w2": _L1_conv_in["w2"],
        "L1_conv_ff_w0": _L1_conv_in["ff_w0"],
        "L1_conv_ff_b0": _L1_conv_in["ff_b0"],
        "L1_conv_ff_w1": _L1_conv_in["ff_w1"],
        "L1_conv_ff_b1": _L1_conv_in["ff_b1"],
        "L1_conv_ln_g": _L1_conv_in["ln_g"],
        "L1_conv_ln_b": _L1_conv_in["ln_b"],
        "L1_ffn_router_w": _L1_ffn_in["router_w"],
        "L1_ffn_router_b": _L1_ffn_in["router_b"],
        "L1_ffn_expert_w": _L1_ffn_in["expert_w"],
        "L1_ffn_expert_b": _L1_ffn_in["expert_b"],
    }

def reference(x, L0_conv_ln_gamma, L0_conv_ln_beta, L0_conv_Wq, L0_conv_Wk, L0_conv_Wv, L0_conv_Wb, L0_conv_Wg, L0_conv_bg, L0_conv_Wo, L0_conv_bo, L0_ffn_gate_w, L0_ffn_gate_b, L0_ffn_weight1, L0_ffn_weight2, L1_conv_w1, L1_conv_w2, L1_conv_ff_w0, L1_conv_ff_b0, L1_conv_ff_w1, L1_conv_ff_b1, L1_conv_ln_g, L1_conv_ln_b, L1_ffn_router_w, L1_ffn_router_b, L1_ffn_expert_w, L1_ffn_expert_b):
    import jax
    import jax.numpy as jnp
    def _L0_conv_ref(pair_representation, ln_gamma, ln_beta, Wq, Wk, Wv, Wb, Wg, bg, Wo, bo):
        import jax, jax.numpy as jnp
        import numpy as np
        C_Z = 128
        N_HEADS = 4
        HEAD_DIM = 32
        TOTAL = N_HEADS * HEAD_DIM
        B, N = (1, 256)
        x = pair_representation
        mu = jnp.mean(x, axis=-1, keepdims=True)
        var = jnp.mean((x - mu) ** 2, axis=-1, keepdims=True)
        x = (x - mu) * jax.lax.rsqrt(var + 1e-05) * ln_gamma + ln_beta
        b, n, _, _ = x.shape
        split = lambda t: t.reshape(b, n, n, N_HEADS, HEAD_DIM)
        Q = split(x @ Wq)
        K = split(x @ Wk)
        V = split(x @ Wv)
        G = jax.nn.sigmoid(split(x @ Wg + bg))
        Bias = x @ Wb
        scores = jnp.einsum('bijhd,bikhd->bijkh', Q, K) / np.float32(np.sqrt(HEAD_DIM))
        scores = scores + Bias[:, None]
        attn = jax.nn.softmax(scores, axis=3)
        vals = jnp.einsum('bijkh,bikhd->bijhd', attn, V)
        vals = (G * vals).reshape(b, n, n, TOTAL)
        return vals @ Wo + bo

    def _L0_ffn_ref(x, gate_w, gate_b, weight1, weight2):
        import jax, jax.numpy as jnp
        import numpy as np
        B, S, D, E, H, O, K = (512, 2048, 128, 64, 512, 128, 8)
        Bn, Sn, Dn = x.shape
        logits = jnp.einsum('bsd,ed->bse', x, gate_w) + gate_b
        probs = jax.nn.softmax(logits, axis=1)
        vals, idx = jax.lax.top_k(probs.transpose(0, 2, 1), K)
        topv = vals.transpose(0, 2, 1)
        topi = idx.transpose(0, 2, 1)
        flat_idx = topi.reshape(Bn, K * E)
        gathered = jnp.take_along_axis(x, flat_idx[:, :, None], axis=1)
        gathered = gathered.reshape(Bn, K, E, Dn)
        pooled = jnp.einsum('bked,bke->bed', gathered, topv)
        ones = jnp.ones((E, Bn, 1), dtype=x.dtype)
        h = jnp.concatenate([pooled.transpose(1, 0, 2), ones], axis=-1)
        h = jax.nn.gelu(jnp.einsum('ebd,edh->ebh', h, weight1), approximate=False)
        h = jnp.concatenate([h, ones], axis=-1)
        out = jnp.einsum('ebh,eho->ebo', h, weight2)
        out = out.transpose(1, 0, 2)
        weighted = jnp.einsum('beo,bke->bkeo', out, topv).reshape(Bn, K * E, O)
        outputs = jnp.zeros((Bn, Sn, O), dtype=x.dtype)
        outputs = outputs.at[jnp.arange(Bn)[:, None], flat_idx].add(weighted)
        return outputs

    def _L1_conv_ref(x, w1, w2, ff_w0, ff_b0, ff_w1, ff_b1, ln_g, ln_b):
        import jax, jax.numpy as jnp
        import numpy as np
        LN_EPS = 1e-05

        def _layer_norm(h, g, b):
            mu = jnp.mean(h, axis=-1, keepdims=True)
            var = jnp.mean(jnp.square(h - mu), axis=-1, keepdims=True)
            return (h - mu) * jax.lax.rsqrt(var + LN_EPS) * g + b

        def _forward_fourier(x, w1, w2):
            xt = jnp.transpose(x, (0, 3, 1, 2))
            B, I, M, N = xt.shape
            nm = w1.shape[2]
            cw1 = w1[..., 0] + 1j * w1[..., 1]
            cw2 = w2[..., 0] + 1j * w2[..., 1]
            O = cw1.shape[1]
            fty = jnp.fft.rfft(xt, axis=-1, norm='ortho')
            f1 = jnp.einsum('bixy,ioy->boxy', fty[..., :nm], cw1)
            pad_y = jnp.zeros((B, O, M, N // 2 + 1 - nm), dtype=f1.dtype)
            xy = jnp.fft.irfft(jnp.concatenate([f1, pad_y], axis=-1), n=N, axis=-1, norm='ortho')
            ftx = jnp.fft.rfft(xt, axis=-2, norm='ortho')
            f2 = jnp.einsum('bixy,iox->boxy', ftx[:, :, :nm, :], cw2)
            pad_x = jnp.zeros((B, O, M // 2 + 1 - nm, N), dtype=f2.dtype)
            xx = jnp.fft.irfft(jnp.concatenate([f2, pad_x], axis=-2), n=M, axis=-2, norm='ortho')
            return jnp.transpose(xx + xy, (0, 2, 3, 1))
        h = _forward_fourier(x, w1, w2)
        h1 = jax.nn.relu(jnp.einsum('bmni,ih->bmnh', h, ff_w0) + ff_b0)
        h2 = jnp.einsum('bmnh,ho->bmno', h1, ff_w1) + ff_b1
        return _layer_norm(h2, ln_g, ln_b)

    def _L1_ffn_ref(x, router_w, router_b, expert_w, expert_b):
        import jax, jax.numpy as jnp
        import numpy as np
        B, N, D, C, E, K = (8, 8192, 128, 128, 8, 2)
        router_probs = jax.nn.softmax(x @ router_w + router_b, axis=-1)
        top_p, top_i = jax.lax.top_k(router_probs, K)
        top_p = top_p / jnp.sum(top_p, axis=-1, keepdims=True)
        expert_out = jnp.einsum('bnd,edc->bnec', x, expert_w) + expert_b
        gathered = jnp.take_along_axis(expert_out, top_i[..., None], axis=2)
        return jnp.einsum('bnk,bnkc->bnc', top_p, gathered)

    def _gn(v, G=32, eps=1e-5):
        B_, H_, W_, C_ = v.shape
        g = v.reshape(B_, H_, W_, G, C_ // G)
        m = jnp.mean(g, axis=(1, 2, 4), keepdims=True)
        s = jnp.var(g, axis=(1, 2, 4), keepdims=True)
        return ((g - m) / jnp.sqrt(s + eps)).reshape(v.shape)

    def _ln_c(v, eps=1e-6):
        m = jnp.mean(v, axis=-1, keepdims=True)
        s = jnp.var(v, axis=-1, keepdims=True)
        return (v - m) / jnp.sqrt(s + eps)

    def _ln_t(v, eps=1e-5):
        m = jnp.mean(v, axis=-1, keepdims=True)
        s = jnp.var(v, axis=-1, keepdims=True)
        return (v - m) / jnp.sqrt(s + eps)

    def _to_tokens(v):
        B_, H_, W_, C_ = v.shape
        return v.reshape(B_, H_ * W_, C_)
    def _from_tokens(t, like):
        return t.reshape(like.shape)

    x = x + _L0_conv_ref(_ln_c(x), L0_conv_ln_gamma, L0_conv_ln_beta, L0_conv_Wq, L0_conv_Wk, L0_conv_Wv, L0_conv_Wb, L0_conv_Wg, L0_conv_bg, L0_conv_Wo, L0_conv_bo)
    t = _to_tokens(x)
    t = t + _L0_ffn_ref(_ln_t(t), L0_ffn_gate_w, L0_ffn_gate_b, L0_ffn_weight1, L0_ffn_weight2)
    x = _from_tokens(t, x)
    x = x + _L1_conv_ref(_ln_c(x), L1_conv_w1, L1_conv_w2, L1_conv_ff_w0, L1_conv_ff_b0, L1_conv_ff_w1, L1_conv_ff_b1, L1_conv_ln_g, L1_conv_ln_b)
    t = _to_tokens(x)
    t = t + _L1_ffn_ref(_ln_t(t), L1_ffn_router_w, L1_ffn_router_b, L1_ffn_expert_w, L1_ffn_expert_b)
    x = _from_tokens(t, x)
    return x


_drawn_inputs = setup_inputs


def setup_inputs(seed=0):
    import zlib

    import numpy as np

    out = dict(_drawn_inputs(seed))
    spreads = {'L0_conv_ln_gamma': (1.0, 0.6),
     'L0_conv_ln_beta': (0.0, 0.1),
     'L0_conv_bg': (0.0, 0.8),
     'L0_conv_bo': (0.0, 0.1),
     'L0_ffn_gate_b': (0.0, 0.8),
     'L1_conv_ff_b0': (0.0, 0.1),
     'L1_conv_ff_b1': (0.0, 0.1),
     'L1_conv_ln_g': (1.0, 0.2),
     'L1_conv_ln_b': (0.0, 0.1),
     'L1_ffn_router_b': (0.0, 0.1),
     'L1_ffn_expert_b': (0.0, 0.1)}
    factors = {'L0_conv_Wq': 8.0,
     'L0_conv_Wk': 8.0,
     'L0_conv_Wb': 8.0,
     'L0_conv_Wg': 8.0,
     'L0_ffn_gate_w': 8.0,
     'L0_ffn_weight1': 8.0,
     'L0_ffn_weight2': 8.0}
    for name, (base, spread) in spreads.items():
        noise = np.random.default_rng([zlib.crc32(name.encode()), seed]).standard_normal(out[name].shape)
        drawn = base * np.exp(spread * noise) if base else spread * noise
        out[name] = jnp.asarray(drawn.astype(out[name].dtype))
    for name, factor in factors.items():
        out[name] = (out[name] * factor).astype(out[name].dtype)
    return out
```

```python
from contextlib import ExitStack

import numpy as np

import concourse.bass as bass
from concourse import mybir

F32 = mybir.dt.float32
U32 = mybir.dt.uint32
ALU = mybir.AluOpType
ACT = mybir.ActivationFunctionType
AXX = mybir.AxisListType.X

P = 128
C = 128
N = 256
TOK = N * N
TILES = TOK // P
NH = 4
HD = 32
E0 = 64
K0 = 8
H0 = 512
NM = 16
M2 = 2 * NM
H1 = 512
E1 = 8
LOW = -3.0e38


class Core:

    def __init__(self, nc, ctx, dram):
        self.nc, self.ctx, self.d = nc, ctx, dram
        self.phase_sems = []
        self.passed = nc.alloc_semaphore("passed")

    def sem(self, name):
        handle = self.nc.alloc_semaphore(name)
        self.phase_sems.append(handle)
        return handle

    def end_phase(self):
        self.nc.clear_and_free_semaphores(self.phase_sems)
        self.phase_sems = []
        self.nc.all_engine_barrier()

    def wait_alone(self, eng, sem, value):
        if not (isinstance(value, int) and value <= 0):
            eng.wait_ge(sem, value)
            eng.sem_inc(self.passed, 1)

    def sb(self, ctx, name, shape, dt=F32):
        return ctx.enter_context(self.nc.sbuf_tensor(name, shape, dt))

    def ps(self, ctx, name, shape, dt=F32):
        return ctx.enter_context(self.nc.psum_tensor(name, shape, dt))


def row_of(vector):
    return vector.rearrange("(a n) -> a n", a=1).broadcast_to([P, vector.shape[0]])


def load_constants(k):
    nc, d = k.nc, k.d
    k.ident = k.sb(k.ctx, "ident", [P, P])
    k.gamma = k.sb(k.ctx, "gamma", [C, 1])
    k.beta = k.sb(k.ctx, "beta", [C, 1])
    k.mean = k.sb(k.ctx, "mean", [P, TILES])
    k.rstd = k.sb(k.ctx, "rstd", [P, TILES])
    k.mhalf = k.sb(k.ctx, "mhalf", [P, 16])
    consts_in = k.sem("consts_in")
    half_set = k.sem("half_set")
    with nc.Block() as block:
        @block.sync
        def _(sp):
            sp.dma_start(k.ident[:], d["identity"]).then_inc(consts_in, 16)
            sp.dma_start(k.gamma[:], d["L0_conv_ln_gamma"].rearrange("(c a) -> c a", a=1)).then_inc(consts_in, 16)
            sp.dma_start(k.beta[:], d["L0_conv_ln_beta"].rearrange("(c a) -> c a", a=1)).then_inc(consts_in, 16)
            sp.wait_ge(consts_in, 48)

        @block.gpsimd
        def _(pool):
            nc.gpsimd.memset(k.mhalf[:], -0.5).then_inc(half_set, 1)
            pool.wait_ge(half_set, 1)


def bias_pass(k, bias):
    nc, d = k.nc, k.d
    G = 8
    STEPS = TILES // G
    with ExitStack() as ctx:
        xin = k.sb(ctx, "b_xin", [P, 2, G, C])
        xn = k.sb(ctx, "b_xn", [P, 2, G, C])
        zt = k.sb(ctx, "b_zt", [C, 2, G, P])
        wb = k.sb(ctx, "b_wb", [C, NH])
        stats = k.sb(ctx, "b_stats", [P, 2, G, 6])
        mv = k.sb(ctx, "b_mv", [P, 2, G, 2])
        var = k.sb(ctx, "b_var", [P, 2, G])
        bias_t = k.sb(ctx, "b_bias_t", [P, 2, NH, N])
        ps_t = k.ps(ctx, "b_ps_t", [C, 2, G, P])
        ps_b = k.ps(ctx, "b_ps_b", [P, 2, 512])
        ps_r = k.ps(ctx, "b_ps_r", [P, 2, 2, N])
        wb_in = k.sem("b_wb_in")
        turned, turned_kept, zero_set = k.sem("b_turned"), k.sem("b_turned_kept"), k.sem("b_zero_set")
        pair = lambda name: [k.sem(f"b_{name}{s}") for s in range(2)]
        x_in, stats_done, mv_done, var_done, rstd_done, xn_done = map(
            pair, ("x_in", "stats_done", "mv_done", "var_done", "rstd_done", "xn_done"))
        t_done, zt_done, b_done, b_kept = map(pair, ("t_done", "zt_done", "b_done", "b_kept"))
        x_v = d["x"].rearrange("a i k c -> (a i k) c").rearrange("(n t p) c -> n p t c", t=G, p=P)

        with nc.Block() as block:
            @block.sync
            def _(sp):
                sp.dma_start(wb[:], d["L0_conv_Wb"]).then_inc(wb_in, 16)
                with sp.Fori(0, STEPS // 2) as r:
                    for s in range(2):
                        sp.wait_ge(xn_done[s], r)
                        sp.dma_start(xin[:, s], x_v[r * 2 + s]).then_inc(x_in[s], 16)

            @block.gpsimd
            def _(pool):
                with pool.Fori(0, STEPS // 2) as r:
                    for s in range(2):
                        pool.wait_ge(var_done[s], r + 1)
                        nc.gpsimd.tensor_tensor(k.rstd[:, bass.ds(r * (2 * G) + s * G, G)], var[:, s],
                                                k.mhalf[:, 0:G], ALU.pow).then_inc(rstd_done[s], 1)

            @block.vector
            def _(dve):
                with dve.Fori(0, STEPS // 2) as r:
                    for s in range(2):
                        dve.wait_ge(x_in[s], r * 16 + 16)
                        for t in range(G):
                            ins = nc.vector.bn_stats(stats[:, s, t], xin[:, s, t])
                        ins.then_inc(stats_done[s], 1)
                    for s in range(2):
                        k.wait_alone(dve, stats_done[s], r + 1)
                        for t in range(G):
                            ins = nc.vector.bn_aggr(mv[:, s, t], stats[:, s, t])
                        ins.then_inc(mv_done[s], 1)
                    for s in range(2):
                        dve.wait_ge(mv_done[s], r + 1)
                        nc.vector.tensor_scalar(var[:, s], mv[:, s, :, 1], 1.0 + 1e-5, 1e-11, ALU.mult, ALU.add)\
                            .then_inc(var_done[s], 1)
                        nc.vector.tensor_copy(k.mean[:, bass.ds(r * (2 * G) + s * G, G)], mv[:, s, :, 0])
                    for s in range(2):
                        dve.wait_ge(rstd_done[s], r + 1)
                        dve.wait_ge(t_done[s], r)
                        for t in range(G):
                            ins = nc.vector.tensor_scalar(
                                xn[:, s, t], xin[:, s, t], mv[:, s, t, 0:1],
                                k.rstd[:, bass.ds(r * (2 * G) + (s * G + t), 1)], ALU.subtract, ALU.mult)
                        ins.then_inc(xn_done[s], 1)
                    for s in range(2):
                        dve.wait_ge(b_done[s], r + 1)
                        nc.vector.tensor_copy(
                            bias_t[:, :, :, bass.ds(r * G + s * (G // 2), G // 2)],
                            ps_b[:, s, 0:G * NH].rearrange("p (j b h) -> p b h j", b=2, h=NH)).then_inc(b_kept[s], 1)
                for q in range(2 * NH):
                    dve.wait_ge(turned, q + 1)
                    nc.vector.tensor_copy(bias[:, :, q // 2, (q % 2) * P:(q % 2 + 1) * P],
                                          ps_r[:, q % 2, :, 0:P]).then_inc(turned_kept, 1)

            @block.tensor
            def _(pe):
                pe.wait_ge(wb_in, 16)
                with pe.Fori(0, STEPS // 2) as r:
                    for s in range(2):
                        pe.wait_ge(xn_done[s], r + 1)
                        pe.wait_ge(zt_done[s], r * 2)
                        for t in range(G):
                            ins = nc.tensor.transpose(ps_t[:, s, t], xn[:, s, t], k.ident[:])
                        ins.then_inc(t_done[s], 1)
                    for s in range(2):
                        pe.wait_ge(zt_done[s], r * 2 + 2)
                        pe.wait_ge(b_kept[s], r)
                        for t in range(G):
                            ins = nc.tensor.matmul(ps_b[:, s, t * NH:(t + 1) * NH], zt[:, s, t], wb[:],
                                                   start=True, stop=True)
                        ins.then_inc(b_done[s], 1)
                pe.wait_ge(b_kept[0], STEPS // 2)
                pe.wait_ge(b_kept[1], STEPS // 2)
                for q in range(2 * NH):
                    h, kb = q // 2, q % 2
                    if q >= 2:
                        pe.wait_ge(turned_kept, q - 1)
                    for jb in range(2):
                        ins = nc.tensor.transpose(ps_r[:, q % 2, jb, 0:P], bias_t[:, kb, h, jb * P:(jb + 1) * P],
                                                  k.ident[:])
                    ins.then_inc(turned, 1)

            @block.scalar
            def _(act):
                with act.Fori(0, STEPS // 2) as r:
                    for s in range(2):
                        act.wait_ge(t_done[s], r + 1)
                        act.wait_ge(b_done[s], r)
                        for half in range(2):
                            a, b = half * G // 2, (half + 1) * G // 2
                            nc.scalar.activation(zt[:, s, a:b], ps_t[:, s, a:b], ACT.Identity, bias=k.beta[:, 0:1],
                                                 scale=k.gamma[:, 0:1]).then_inc(zt_done[s], 1)


class Turn:

    def __init__(self, place, lap, of):
        self.place, self.lap, self.of = place, lap, of
        self.s, self.before = place % 2, lap * (of // 2) + place // 2

    def shift(self, by):
        return Turn((self.place + by) % self.of, self.lap + (self.place + by) // self.of, self.of)

    @property
    def index(self):
        return self.lap * self.of + self.place


def wait(eng, sem, value):
    if not (isinstance(value, int) and value <= 0):
        eng.wait_ge(sem, value)


def run_steps(eng, step, first, head, tail, last, of=2):
    for i in range(first, head):
        step(Turn(i % of, i // of, of), i)
    with eng.Fori(0, (tail - head) // of) as r:
        for place in range(of):
            step(Turn(place, r + head // of, of), None)
    for i in range(tail, last):
        step(Turn(i % of, i // of, of), i)


def attention(k, bias):
    nc, d = k.nc, k.d
    SCALE = float(HD) ** -0.25
    B = 2
    with ExitStack() as ctx:
        sb = lambda name, shape: k.sb(ctx, "a_" + name, shape)
        wqk, wg, wv, wo = sb("wqk", [C, 2, C]), sb("wg", [C, C]), sb("wv", [C, C]), sb("wo", [C, C])
        bg, bg_half, bo = sb("bg", [C, 1]), sb("bg_half", [C, 1]), sb("bo", [P, C])
        xr, xn, xo = (sb(n, [P, 2, B, C]) for n in ("xr", "xn", "xo"))
        xb = sb("xb", [P, 4, B, C])
        v = sb("v", [P, 2, B * C])
        zt = sb("zt", [C, 2, N])
        qk = sb("qk", [C, 2, 2, N])
        keys = sb("keys", [C, 2, NH, N])
        g, gate, vals = (sb(n, [C, 2, N]) for n in ("g", "gate", "vals"))
        prob = sb("prob", [P, 2, NH, B, N])
        top, ntop, total, rden = (sb(n, [P, 2, NH, B]) for n in ("top", "ntop", "total", "rden"))
        share = sb("share", [P, 2, B, C])
        pt = sb("pt", [P, NH, B, N])
        ps_s = k.ps(ctx, "a_ps_s", [P, NH, B, N])
        ps_p = k.ps(ctx, "a_ps_p", [P, 2, B, N])
        ps_a = k.ps(ctx, "a_ps_a", [P, 2, N])
        ps_o = k.ps(ctx, "a_ps_o", [P, 2, N])

        pair = lambda name: [k.sem(f"a_{name}{s}") for s in range(2)]
        w_in, ready = k.sem("a_w_in"), k.sem("a_ready")
        x_in, stored = pair("x_in"), pair("stored")
        xn_done, keys_done, top_done, ntop_done, rden_done, pt_even, gate_done, vals_done, xo_done = map(
            pair, ("xn_done", "keys_done", "top_done", "ntop_done", "rden_done", "pt_even", "gate_done", "vals_done", "xo_done"))
        zt_done, qk_kept, tanh_done, v_kept, exp_done, pt_odd = map(
            pair, ("zt_done", "qk_kept", "tanh_done", "v_kept", "exp_done", "pt_odd"))
        t_done, qk_done, gv_done, s_done, pt_done, av_done, share_turned, y_done = map(
            pair, ("t_done", "qk_done", "gv_done", "s_done", "pt_done", "av_done", "share_turned", "y_done"))
        xb_done, share_done = map(pair, ("xb_done", "share_done"))

        x_v = d["x"].rearrange("a i (b p) c -> (a i) p b c", p=P)
        x1_v = d["x1"].rearrange("(i b p) c -> i p b c", b=B, p=P)

        def exists(i, by):
            return i is None or 0 <= i + by < N

        def head(h):
            return slice(h * HD, (h + 1) * HD)

        def sp_step(step, i, sp):
            if exists(i, 2):
                L = step.shift(2)
                k.wait_alone(sp, xn_done[L.s], L.before)
                k.wait_alone(sp, xb_done[L.s], L.before)
                sp.dma_start(xr[:, L.s], x_v[L.index]).then_inc(x_in[L.s], 16)
            if exists(i, -3):
                row = step.shift(-3)
                k.wait_alone(sp, xo_done[row.s], row.before + 1)
                sp.dma_start(x1_v[row.index], xo[:, row.s]).then_inc(stored[row.s], 16)

        def pool_step(step, i, pool):
            L, D = step.shift(2), step.shift(-1)
            if exists(i, -1):
                k.wait_alone(pool, rden_done[D.s], D.before + 1)
                k.wait_alone(pool, share_turned[D.s], D.before)
                nc.gpsimd.tensor_copy(share[:, D.s].rearrange("p b (h c) -> p b h c", h=NH),
                                      rden[:, D.s].rearrange("p h b -> p b h").unsqueeze(3).broadcast_to([P, B, NH, HD]))\
                    .then_inc(share_done[D.s], 1)
            if exists(i, 2):
                wait(pool, x_in[L.s], L.before * 16 + 16)
                wait(pool, xo_done[L.s], L.before - 1)
                nc.gpsimd.tensor_tensor(xb[:, L.place], xr[:, L.s], bo[:].unsqueeze(1).broadcast_to([P, B, C]),
                                        ALU.add).then_inc(xb_done[L.s], 1)

        def dve_step(step, i, dve):
            L, A, R, D, O = (step.shift(by) for by in (2, 1, 0, -1, -2))

            def turned(h):
                wait(dve, pt_done[D.s], D.before * 4 + (h + 1))
                wait(dve, av_done[1 - D.s], D.shift(-1).before + 1)
                nc.vector.tensor_copy(pt[:, h], ps_p[:, 0]).then_inc(pt_even[D.s], 1)

            def scored(h):
                wait(dve, s_done[R.s], R.before * 4 + (h + 1))
                k.wait_alone(dve, pt_done[R.s], R.before * 4)
                for b in range(B):
                    ins = nc.vector.tensor_tensor_reduce(prob[:, R.s, h, b], ps_s[:, h, b], bias[:, b, h], 1.0, LOW,
                                                         ALU.add, ALU.max, top[:, R.s, h, b:b + 1])
                ins.then_inc(top_done[R.s], 1)
                if h % 2:
                    wait(dve, top_done[R.s], R.before * 4 + (h + 1))
                    nc.vector.tensor_scalar(ntop[:, R.s, h - 1:h + 1], top[:, R.s, h - 1:h + 1], -1.0, None, ALU.mult)\
                        .then_inc(ntop_done[R.s], 1)

            if exists(i, -2):
                wait(dve, y_done[O.s], O.before + 1)
                wait(dve, xb_done[O.s], O.before + 1)
                wait(dve, stored[O.s], O.before * 16)
                nc.vector.scalar_tensor_tensor(xo[:, O.s].rearrange("p b c -> p (b c)"), ps_o[:, 0], 0.5,
                                               xb[:, O.place].rearrange("p b c -> p (b c)"), ALU.mult, ALU.add)\
                    .then_inc(xo_done[O.s], 1)
            if exists(i, 0):
                scored(0)
                scored(1)
            if exists(i, -1):
                turned(0)
                wait(dve, exp_done[D.s], D.before * 4 + 4)
                wait(dve, share_done[D.s], D.before)
                nc.vector.reciprocal(rden[:, D.s], total[:, D.s]).then_inc(rden_done[D.s], 1)
            if exists(i, 0):
                scored(2)
            if exists(i, -1):
                turned(2)
            if exists(i, 0):
                scored(3)
            if exists(i, 2):
                wait(dve, x_in[L.s], L.before * 16 + 16)
                wait(dve, t_done[L.s], L.before)
                for b in range(B):
                    col = bass.ds(L.index * B + b, 1)
                    ins = nc.vector.tensor_scalar(xn[:, L.s, b], xr[:, L.s, b], k.mean[:, col], k.rstd[:, col],
                                                  ALU.subtract, ALU.mult)
                ins.then_inc(xn_done[L.s], 1)
            if exists(i, 1):
                wait(dve, qk_kept[A.s], A.before + 1)
                wait(dve, s_done[A.s], A.before * NH)
                for h in range(NH):
                    ins = nc.vector.tensor_copy(keys[head(h), A.s, h], qk[head(h), A.s, 1])
                ins.then_inc(keys_done[A.s], 1)
            if exists(i, -1):
                wait(dve, share_turned[D.s], D.before + 1)
                wait(dve, tanh_done[D.s], D.before + 1)
                wait(dve, av_done[D.s], D.before + 1)
                nc.vector.scalar_tensor_tensor(gate[:, D.s], g[:, D.s], 1.0, ps_o[:, 1], ALU.add, ALU.mult)\
                    .then_inc(gate_done[D.s], 1)
                wait(dve, gate_done[D.s], D.before + 1)
                wait(dve, y_done[D.s], D.before)
                nc.vector.tensor_tensor(vals[:, D.s], ps_o[:, 0], gate[:, D.s], ALU.mult).then_inc(vals_done[D.s], 1)

        def act_step(step, i, act):
            A, R, D = step.shift(1), step, step.shift(-1)

            def turned(h):
                wait(act, pt_done[D.s], D.before * 4 + (h + 1))
                wait(act, av_done[1 - D.s], D.shift(-1).before + 1)
                nc.scalar.copy(pt[:, h], ps_p[:, 1]).then_inc(pt_odd[D.s], 1)

            def exps(row, h):
                wait(act, ntop_done[row.s], row.before * 2 + (h // 2 + 1))
                wait(act, rden_done[row.s], row.before)
                for b in range(B):
                    ins = nc.scalar.activation(prob[:, row.s, h, b], prob[:, row.s, h, b], ACT.Exp,
                                               bias=ntop[:, row.s, h, b:b + 1], accum_out=total[:, row.s, h, b:b + 1])
                ins.then_inc(exp_done[row.s], 1)

            if exists(i, -1):
                exps(D, 2)
                exps(D, 3)
            if exists(i, 1):
                wait(act, t_done[A.s], A.before + 1)
                wait(act, gv_done[A.s], A.before)
                nc.scalar.activation(zt[:, A.s], ps_a[:, 0], ACT.Identity,
                                     bias=k.beta[:, 0:1], scale=k.gamma[:, 0:1]).then_inc(zt_done[A.s], 1)
            if exists(i, -1):
                turned(1)
                turned(3)
            if exists(i, 1):
                wait(act, qk_done[A.s], A.before + 1)
                wait(act, s_done[A.s], A.before * 4)
                wait(act, keys_done[A.s], A.before)
                nc.scalar.activation(qk[:, A.s], ps_a[:], ACT.Copy, scale=SCALE).then_inc(qk_kept[A.s], 1)
            if exists(i, 0):
                exps(R, 0)
            if exists(i, 1):
                wait(act, gv_done[A.s], A.before + 1)
                wait(act, gate_done[A.s], A.before)
                nc.scalar.activation(g[:, A.s], ps_a[:, 0], ACT.Tanh, bias=bg_half[:, 0:1], scale=0.5)\
                    .then_inc(tanh_done[A.s], 1)
                wait(act, av_done[A.s], A.before)
                nc.scalar.copy(v[:, A.s], ps_a[:, 1]).then_inc(v_kept[A.s], 1)
            if exists(i, 0):
                exps(R, 1)

        def pe_step(step, i, pe):
            A, R, D, O = (step.shift(by) for by in (1, 0, -1, -2))

            def turn(h):
                kept = pt_odd if h % 2 else pt_even
                wait(pe, exp_done[D.s], D.before * 4 + (h + 1))
                if h < 2:
                    wait(pe, kept[1 - D.s], (D.shift(-1).before + 1) * 2)
                else:
                    wait(pe, kept[D.s], D.before * 2 + 1)
                for kb in range(B):
                    for b in range(B):
                        ins = nc.tensor.transpose(ps_p[:, h % 2, kb, b * P:(b + 1) * P],
                                                  prob[:, D.s, h, b, kb * P:(kb + 1) * P], k.ident[:])
                ins.then_inc(pt_done[D.s], 1)

            def score(h):
                if h == 0:
                    wait(pe, keys_done[R.s], R.before + 1)
                wait(pe, top_done[1 - R.s], R.shift(-1).before * 4 + (h + 1))
                for b in range(B):
                    ins = nc.tensor.matmul(ps_s[:, h, b], qk[:, R.s, 0, b * P:(b + 1) * P], keys[:, R.s, h],
                                           start=True, stop=True)
                ins.then_inc(s_done[R.s], 1)

            if exists(i, 0):
                score(0)
                score(1)
            if exists(i, 1):
                wait(pe, xn_done[A.s], A.before + 1)
                wait(pe, v_kept[1 - A.s], A.shift(-1).before + 1)
                for b in range(B):
                    ins = nc.tensor.transpose(ps_a[:, 0, b * P:(b + 1) * P], xn[:, A.s, b], k.ident[:])
                ins.then_inc(t_done[A.s], 1)
            if exists(i, -2):
                wait(pe, vals_done[O.s], O.before + 1)
                for b in range(B):
                    ins = nc.tensor.matmul(ps_o[:, 0, b * C:(b + 1) * C], vals[:, O.s, b * P:(b + 1) * P], wo[:],
                                           start=True, stop=True)
                ins.then_inc(y_done[O.s], 1)
            if exists(i, -1):
                turn(0)
                turn(1)
            if exists(i, 0):
                score(2)
            if exists(i, -1):
                turn(2)
            if exists(i, 0):
                score(3)
            if exists(i, -1):
                turn(3)
            if exists(i, 1):
                wait(pe, zt_done[A.s], A.before + 1)
                for a in range(2):
                    ins = nc.tensor.matmul(ps_a[:, a], wqk[:, a], zt[:, A.s], start=True, stop=True)
                ins.then_inc(qk_done[A.s], 1)
            if exists(i, -1):
                wait(pe, xo_done[1 - D.s], D.shift(-1).before + 1)
                wait(pe, share_done[D.s], D.before + 1)
                for b in range(B):
                    ins = nc.tensor.transpose(ps_o[:, 1, b * P:(b + 1) * P], share[:, D.s, b], k.ident[:])
                ins.then_inc(share_turned[D.s], 1)
                wait(pe, pt_even[D.s], D.before * 2 + 2)
                wait(pe, pt_odd[D.s], D.before * 2 + 2)
                wait(pe, v_kept[D.s], D.before + 1)
                for kb in range(B):
                    for h in range(NH):
                        ins = nc.tensor.matmul(ps_o[head(h), 0], v[:, D.s, kb * C + h * HD:kb * C + (h + 1) * HD],
                                               pt[:, h, kb], start=kb == 0, stop=kb == B - 1)
                ins.then_inc(av_done[D.s], 1)
            if exists(i, 1):
                wait(pe, qk_kept[A.s], A.before + 1)
                nc.tensor.matmul(ps_a[:, 0], wg[:], zt[:, A.s], start=True, stop=True)
                for b in range(B):
                    ins = nc.tensor.matmul(ps_a[:, 1, b * C:(b + 1) * C], zt[:, A.s, b * P:(b + 1) * P], wv[:],
                                           start=True, stop=True)
                ins.then_inc(gv_done[A.s], 1)

        run = lambda eng, f: run_steps(eng, lambda step, i: f(step, i, eng), -2, 4, N - 4, N + 3, 4)
        with nc.Block() as block:
            @block.sync
            def _(sp):
                for place, name in ((wqk[:, 0], "Wq"), (wqk[:, 1], "Wk"), (wg[:], "Wg"), (wv[:], "Wv"), (wo[:], "Wo")):
                    sp.dma_start(place, d["L0_conv_" + name]).then_inc(w_in, 16)
                sp.dma_start(bg[:], d["L0_conv_bg"].rearrange("(c a) -> c a", a=1)).then_inc(w_in, 16)
                sp.dma_start(bo[:], row_of(d["L0_conv_bo"])).then_inc(w_in, 16)
                run(sp, sp_step)
                for s in range(2):
                    sp.wait_ge(stored[s], 16 * N // 2)

            @block.gpsimd
            def _(pool):
                nc.gpsimd.memset(keys[:], 0.0).then_inc(ready, 1)
                pool.wait_ge(w_in, 16 * 7)
                pool.wait_ge(ready, 2)
                run(pool, pool_step)

            @block.vector
            def _(dve):
                dve.wait_ge(w_in, 16 * 7)
                nc.vector.tensor_scalar(bg_half[:], bg[:], 0.5, None, ALU.mult).then_inc(ready, 1)
                run(dve, dve_step)

            @block.scalar
            def _(act):
                act.wait_ge(ready, 2)
                run(act, act_step)

            @block.tensor
            def _(pe):
                pe.wait_ge(w_in, 16 * 7)
                run(pe, pe_step)


def gate_pass(k, kept_top, kept_at, kept_sum):
    nc, d = k.nc, k.d
    G = 8
    STEPS = TILES // G
    HALF = G // 2 * P
    with ExitStack() as ctx:
        sb = lambda name, shape, dt=F32: k.sb(ctx, "g_" + name, shape, dt)
        xin, xn = sb("xin", [P, 2, G, C]), sb("xn", [P, 2, G, C])
        ut = sb("ut", [C, 2, G, P])
        stats, mv, var, rstd = sb("stats", [P, 2, G, 6]), sb("mv", [P, 2, G, 2]), sb("var", [P, 2, G]), sb("rstd", [P, 2, G])
        gate_in, gate_t, gate_b = sb("gate_in", [E0, C]), sb("gate_t", [C, E0]), sb("gate_b", [2 * E0, 1])
        logit, ex = sb("logit", [P, 2, HALF]), sb("ex", [P, 2, HALF])
        best, at, nbest, esum = sb("best", [P, 2, K0]), sb("at", [P, 2, K0], U32), sb("nbest", [P, 2]), sb("esum", [P, 2])
        ps_t = k.ps(ctx, "g_ps_t", [C, 2, G, P])
        ps_l = k.ps(ctx, "g_ps_l", [P, 2, HALF])
        ps_g = k.ps(ctx, "g_ps_g", [C, 512])
        w_in, gate_turned, gate_kept = k.sem("g_w_in"), k.sem("g_gate_turned"), k.sem("g_gate_kept")
        pair = lambda name: [k.sem(f"g_{name}{s}") for s in range(2)]
        x_in, stats_done, mv_done, var_done, rstd_done, xn_done = map(
            pair, ("x_in", "stats_done", "mv_done", "var_done", "rstd_done", "xn_done"))
        t_done, ut_done, l_done, logit_done = map(pair, ("t_done", "ut_done", "l_done", "logit_done"))
        best_done, nbest_done, at_done, esum_done, kept = map(
            pair, ("best_done", "nbest_done", "at_done", "esum_done", "kept"))
        x_v = d["x1"].rearrange("(n t p) c -> n p t c", t=G, p=P)

        with nc.Block() as block:
            @block.sync
            def _(sp):
                sp.dma_start(gate_in[:], d["L0_ffn_gate_w"]).then_inc(w_in, 16)
                for half in range(2):
                    sp.dma_start(gate_b[half * E0:(half + 1) * E0], d["L0_ffn_gate_b"].rearrange("(e a) -> e a", a=1))\
                        .then_inc(w_in, 16)
                with sp.Fori(0, STEPS // 2) as r:
                    for s in range(2):
                        sp.wait_ge(xn_done[s], r)
                        sp.dma_start(xin[:, s], x_v[r * 2 + s]).then_inc(x_in[s], 16)

            @block.gpsimd
            def _(pool):
                with pool.Fori(0, STEPS // 2) as r:
                    for s in range(2):
                        pool.wait_ge(var_done[s], r + 1)
                        nc.gpsimd.tensor_tensor(rstd[:, s], var[:, s], k.mhalf[:, 0:G], ALU.pow).then_inc(rstd_done[s], 1)

            @block.vector
            def _(dve):
                dve.wait_ge(gate_turned, 1)
                nc.vector.tensor_copy(gate_t[:], ps_g[:, 0:E0]).then_inc(gate_kept, 1)
                with dve.Fori(0, STEPS // 2) as r:
                    for s in range(2):
                        dve.wait_ge(x_in[s], r * 16 + 16)
                        for t in range(G):
                            ins = nc.vector.bn_stats(stats[:, s, t], xin[:, s, t])
                        ins.then_inc(stats_done[s], 1)
                    for s in range(2):
                        k.wait_alone(dve, stats_done[s], r + 1)
                        for t in range(G):
                            ins = nc.vector.bn_aggr(mv[:, s, t], stats[:, s, t])
                        ins.then_inc(mv_done[s], 1)
                    for s in range(2):
                        dve.wait_ge(mv_done[s], r + 1)
                        nc.vector.tensor_scalar(var[:, s], mv[:, s, :, 1], 1e-5, None, ALU.add).then_inc(var_done[s], 1)
                    for s in range(2):
                        dve.wait_ge(rstd_done[s], r + 1)
                        dve.wait_ge(t_done[s], r)
                        for t in range(G):
                            ins = nc.vector.tensor_scalar(xn[:, s, t], xin[:, s, t], mv[:, s, t, 0:1],
                                                          rstd[:, s, t:t + 1], ALU.subtract, ALU.mult)
                        ins.then_inc(xn_done[s], 1)
                    for s in range(2):
                        k.wait_alone(dve, logit_done[s], r + 1)
                        nc.vector.max(best[:, s], logit[:, s]).then_inc(best_done[s], 1)
                    for s in range(2):
                        dve.wait_ge(best_done[s], r + 1)
                        nc.vector.tensor_scalar(nbest[:, s:s + 1], best[:, s, 0:1], -1.0, None, ALU.mult)\
                            .then_inc(nbest_done[s], 1)
                        nc.vector.max_index(at[:, s], best[:, s], logit[:, s]).then_inc(at_done[s], 1)
                        nc.vector.tensor_copy(kept_top[:, bass.ds((r * 2 + s) * K0, K0)], best[:, s]).then_inc(kept[s], 1)
                    for s in range(2):
                        dve.wait_ge(at_done[s], r + 1)
                        nc.vector.tensor_copy(kept_at[:, bass.ds((r * 2 + s) * K0, K0)], at[:, s]).then_inc(kept[s], 1)
                        dve.wait_ge(esum_done[s], r + 1)
                        nc.vector.tensor_copy(kept_sum[:, bass.ds(r * 2 + s, 1)], esum[:, s:s + 1]).then_inc(kept[s], 1)

            @block.tensor
            def _(pe):
                pe.wait_ge(w_in, 48)
                nc.tensor.transpose(ps_g[:, 0:E0], gate_in[:], k.ident[0:E0, 0:E0]).then_inc(gate_turned, 1)
                pe.wait_ge(gate_kept, 1)
                with pe.Fori(0, STEPS // 2) as r:
                    for s in range(2):
                        pe.wait_ge(xn_done[s], r + 1)
                        pe.wait_ge(ut_done[s], r * 2)
                        for t in range(G):
                            ins = nc.tensor.transpose(ps_t[:, s, t], xn[:, s, t], k.ident[:])
                        ins.then_inc(t_done[s], 1)
                    for s in range(2):
                        pe.wait_ge(ut_done[s], r * 2 + 2)
                        pe.wait_ge(logit_done[s], r)
                        for half in range(2):
                            ins = nc.tensor.matmul(ps_l[half * E0:(half + 1) * E0, s], gate_t[:],
                                                   ut[:, s, half * G // 2:(half + 1) * G // 2], start=True, stop=True)
                        ins.then_inc(l_done[s], 1)

            @block.scalar
            def _(act):
                with act.Fori(0, STEPS // 2) as r:
                    for s in range(2):
                        act.wait_ge(t_done[s], r + 1)
                        act.wait_ge(l_done[s], r)
                        for half in range(2):
                            a, b = half * G // 2, (half + 1) * G // 2
                            nc.scalar.copy(ut[:, s, a:b], ps_t[:, s, a:b]).then_inc(ut_done[s], 1)
                    for s in range(2):
                        act.wait_ge(l_done[s], r + 1)
                        act.wait_ge(at_done[s], r)
                        nc.scalar.activation(logit[:, s], ps_l[:, s], ACT.Identity, bias=gate_b[:, 0:1])\
                            .then_inc(logit_done[s], 1)
                    for s in range(2):
                        act.wait_ge(nbest_done[s], r + 1)
                        act.wait_ge(kept[s], r * 3)
                        nc.scalar.activation(ex[:, s], logit[:, s], ACT.Exp, bias=nbest[:, s:s + 1],
                                             accum_out=esum[:, s:s + 1]).then_inc(esum_done[s], 1)


def experts(k, kept_top, kept_at, kept_sum):
    nc, d = k.nc, k.d
    STEPS = TILES // 8
    CAND = STEPS * 2 * K0
    HB = H0 // P
    W = 4
    with ExitStack() as ctx:
        sb = lambda name, shape, dt=F32: k.sb(ctx, "e_" + name, shape, dt)
        offs, iota, upper, ones = sb("offs", [P, STEPS * K0]), sb("iota", [E0, CAND]), sb("upper", [E0, E0]), sb("ones", [E0, 1])
        at_all = sb("at_all", [P, STEPS * K0])
        cand, cand_at = sb("cand", [E0, STEPS, 2, K0]), sb("cand_at", [E0, STEPS, 2, K0])
        sums = sb("sums", [E0, 2, STEPS])
        top, pos, posf, ntop = sb("top", [E0, K0]), sb("pos", [E0, K0], U32), sb("posf", [E0, K0]), sb("ntop", [E0, 1])
        junk = sb("junk", [E0, CAND])
        tok, tok_u, keep_u = sb("tok", [E0, K0]), sb("tok_u", [E0, K0], U32), sb("keep_u", [E0, K0], U32)
        esc, prod, tsum, tinv = sb("esc", [E0, 2, STEPS]), sb("prod", [E0, 2, STEPS]), sb("tsum", [E0, 1]), sb("tinv", [E0, 1])
        ptop, prob = sb("ptop", [E0, K0]), sb("prob", [E0, K0])
        x, u = sb("x", [E0, K0, C]), sb("u", [E0, K0, C])
        stats, mv, var, rstd = sb("stats", [E0, K0, 6]), sb("mv", [E0, K0, 2]), sb("var", [E0, K0]), sb("rstd", [E0, K0])
        pooled, pooled_t = sb("pooled", [E0, C]), sb("pooled_t", [C, E0])
        w1, w2 = sb("w1", [P, 2, W, H0]), sb("w2", [P, 2, W, HB, C])
        b1, b1_t, b2 = sb("b1", [E0, H0]), sb("b1_t", [P, HB, E0]), sb("b2", [E0, C])
        hb, hid = sb("hb", [P, HB, E0]), sb("hid", [P, HB, E0])
        o_t, o_e = sb("o_t", [C, E0]), sb("o_e", [E0, C])
        weighted = sb("weighted", [E0, K0, C])
        spread, others = sb("spread", [E0, K0, E0]), sb("others", [E0, K0, E0])
        same, earlier = sb("same", [E0, K0, K0, E0]), sb("earlier", [E0, K0, E0])
        count, skip = sb("count", [E0, K0]), sb("skip", [E0, K0])
        xnew = sb("xnew", [E0, K0, C])
        ps_h, ps_b1, ps_o = k.ps(ctx, "e_ps_h", [P, 512]), k.ps(ctx, "e_ps_b1", [P, HB, P]), k.ps(ctx, "e_ps_o", [P, 512])
        ps_m, ps_s = k.ps(ctx, "e_ps_m", [P, 512]), k.ps(ctx, "e_ps_s", [P, K0 * E0])
        ps_u = k.ps(ctx, "e_ps_u", [P, K0, C])
        names = """consts_in offs_done cand_in top_done pos_done posf_done tok_done tok_u_done ntop_done esc_done ptop_done
            prod_done tsum_done tinv_done prob_done x_in stats_done mv_done var_done rstd_done u_done pooled_acc
            pooled_turned pooled_kept b1_turned b1_kept h_all hb_done hid_done o_all o_kept o_turned oe_done
            weighted_done spread_done others_turned others_kept same_done u_all count_all skip_done keep_done
            xnew_done written""".split()
        S = {n: k.sem("e_" + n) for n in names}
        pair = lambda name: [k.sem(f"e_{name}{s}") for s in range(2)]
        w1_in, w2_in, h_done, o_done = map(pair, ("w1_in", "w2_in", "h_done", "o_done"))
        col = lambda v, j: v[:, j:j + 1]
        x1_rows = d["x1"]

        with nc.Block() as block:
            @block.sync
            def _(sp):
                sp.dma_start(offs[:], d["offs"]).then_inc(S["consts_in"], 16)
                sp.dma_start(iota[:], d["iota"]).then_inc(S["consts_in"], 16)
                sp.dma_start(upper[:], d["upper"]).then_inc(S["consts_in"], 16)
                sp.dma_start(b1[:], d["L0_ffn_weight1"][:, C]).then_inc(S["consts_in"], 16)
                sp.dma_start(b2[:], d["L0_ffn_weight2"][:, H0]).then_inc(S["consts_in"], 16)
                for half in range(2):
                    rows = slice(half * E0, (half + 1) * E0)
                    sp.dma_start(cand[:, :, half], kept_top[rows].rearrange("e (n k) -> e n k", k=K0)).then_inc(S["cand_in"], 16)
                    sp.dma_start(sums[:, half], kept_sum[rows]).then_inc(S["cand_in"], 16)
                sp.wait_ge(S["offs_done"], 1)
                for half in range(2):
                    rows = slice(half * E0, (half + 1) * E0)
                    sp.dma_start(cand_at[:, :, half], at_all[rows].rearrange("e (n k) -> e n k", k=K0)).then_inc(S["cand_in"], 16)
                w1_v = d["L0_ffn_weight1"].rearrange("(n w) c h -> n c w h", w=W)
                w2_v = d["L0_ffn_weight2"].rearrange("(n w) h o -> n w h o", w=W)
                with sp.Fori(0, E0 // W // 2) as r:
                    for s in range(2):
                        sp.wait_ge(h_done[s], r)
                        sp.dma_start(w1[:, s], w1_v[r * 2 + s][0:C]).then_inc(w1_in[s], 16)
                with sp.Fori(0, E0 // W // 2) as r:
                    for s in range(2):
                        sp.wait_ge(o_done[s], r)
                        sp.dma_start(w2[:, s], w2_v[r * 2 + s][:, 0:H0].rearrange("w (p b) o -> p w b o", b=HB))\
                            .then_inc(w2_in[s], 16)

            @block.gpsimd
            def _(pool):
                pool.wait_ge(S["tok_u_done"], 1)
                for j in range(K0):
                    nc.gpsimd.indirect_dma_start(
                        out=x[:, j], out_offset=None, in_=x1_rows,
                        in_offset=bass.IndirectOffsetOnAxis(ap=col(tok_u, j), axis=0)).then_inc(S["x_in"], 16)
                pool.wait_ge(S["var_done"], 1)
                nc.gpsimd.tensor_tensor(rstd[:], var[:], k.mhalf[0:E0, 0:K0], ALU.pow).then_inc(S["rstd_done"], 1)
                pool.wait_ge(S["x_in"], 16 * K0)
                pool.wait_ge(S["keep_done"], 1)
                pool.wait_ge(S["xnew_done"], K0)
                for j in range(K0):
                    nc.gpsimd.indirect_dma_start(
                        out=x1_rows, out_offset=bass.IndirectOffsetOnAxis(ap=col(keep_u, j), axis=0), in_=xnew[:, j],
                        in_offset=None, bounds_check=TOK - 1, oob_is_err=False).then_inc(S["written"], 16)
                pool.wait_ge(S["written"], 16 * K0)

            @block.vector
            def _(dve):
                dve.wait_ge(S["consts_in"], 80)
                nc.vector.memset(ones[:], 1.0)
                nc.vector.tensor_tensor(at_all[:], kept_at[:], offs[:], ALU.add).then_inc(S["offs_done"], 1)
                dve.wait_ge(S["cand_in"], 16 * 6)
                flat = cand[:].rearrange("e n a k -> e (n a k)")
                nc.vector.max(top[:], flat).then_inc(S["top_done"], 1)
                dve.wait_ge(S["top_done"], 1)
                nc.vector.tensor_scalar(ntop[:], top[:, 0:1], -1.0, None, ALU.mult).then_inc(S["ntop_done"], 1)
                nc.vector.max_index(pos[:], top[:], flat).then_inc(S["pos_done"], 1)
                dve.wait_ge(S["pos_done"], 1)
                nc.vector.tensor_copy(posf[:], pos[:]).then_inc(S["posf_done"], 1)
                dve.wait_ge(S["posf_done"], 1)
                for j in range(K0):
                    if j:
                        dve.wait_ge(S["tok_done"], j)
                    nc.vector.scalar_tensor_tensor(junk[:], iota[:], col(posf, j), cand_at[:].rearrange("e n a k -> e (n a k)"),
                                                   ALU.is_equal, ALU.mult, accum_out=col(tok, j)).then_inc(S["tok_done"], 1)
                dve.wait_ge(S["tok_done"], K0)
                nc.vector.tensor_copy(tok_u[:], tok[:]).then_inc(S["tok_u_done"], 1)
                dve.wait_ge(S["esc_done"], 1)
                nc.vector.tensor_tensor(prod[:], esc[:], sums[:], ALU.mult).then_inc(S["prod_done"], 1)
                dve.wait_ge(S["prod_done"], 1)
                nc.vector.tensor_reduce(tsum[:], prod[:].rearrange("e a n -> e (a n)"), AXX, ALU.add).then_inc(S["tsum_done"], 1)
                dve.wait_ge(S["tsum_done"], 1)
                nc.vector.reciprocal(tinv[:], tsum[:]).then_inc(S["tinv_done"], 1)
                dve.wait_ge(S["tinv_done"], 1)
                dve.wait_ge(S["ptop_done"], 1)
                nc.vector.tensor_scalar(prob[:], ptop[:], tinv[:, 0:1], None, ALU.mult).then_inc(S["prob_done"], 1)
                dve.wait_ge(S["x_in"], 16 * K0)
                for j in range(K0):
                    ins = nc.vector.bn_stats(stats[:, j], x[:, j])
                ins.then_inc(S["stats_done"], 1)
                dve.wait_ge(S["stats_done"], 1)
                for j in range(K0):
                    ins = nc.vector.bn_aggr(mv[:, j], stats[:, j])
                ins.then_inc(S["mv_done"], 1)
                dve.wait_ge(S["mv_done"], 1)
                nc.vector.tensor_scalar(var[:], mv[:, :, 1], 1e-5, None, ALU.add).then_inc(S["var_done"], 1)
                dve.wait_ge(S["rstd_done"], 1)
                for j in range(K0):
                    ins = nc.vector.tensor_scalar(u[:, j], x[:, j], mv[:, j, 0:1], col(rstd, j), ALU.subtract, ALU.mult)
                ins.then_inc(S["u_done"], 1)
                dve.wait_ge(S["u_done"], 1)
                dve.wait_ge(S["prob_done"], 1)
                for j in range(K0):
                    if j == 0:
                        nc.vector.tensor_scalar(pooled[:], u[:, 0], prob[:, 0:1], None, ALU.mult).then_inc(S["pooled_acc"], 1)
                        continue
                    dve.wait_ge(S["pooled_acc"], j)
                    nc.vector.scalar_tensor_tensor(pooled[:], u[:, j], col(prob, j), pooled[:], ALU.mult, ALU.add)\
                        .then_inc(S["pooled_acc"], 1)
                dve.wait_ge(S["pooled_turned"], 1)
                nc.vector.tensor_copy(pooled_t[:], ps_m[:, 0:E0]).then_inc(S["pooled_kept"], 1)
                dve.wait_ge(S["b1_turned"], 1)
                nc.vector.tensor_copy(b1_t[:], ps_b1[:, :, 0:E0]).then_inc(S["b1_kept"], 1)
                for j in range(K0):
                    ins = nc.vector.tensor_copy(spread[:, j], col(tok, j).broadcast_to([E0, E0]))
                ins.then_inc(S["spread_done"], 1)
                dve.wait_ge(S["others_turned"], 1)
                nc.vector.tensor_copy(others[:].rearrange("e j f -> e (j f)"), ps_s[0:E0]).then_inc(S["others_kept"], 1)
                dve.wait_ge(S["others_kept"], 1)
                for j in range(K0):
                    ins = nc.vector.tensor_scalar(same[:, j], others[:], col(tok, j), None, ALU.is_equal)
                ins.then_inc(S["same_done"], 1)
                dve.wait_ge(S["same_done"], 1)
                for j in range(K0):
                    ins = nc.vector.tensor_tensor(earlier[:, j], same[:, j, j], upper[:], ALU.mult)
                ins.then_inc(S["same_done"], 1)
                dve.wait_ge(S["h_all"], 1)
                dve.wait_ge(S["b1_kept"], 1)
                nc.vector.tensor_tensor(hb[:], ps_h[:, 0:HB * E0].rearrange("p (b e) -> p b e", b=HB), b1_t[:], ALU.add)\
                    .then_inc(S["hb_done"], 1)
                dve.wait_ge(S["o_all"], 1)
                nc.vector.tensor_copy(o_t[:], ps_o[:, 0:E0]).then_inc(S["o_kept"], 1)
                dve.wait_ge(S["o_turned"], 1)
                nc.vector.tensor_tensor(o_e[:], ps_m[0:E0, C:2 * C], b2[:], ALU.add).then_inc(S["oe_done"], 1)
                dve.wait_ge(S["oe_done"], 1)
                for j in range(K0):
                    ins = nc.vector.tensor_scalar(weighted[:, j], o_e[:], col(prob, j), None, ALU.mult)
                ins.then_inc(S["weighted_done"], 1)
                dve.wait_ge(S["u_all"], K0)
                for j in range(K0):
                    nc.vector.tensor_tensor(xnew[:, j], ps_u[0:E0, j], x[:, j], ALU.add).then_inc(S["xnew_done"], 1)
                dve.wait_ge(S["count_all"], 1)
                nc.vector.tensor_scalar(skip[:], ps_m[0:E0, 2 * C:2 * C + K0], 0.5, float(2 * TOK), ALU.is_gt, ALU.mult)\
                    .then_inc(S["skip_done"], 1)
                dve.wait_ge(S["skip_done"], 1)
                nc.vector.tensor_tensor(keep_u[:], skip[:], tok[:], ALU.add).then_inc(S["keep_done"], 1)

            @block.scalar
            def _(act):
                act.wait_ge(S["ntop_done"], 1)
                nc.scalar.activation(esc[:], cand[:, :, :, 0].rearrange("e n a -> e a n"), ACT.Exp, bias=ntop[:, 0:1]).then_inc(S["esc_done"], 1)
                nc.scalar.activation(ptop[:], top[:], ACT.Exp, bias=ntop[:, 0:1]).then_inc(S["ptop_done"], 1)
                act.wait_ge(S["hb_done"], 1)
                nc.scalar.activation(hid[:], hb[:], ACT.Gelu).then_inc(S["hid_done"], 1)

            @block.tensor
            def _(pe):
                pe.wait_ge(S["consts_in"], 80)
                for b in range(HB):
                    ins = nc.tensor.transpose(ps_b1[:, b, 0:E0], b1[:].rearrange("e (p b) -> e b p", b=HB)[:, b],
                                              k.ident[0:E0, 0:E0])
                ins.then_inc(S["b1_turned"], 1)
                pe.wait_ge(S["pooled_acc"], K0)
                nc.tensor.transpose(ps_m[:, 0:E0], pooled[:], k.ident[0:E0, 0:E0]).then_inc(S["pooled_turned"], 1)
                pe.wait_ge(S["spread_done"], 1)
                for j in range(K0):
                    ins = nc.tensor.transpose(ps_s[0:E0, j * E0:(j + 1) * E0], spread[:, j], k.ident[0:E0, 0:E0])
                ins.then_inc(S["others_turned"], 1)
                pe.wait_ge(S["pooled_kept"], 1)
                with pe.Fori(0, E0 // W // 2) as r:
                    for s in range(2):
                        pe.wait_ge(w1_in[s], r * 16 + 16)
                        for w in range(W):
                            e = r * (2 * W) + (s * W + w)
                            for b in range(HB):
                                ins = nc.tensor.matmul(ps_h[:, bass.ds(e + b * E0, 1)],
                                                       w1[:, s, w].rearrange("c (p b) -> c b p", b=HB)[:, b],
                                                       pooled_t[:, bass.ds(e, 1)], start=True, stop=True)
                        ins.then_inc(h_done[s], 1)
                nc.tensor.drain().then_inc(S["h_all"], 1)
                pe.wait_ge(S["hid_done"], 1)
                with pe.Fori(0, E0 // W // 2) as r:
                    for s in range(2):
                        pe.wait_ge(w2_in[s], r * 16 + 16)
                        for w in range(W):
                            e = r * (2 * W) + (s * W + w)
                            for b in range(HB):
                                ins = nc.tensor.matmul(ps_o[:, bass.ds(e, 1)], w2[:, s, w, b], hid[:, b, bass.ds(e, 1)],
                                                       start=b == 0, stop=b == HB - 1)
                        ins.then_inc(o_done[s], 1)
                nc.tensor.drain().then_inc(S["o_all"], 1)
                pe.wait_ge(S["o_kept"], 1)
                nc.tensor.transpose(ps_m[0:E0, C:2 * C], o_t[:], k.ident[:]).then_inc(S["o_turned"], 1)
                pe.wait_ge(S["weighted_done"], 1)
                pe.wait_ge(S["same_done"], 2)
                for j in range(K0):
                    for f in range(K0):
                        ins = nc.tensor.matmul(ps_u[0:E0, j], same[:, f, j], weighted[:, f], start=f == 0, stop=f == K0 - 1)
                    ins.then_inc(S["u_all"], 1)
                pe.wait_ge(S["oe_done"], 1)
                for j in range(K0):
                    for f in range(j + 1):
                        ins = nc.tensor.matmul(ps_m[0:E0, 2 * C + j:2 * C + j + 1], same[:, f, j] if f < j else earlier[:, j],
                                               ones[:], start=f == 0, stop=f == j)
                ins.then_inc(S["count_all"], 1)


def transform(k, along_rows, mean_t, rstd_t, modes):
    nc, d = k.nc, k.d
    G, LINES = 8, 4
    U = 4
    STEPS = N // LINES
    tag = "r_" if along_rows else "c_"
    with ExitStack() as ctx:
        sb = lambda name, shape, dt=F32: k.sb(ctx, tag + name, shape, dt)
        xin, xn = sb("xin", [P, 2, G, C]), sb("xn", [P, 2, G, C])
        stats, mv, var = sb("stats", [P, 2, G, 6]), sb("mv", [P, 2, G, 2]), sb("var", [P, 2, G])
        basis = sb("basis", [P, 2, M2])
        by_mode = sb("by_mode", [P, LINES, C])
        ps_m = k.ps(ctx, tag + "ps_m", [P, LINES, C])
        ps_t = k.ps(ctx, tag + "ps_t", [C, LINES, P])
        basis_in, m_kept, m_turned, modes_kept = (k.sem(tag + n) for n in ("basis_in", "m_kept", "m_turned", "modes_kept"))
        pair = lambda name: [k.sem(f"{tag}{name}{s}") for s in range(2)]
        x_in, stats_done, mv_done, var_done, rstd_done, xn_done, m_done = map(
            pair, ("x_in", "stats_done", "mv_done", "var_done", "rstd_done", "xn_done", "m_done"))
        if along_rows:
            x_v = d["x1"].rearrange("(n t p) c -> n p t c", t=G, p=P)
            tile_of = lambda line, block: line * 2 + block
        else:
            x_v = d["x1"].rearrange("(b p n w) c -> n p b (w c)", b=2, p=P, w=LINES)
            tile_of = lambda line, block: block * LINES + line

        with nc.Block() as block:
            @block.sync
            def _(sp):
                sp.dma_start(basis[:], d["forward"].rearrange("(b p) m -> p b m", p=P)).then_inc(basis_in, 16)
                with sp.Fori(0, STEPS // U) as r:
                    for g in range(U):
                        s, before = g % 2, r * 2 + g // 2
                        sp.wait_ge(xn_done[s], before)
                        dst = xin[:, s] if along_rows else xin[:, s].rearrange("p (b w) c -> p b (w c)", b=2)
                        sp.dma_start(dst, x_v[r * U + g]).then_inc(x_in[s], 16)

            @block.gpsimd
            def _(pool):
                if along_rows:
                    with pool.Fori(0, STEPS // U) as r:
                        for g in range(U):
                            s, before = g % 2, r * 2 + g // 2
                            pool.wait_ge(var_done[s], before + 1)
                            nc.gpsimd.tensor_tensor(k.rstd[:, bass.ds(r * (U * G) + g * G, G)], var[:, s],
                                                    k.mhalf[:, 0:G], ALU.pow).then_inc(rstd_done[s], 1)

            @block.vector
            def _(dve):
                with dve.Fori(0, STEPS // U) as r:
                    for g in range(U):
                        s, before = g % 2, r * 2 + g // 2
                        dve.wait_ge(x_in[s], before * 16 + 16)
                        if along_rows:
                            for t in range(G):
                                ins = nc.vector.bn_stats(stats[:, s, t], xin[:, s, t])
                            ins.then_inc(stats_done[s], 1)
                            k.wait_alone(dve, stats_done[s], before + 1)
                            for t in range(G):
                                ins = nc.vector.bn_aggr(mv[:, s, t], stats[:, s, t])
                            ins.then_inc(mv_done[s], 1)
                            dve.wait_ge(mv_done[s], before + 1)
                            nc.vector.tensor_scalar(var[:, s], mv[:, s, :, 1], 1e-6, None, ALU.add).then_inc(var_done[s], 1)
                            nc.vector.tensor_copy(k.mean[:, bass.ds(r * (U * G) + g * G, G)], mv[:, s, :, 0])
                            dve.wait_ge(rstd_done[s], before + 1)
                        dve.wait_ge(m_done[s], before)
                        for t in range(G):
                            if along_rows:
                                mean, rstd = mv[:, s, t, 0:1], k.rstd[:, bass.ds(r * (U * G) + (g * G + t), 1)]
                            else:
                                at = bass.ds(r * (U * LINES) + (g * LINES + t % LINES), 1)
                                mean, rstd = mean_t[:, t // LINES, at], rstd_t[:, t // LINES, at]
                            ins = nc.vector.tensor_scalar(xn[:, s, t], xin[:, s, t], mean, rstd, ALU.subtract, ALU.mult)
                        ins.then_inc(xn_done[s], 1)

            @block.scalar
            def _(act):
                with act.Fori(0, STEPS // U) as r:
                    act.wait_ge(m_done[1], r * 2 + 2)
                    act.wait_ge(m_turned, r)
                    nc.scalar.copy(by_mode[:], ps_m[:]).then_inc(m_kept, 1)
                    k.wait_alone(act, m_turned, r + 1)
                    nc.scalar.copy(modes[:, bass.ds(r * (U * LINES), U * LINES)].rearrange("c (g w) m -> c w g m", w=LINES),
                                   ps_t[:].rearrange("c w (g m) -> c w g m", m=M2)).then_inc(modes_kept, 1)

            @block.tensor
            def _(pe):
                pe.wait_ge(basis_in, 16)
                with pe.Fori(0, STEPS // U) as r:
                    for g in range(U):
                        s, before = g % 2, r * 2 + g // 2
                        pe.wait_ge(xn_done[s], before + 1)
                        if g == 0:
                            pe.wait_ge(m_kept, r)
                        for b in range(2):
                            if along_rows:
                                rhs = xn[:, s].rearrange("p (w b) c -> p b w c", b=2)[:, b]
                            else:
                                rhs = xn[:, s].rearrange("p (b w) c -> p b w c", b=2)[:, b]
                            ins = nc.tensor.matmul(ps_m[g * M2:(g + 1) * M2], basis[:, b], rhs, start=b == 0, stop=b == 1)
                        ins.then_inc(m_done[s], 1)
                    pe.wait_ge(m_kept, r + 1)
                    pe.wait_ge(modes_kept, r)
                    for w in range(LINES):
                        ins = nc.tensor.transpose(ps_t[:, w], by_mode[:, w], k.ident[:])
                    ins.then_inc(m_turned, 1)


def turn_statistics(k, mean_t, rstd_t):
    nc = k.nc
    with ExitStack() as ctx:
        ps = k.ps(ctx, "u_ps", [P, 2, 2, N])
        turned, kept = k.sem("u_turned"), k.sem("u_kept")
        with nc.Block() as block:
            @block.tensor
            def _(pe):
                for i, what in enumerate((k.mean, k.rstd)):
                    for xb in range(2):
                        for yb in range(2):
                            ins = nc.tensor.transpose(
                                ps[:, i, xb, yb * P:(yb + 1) * P],
                                what[:].rearrange("p (x b) -> p b x", b=2)[:, yb, xb * P:(xb + 1) * P], k.ident[:])
                    ins.then_inc(turned, 1)

            @block.vector
            def _(dve):
                for i, to in enumerate((mean_t, rstd_t)):
                    dve.wait_ge(turned, i + 1)
                    nc.vector.tensor_copy(to[:], ps[:, i]).then_inc(kept, 1)


def mix_modes(k, modes, weight, mixed):
    nc, d = k.nc, k.d
    tag = "m" + weight[-1] + "_"
    with ExitStack() as ctx:
        w = k.sb(ctx, tag + "w", [C, C, NM, 2])
        ww = k.sb(ctx, tag + "ww", [C, NM, 3, C])
        z = k.sb(ctx, tag + "z", [P, 2, 2, NM, C])
        ps = k.ps(ctx, tag + "ps", [P, 4, 512])
        w_in, ww_done, mixed_done, kept_a, kept_v, written = (
            k.sem(tag + n) for n in ("w_in", "ww_done", "mixed", "kept_a", "kept_v", "written"))
        with nc.Block() as block:
            @block.sync
            def _(sp):
                sp.dma_start(w[:], d[weight]).then_inc(w_in, 16)
                for lb in range(2):
                    sp.wait_ge(kept_a, (lb + 1) * NM // 2)
                    sp.wait_ge(kept_v, (lb + 1) * NM // 2)
                    for part in range(2):
                        sp.dma_start(mixed[part, :, lb * P:(lb + 1) * P].rearrange("m l o -> l m o"), z[:, lb, part])\
                            .then_inc(written, 16)
                sp.wait_ge(written, 16 * 4)

            @block.vector
            def _(dve):
                dve.wait_ge(w_in, 16)
                for m in range(NM):
                    nc.vector.tensor_scalar(ww[:, m, 0], w[:, :, m, 1], -1.0, None, ALU.mult)
                    nc.vector.tensor_copy(ww[:, m, 1:3], w[:, :, m].rearrange("i o a -> i a o")).then_inc(ww_done, 1)
                for n in range(0, 2 * NM, 2):
                    lb, m = n // NM, n % NM
                    dve.wait_ge(mixed_done, n + 1)
                    nc.vector.tensor_copy(z[:, lb, :, m], ps[:, n % 4, 0:2 * C].rearrange("p (a o) -> p a o", a=2))\
                        .then_inc(kept_v, 1)

            @block.scalar
            def _(act):
                for n in range(1, 2 * NM, 2):
                    lb, m = n // NM, n % NM
                    act.wait_ge(mixed_done, n + 1)
                    nc.scalar.copy(z[:, lb, :, m], ps[:, n % 4, 0:2 * C].rearrange("p (a o) -> p a o", a=2))\
                        .then_inc(kept_a, 1)

            @block.tensor
            def _(pe):
                for n in range(2 * NM):
                    lb, m = n // NM, n % NM
                    pe.wait_ge(ww_done, m + 1)
                    if n >= 4:
                        pe.wait_ge(kept_a if n % 2 else kept_v, n // 2 - 1)
                    lines = slice(lb * P, (lb + 1) * P)
                    nc.tensor.matmul(ps[:, n % 4, 0:2 * C], modes[:, lines, m], ww[:, m, 1:3], start=True, stop=False)
                    nc.tensor.matmul(ps[:, n % 4, 0:2 * C], modes[:, lines, NM + m], ww[:, m, 0:2], start=False, stop=True)\
                        .then_inc(mixed_done, 1)


def spectra(k):
    nc, d = k.nc, k.d
    with ExitStack() as ctx:
        modes = k.sb(ctx, "f_modes", [C, N, M2])
        mean_t, rstd_t = k.sb(ctx, "f_mean_t", [P, 2, N]), k.sb(ctx, "f_rstd_t", [P, 2, N])
        transform(k, True, mean_t, rstd_t, modes)
        k.end_phase()
        turn_statistics(k, mean_t, rstd_t)
        k.end_phase()
        mix_modes(k, modes, "L1_conv_w1", d["z1"])
        k.end_phase()
        transform(k, False, mean_t, rstd_t, modes)
        k.end_phase()
        mix_modes(k, modes, "L1_conv_w2", d["z2"])
        k.end_phase()


def layer1(k):
    nc, d = k.nc, k.d
    BX, BY, T = 16, 32, 4
    U = N // BY
    LAPS = N // BX
    BLOCKS = U * LAPS
    HB = H1 // P
    Q = T * P
    LOADS = 22
    with ExitStack() as ctx:
        sb = lambda name, shape, dt=F32: k.sb(ctx, "l_" + name, shape, dt)
        z1_next, z1 = sb("z1_next", [P, BX // 4, C]), sb("z1", [P, BX // 4, C])
        zero_z = sb("zero_z", [P, BX // 4, C])
        z2 = sb("z2", [P, N // 4, C])
        basis, basis_x = sb("basis", [P, 4, N]), sb("basis_x", [P, 4, BX])
        w0, b0, w1, b1 = sb("w0", [C, HB, P]), sb("b0", [P, HB]), sb("w1", [P, HB, C]), sb("b1", [P, C])
        ln_g, ln_b = sb("ln_g", [P, C]), sb("ln_b", [P, C])
        router, router_b = sb("router", [C, 32]), sb("router_b", [P, 1])
        we, eb = sb("we", [C, E1, C]), sb("eb", [P, T, C])
        iota = sb("iota", [P, T, E1])
        ht, hid = sb("ht", [C, 2, Q]), sb("hid", [P, 2, HB, Q])
        x2, xb, h2, x3, u, acc, out = (sb(n, [P, 2, T, C]) for n in ("x2", "xb", "h2", "x3", "u", "acc", "out"))
        ut = sb("ut", [C, 2, Q])
        stats, mv, var, rstd = sb("stats", [P, 2, T, 6]), sb("mv", [P, 2, T, 2]), sb("var", [P, 2, T]), sb("rstd", [P, 2, T])
        stats3, mv3, var3, rstd3 = sb("stats3", [P, 2, T, 6]), sb("mv3", [P, 2, T, 2]), sb("var3", [P, 2, T]), sb("rstd3", [P, 2, T])
        logit_t, logit = sb("logit_t", [P, P]), sb("logit", [P, T, E1])
        top, at, atf = sb("top", [P, T, 8]), sb("at", [P, T, 8], U32), sb("atf", [P, T, 2])
        diff, ratio, den = sb("diff", [P, T]), sb("ratio", [P, T]), sb("den", [P, T])
        share = sb("share", [P, 2, T])
        pick = sb("pick", [P, 2, T, E1])
        weight, weight_t = sb("weight", [P, 2, T, 32]), sb("weight_t", [P, P])
        ps_h, ps_f, ps_g = k.ps(ctx, "l_ps_h", [C, Q]), k.ps(ctx, "l_ps_f", [P, 2, Q]), k.ps(ctx, "l_ps_g", [P, T, C])
        ps_t, ps_e, ps_x = k.ps(ctx, "l_ps_t", [P, 512]), k.ps(ctx, "l_ps_e", [P, 2, 512]), k.ps(ctx, "l_ps_x", [P, T, C])

        w_in, zeroed, z1_in, z1_done, logit_kept = (k.sem("l_" + n) for n in ("w_in", "zeroed", "z1_in", "z1_done", "logit_kept"))
        pair = lambda name: [k.sem(f"l_{name}{s}") for s in range(2)]
        x_in, stored = pair("x_in"), pair("stored")
        i_done, f_done, g_done, t_done, rl_done, rt_done, e_done, wt_done, x_done = map(
            pair, ("i_done", "f_done", "g_done", "t_done", "rl_done", "rt_done", "e_done", "wt_done", "x_done"))
        ht_done, relu_act, ut_done, rl_kept, ratio_done, wt_kept = map(
            pair, ("ht_done", "relu_act", "ut_done", "rl_kept", "ratio_done", "wt_kept"))
        h2_done, stats_done, mv_done, var_done, scaled, x3_done, relu_dve = map(
            pair, ("h2_done", "stats_done", "mv_done", "var_done", "scaled", "x3_done", "relu_dve"))
        stats3_done, mv3_done, var3_done, u_done, rt_kept, top_done, at_done, diff_done = map(
            pair, ("stats3_done", "mv3_done", "var3_done", "u_done", "rt_kept", "top_done", "at_done", "diff_done"))
        share_done, pick_done, w_done, acc_done, out_done = map(pair, ("share_done", "pick_done", "w_done", "acc_done", "out_done"))
        at_done_f = pair("at_done_f")
        rstd_done, rstd3_done, xb_done = map(pair, ("rstd_done", "rstd3_done", "xb_done"))

        grid = "(X t a Y y) c -> X Y a y t c"
        x2_v = d["x1"].rearrange(grid, X=LAPS, t=T, a=4, Y=U, y=BY)
        out_v = d["out"].rearrange("o x y c -> (o x y) c").rearrange(grid, X=LAPS, t=T, a=4, Y=U, y=BY)
        z1_v = d["z1"].rearrange("r m (X q a) o -> X a (r m) q o", X=LAPS, a=4)
        z2_v = d["z2"].rearrange("r m (q a) o -> a (r m) q o", a=4)

        def exists(i, by):
            return i is None or 0 <= i + by < BLOCKS

        def quarter(a):
            return slice(a * 32, (a + 1) * 32)

        def sp_step(step, i, sp):
            if exists(i, 2) and step.shift(2).place == 0:
                lap = step.shift(2).lap
                k.wait_alone(sp, z1_done, lap * 2)
                for a in range(4):
                    sp.dma_start(z1_next[quarter(a)], z1_v[lap, a]).then_inc(z1_in, 16)
            if exists(i, 1):
                F = step.shift(1)
                k.wait_alone(sp, xb_done[F.s], F.before)
                for a in range(4):
                    sp.dma_start(x2[quarter(a), F.s], x2_v[F.lap, F.place, a]).then_inc(x_in[F.s], 16)
            if exists(i, 0):
                O = step
                k.wait_alone(sp, out_done[O.s], O.before + 1)
                for a in range(4):
                    sp.dma_start(out_v[O.lap, O.place, a], out[quarter(a), O.s]).then_inc(stored[O.s], 16)

        def pool_step(step, i, pool):
            if exists(i, 2) and step.shift(2).place == 0:
                I = step.shift(2)
                before = I.shift(-1)
                wait(pool, z1_in, I.lap * 64 + 64)
                wait(pool, i_done[before.s], before.before + 1)
                nc.gpsimd.tensor_tensor(z1[:], z1_next[:], zero_z[:], ALU.add).then_inc(z1_done, 1)
                nc.gpsimd.tensor_copy(basis_x[:], basis[:, :, bass.ds(I.lap * BX, BX)]).then_inc(z1_done, 1)
            if exists(i, 0):
                s = step.s
                wait(pool, var_done[s], step.before + 1)
                nc.gpsimd.tensor_tensor(rstd[:, s], var[:, s], k.mhalf[:, 0:T], ALU.pow).then_inc(rstd_done[s], 1)
                wait(pool, var3_done[s], step.before + 1)
                nc.gpsimd.tensor_tensor(rstd3[:, s], var3[:, s], k.mhalf[:, 0:T], ALU.pow).then_inc(rstd3_done[s], 1)
            if exists(i, 1):
                F = step.shift(1)
                wait(pool, x_in[F.s], F.before * 64 + 64)
                wait(pool, x3_done[F.s], F.before * T)
                nc.gpsimd.tensor_tensor(xb[:, F.s], x2[:, F.s], ln_b[:].unsqueeze(1).broadcast_to([P, T, C]), ALU.add)\
                    .then_inc(xb_done[F.s], 1)

        def dve_step(step, i, dve):
            E, F = step, step.shift(1)
            s, n = E.s, E.before

            def relu(hb):
                wait(dve, f_done[F.s], F.before * HB + hb + 1)
                wait(dve, g_done[F.s], F.before)
                nc.vector.tensor_scalar(hid[:, F.s, hb], ps_f[:, hb % 2], b0[:, hb:hb + 1], 0.0, ALU.add, ALU.max)\
                    .then_inc(relu_dve[F.s], 1)

            if exists(i, 0):
                wait(dve, g_done[s], n + 1)
                nc.vector.tensor_tensor(h2[:, s], ps_g[:], b1[:].unsqueeze(1).broadcast_to([P, T, C]), ALU.add)\
                    .then_inc(h2_done[s], 1)
                k.wait_alone(dve, h2_done[s], n + 1)
                for t in range(T):
                    ins = nc.vector.bn_stats(stats[:, s, t], h2[:, s, t])
                ins.then_inc(stats_done[s], 1)
                k.wait_alone(dve, stats_done[s], n + 1)
                for t in range(T):
                    ins = nc.vector.bn_aggr(mv[:, s, t], stats[:, s, t])
                ins.then_inc(mv_done[s], 1)
                wait(dve, mv_done[s], n + 1)
                nc.vector.tensor_scalar(var[:, s], mv[:, s, :, 1], 1e-5, None, ALU.add).then_inc(var_done[s], 1)
                for t in range(T):
                    ins = nc.vector.scalar_tensor_tensor(h2[:, s, t], h2[:, s, t], mv[:, s, t, 0:1], ln_g[:],
                                                         ALU.subtract, ALU.mult)
                ins.then_inc(scaled[s], 1)
            if exists(i, 1):
                relu(1)
            if exists(i, 0):
                wait(dve, scaled[s], n + 1)
                wait(dve, rstd_done[s], n + 1)
                wait(dve, xb_done[s], n + 1)
                for t in range(T):
                    nc.vector.scalar_tensor_tensor(x3[:, s, t], h2[:, s, t], rstd[:, s, t:t + 1], xb[:, s, t],
                                                   ALU.mult, ALU.add).then_inc(x3_done[s], 1)
                k.wait_alone(dve, x3_done[s], n * T + T)
                for t in range(T):
                    ins = nc.vector.bn_stats(stats3[:, s, t], x3[:, s, t])
                ins.then_inc(stats3_done[s], 1)
                k.wait_alone(dve, stats3_done[s], n + 1)
                for t in range(T):
                    ins = nc.vector.bn_aggr(mv3[:, s, t], stats3[:, s, t])
                ins.then_inc(mv3_done[s], 1)
                wait(dve, mv3_done[s], n + 1)
                nc.vector.tensor_scalar(var3[:, s], mv3[:, s, :, 1], 1e-5, None, ALU.add).then_inc(var3_done[s], 1)
            if exists(i, 1):
                relu(3)
            if exists(i, 0):
                wait(dve, rstd3_done[s], n + 1)
                wait(dve, t_done[s], n)
                for t in range(T):
                    ins = nc.vector.tensor_scalar(u[:, s, t], x3[:, s, t], mv3[:, s, t, 0:1], rstd3[:, s, t:t + 1],
                                                  ALU.subtract, ALU.mult)
                ins.then_inc(u_done[s], 1)
                wait(dve, rt_done[s], n + 1)
                nc.vector.tensor_copy(logit[:], ps_t[:, P:2 * P].rearrange("p (t e) -> p t e", t=T)[:, :, 0:E1])\
                    .then_inc(rt_kept[s], 1)
                k.wait_alone(dve, rt_kept[s], n + 1)
                for t in range(T):
                    ins = nc.vector.max(top[:, t], logit[:, t])
                ins.then_inc(top_done[s], 1)
                wait(dve, top_done[s], n + 1)
                nc.vector.tensor_tensor(diff[:], top[:, :, 1], top[:, :, 0], ALU.subtract).then_inc(diff_done[s], 1)
                for t in range(T):
                    ins = nc.vector.max_index(at[:, t], top[:, t], logit[:, t])
                ins.then_inc(at_done[s], 1)
                wait(dve, at_done[s], n + 1)
                nc.vector.tensor_copy(atf[:], at[:, :, 0:2]).then_inc(at_done_f[s], 1)
                wait(dve, ratio_done[s], n + 1)
                nc.vector.tensor_scalar(den[:], ratio[:], 1.0, None, ALU.add).then_inc(share_done[s], 1)
                wait(dve, share_done[s], n * 3 + 1)
                nc.vector.reciprocal(share[:, 0], den[:]).then_inc(share_done[s], 1)
                wait(dve, share_done[s], n * 3 + 2)
                nc.vector.tensor_tensor(share[:, 1], ratio[:], share[:, 0], ALU.mult).then_inc(share_done[s], 1)
                wait(dve, at_done_f[s], n + 1)
                for j in range(2):
                    ins = nc.vector.tensor_tensor(pick[:, j], iota[:], atf[:, :, j:j + 1].broadcast_to([P, T, E1]),
                                                  ALU.is_equal)
                ins.then_inc(pick_done[s], 1)
                wait(dve, share_done[s], n * 3 + 3)
                wait(dve, pick_done[s], n * 2 + 1)
                for j in range(2):
                    ins = nc.vector.tensor_tensor(pick[:, j], pick[:, j],
                                                  share[:, j].unsqueeze(2).broadcast_to([P, T, E1]), ALU.mult)
                ins.then_inc(pick_done[s], 1)
                wait(dve, pick_done[s], n * 2 + 2)
                wait(dve, wt_done[s], n)
                nc.vector.tensor_tensor(weight[:, s, :, 0:E1], pick[:, 0], pick[:, 1], ALU.add).then_inc(w_done[s], 1)
                wait(dve, w_done[s], n + 1)
                for t in range(T):
                    for e in range(E1):
                        if e % 4 == 0:
                            wait(dve, e_done[s], n * (2 * T) + (2 * t + e // 4 + 1))
                        if e:
                            wait(dve, acc_done[s], n * (T * E1) + (t * E1 + e))
                        nc.vector.scalar_tensor_tensor(
                            acc[:, s, t], ps_e[:, e // 4, e % 4 * C:(e % 4 + 1) * C], weight[:, s, t, e:e + 1],
                            acc[:, s, t] if e else x3[:, s, t], ALU.mult, ALU.add).then_inc(acc_done[s], 1)
                wait(dve, x_done[s], n + 1)
                wait(dve, acc_done[s], (n + 1) * (T * E1))
                wait(dve, stored[s], n * 64)
                nc.vector.tensor_tensor(out[:, s], ps_x[:], acc[:, s], ALU.add).then_inc(out_done[s], 1)

        def act_step(step, i, act):
            I, F, E = step.shift(2), step.shift(1), step
            if exists(i, 2):
                wait(act, i_done[I.s], I.before + 1)
                wait(act, f_done[I.s], I.before * HB)
                nc.scalar.copy(ht[:, I.s], ps_h[:]).then_inc(ht_done[I.s], 1)
            if exists(i, 1):
                for hb in (0, 2):
                    wait(act, f_done[F.s], F.before * HB + hb + 1)
                    wait(act, g_done[F.s], F.before)
                    nc.scalar.activation(hid[:, F.s, hb], ps_f[:, hb % 2], ACT.Relu, bias=b0[:, hb:hb + 1])\
                        .then_inc(relu_act[F.s], 1)
            if exists(i, 0):
                s, n = E.s, E.before
                wait(act, t_done[s], n + 1)
                wait(act, e_done[s], n * 2 * T)
                nc.scalar.copy(ut[:, s], ps_t[:]).then_inc(ut_done[s], 1)
                wait(act, rl_done[s], n + 1)
                nc.scalar.activation(logit_t[:], ps_t[:, 0:P], ACT.Identity, bias=router_b[:, 0:1]).then_inc(rl_kept[s], 1)
                wait(act, diff_done[s], n + 1)
                nc.scalar.activation(ratio[:], diff[:], ACT.Exp).then_inc(ratio_done[s], 1)
                wait(act, wt_done[s], n + 1)
                nc.scalar.copy(weight_t[:], ps_t[:, 0:P]).then_inc(wt_kept[s], 1)

        def pe_step(step, i, pe):
            I, F, E = step.shift(2), step.shift(1), step

            def second(tiles):
                for t in tiles:
                    for hb in range(HB):
                        ins = nc.tensor.matmul(ps_g[:, t], hid[:, F.s, hb, t * P:(t + 1) * P], w1[:, hb],
                                               start=hb == 0, stop=hb == HB - 1)
                return ins

            if exists(i, 2):
                if I.place == 0:
                    wait(pe, z1_done, I.lap * 2 + 2)
                wait(pe, ht_done[1 - I.s], I.shift(-1).before + 1)
                for q in range(BX // 4):
                    nc.tensor.matmul(ps_h[:, q * 4 * BY:(q + 1) * 4 * BY], z1[:, q],
                                     basis[:, :, I.place * BY:(I.place + 1) * BY], start=q == 0, stop=False,
                                     skip_group_check=True)
                by_column = ps_h[:].rearrange("c (x q a) -> c q a x", x=BX, a=4)
                for q in range(BY // 4):
                    ins = nc.tensor.matmul(by_column[:, q], z2[:, I.place * (BY // 4) + q], basis_x[:], start=False,
                                           stop=q == BY // 4 - 1, skip_group_check=True)
                ins.then_inc(i_done[I.s], 1)
            if exists(i, 1):
                wait(pe, ht_done[F.s], F.before + 1)
                for hb in range(HB):
                    kept = relu_dve if hb % 2 else relu_act
                    if hb < 2:
                        wait(pe, kept[1 - F.s], (F.shift(-1).before + 1) * 2)
                    else:
                        wait(pe, kept[F.s], F.before * 2 + 1)
                    nc.tensor.matmul(ps_f[:, hb % 2], w0[:, hb], ht[:, F.s], start=True, stop=True).then_inc(f_done[F.s], 1)
            if exists(i, 0):
                wait(pe, u_done[E.s], E.before + 1)
                wait(pe, wt_kept[1 - E.s], E.shift(-1).before + 1)
                for t in range(T):
                    ins = nc.tensor.transpose(ps_t[:, t * P:(t + 1) * P], u[:, E.s, t], k.ident[:])
                ins.then_inc(t_done[E.s], 1)
            if exists(i, 1):
                wait(pe, relu_act[F.s], F.before * 2 + 2)
                wait(pe, relu_dve[F.s], F.before * 2 + 2)
                wait(pe, h2_done[1 - F.s], F.shift(-1).before + 1)
                second((0, 1))
            if exists(i, 0):
                wait(pe, ut_done[E.s], E.before + 1)
                for t in range(T):
                    ins = nc.tensor.matmul(ps_t[quarter(t), 0:P], router[:], ut[:, E.s, t * P:(t + 1) * P],
                                           start=True, stop=True)
                ins.then_inc(rl_done[E.s], 1)
            if exists(i, 1):
                second((2, 3)).then_inc(g_done[F.s], 1)
            if exists(i, 0):
                s, n = E.s, E.before
                wait(pe, rl_kept[s], n + 1)
                nc.tensor.transpose(ps_t[:, P:2 * P], logit_t[:], k.ident[:]).then_inc(rt_done[s], 1)
                for t in range(T):
                    for half in range(2):
                        if t:
                            wait(pe, acc_done[s], n * (T * E1) + ((t - 1) * E1 + half * 4 + 4))
                        elif E.place == 0:
                            wait(pe, acc_done[1 - s], (E.shift(-1).before + 1) * (T * E1))
                        else:
                            wait(pe, acc_done[1 - s], E.shift(-1).before * (T * E1) + ((T - 1) * E1 + half * 4 + 4))
                        nc.tensor.matmul(ps_e[:, half], ut[:, s, t * P:(t + 1) * P], we[:, half * 4:(half + 1) * 4],
                                         start=True, stop=True).then_inc(e_done[s], 1)
                wait(pe, w_done[s], n + 1)
                nc.tensor.transpose(ps_t[:, 0:P], weight[:, s].rearrange("p t e -> p (t e)"), k.ident[:]).then_inc(wt_done[s], 1)
                wait(pe, wt_kept[s], n + 1)
                wait(pe, out_done[1 - s], E.shift(-1).before + 1)
                for t in range(T):
                    ins = nc.tensor.matmul(ps_x[:, t], weight_t[:], eb[:, t], start=True, stop=True)
                ins.then_inc(x_done[s], 1)

        run = lambda eng, f: run_steps(eng, lambda step, i: f(step, i, eng), -2, 0, BLOCKS - U, BLOCKS, U)
        with nc.Block() as block:
            @block.sync
            def _(sp):
                def load(place, array):
                    loads.append(1)
                    sp.dma_start(place, array).then_inc(w_in, 16)

                loads = []
                sp.wait_ge(zeroed, 3)
                load(basis[:], d["inverse"].rearrange("p (a n) -> p a n", a=4))
                for a in range(4):
                    load(z2[quarter(a)], z2_v[a])
                load(w0[:].rearrange("c b h -> c (b h)"), d["L1_conv_ff_w0"])
                load(b0[:], d["L1_conv_ff_b0_t"])
                load(w1[:], d["L1_conv_ff_w1"].rearrange("(b h) o -> h b o", b=HB))
                load(b1[:], row_of(d["L1_conv_ff_b1"]))
                load(ln_g[:], row_of(d["L1_conv_ln_g"]))
                load(ln_b[:], row_of(d["L1_conv_ln_b"]))
                load(router[:, 0:E1], d["L1_ffn_router_w"])
                load(we[:], d["L1_ffn_expert_w"].rearrange("e c o -> c e o"))
                load(iota[:], d["iota8"].rearrange("p (t e) -> p t e", t=T))
                for t in range(T):
                    rows = slice(32 * t, 32 * t + E1)
                    load(router_b[rows], d["L1_ffn_router_b"].rearrange("(e a) -> e a", a=1))
                    load(eb[rows, t], d["L1_ffn_expert_b"])
                assert len(loads) == LOADS
                run(sp, sp_step)
                for s in range(2):
                    sp.wait_ge(stored[s], 64 * BLOCKS // 2)

            @block.gpsimd
            def _(pool):
                nc.gpsimd.memset(zero_z[:], 0.0).then_inc(zeroed, 1)
                pool.wait_ge(w_in, 16 * LOADS)
                run(pool, pool_step)

            @block.vector
            def _(dve):
                nc.vector.memset(router[:], 0.0)
                nc.vector.memset(router_b[:], 0.0)
                nc.vector.memset(eb[:], 0.0).then_inc(zeroed, 1)
                nc.vector.memset(weight[:], 0.0).then_inc(zeroed, 1)
                dve.wait_ge(w_in, 16 * LOADS)
                dve.wait_ge(zeroed, 3)
                run(dve, dve_step)

            @block.scalar
            def _(act):
                act.wait_ge(w_in, 16 * LOADS)
                run(act, act_step)

            @block.tensor
            def _(pe):
                pe.wait_ge(w_in, 16 * LOADS)
                run(pe, pe_step)


def program(nc, dram):
    with ExitStack() as ctx:
        k = Core(nc, ctx, dram)
        load_constants(k)
        k.end_phase()
        with ExitStack() as part:
            bias = k.sb(part, "bias", [P, 2, NH, N])
            bias_pass(k, bias)
            k.end_phase()
            attention(k, bias)
            k.end_phase()
        with ExitStack() as part:
            kept_top = k.sb(part, "kept_top", [P, TILES // 8 * K0])
            kept_at = k.sb(part, "kept_at", [P, TILES // 8 * K0], U32)
            kept_sum = k.sb(part, "kept_sum", [P, TILES // 8])
            gate_pass(k, kept_top, kept_at, kept_sum)
            k.end_phase()
            experts(k, kept_top, kept_at, kept_sum)
            k.end_phase()
        spectra(k)
        layer1(k)


def shape_constants():
    mode = np.arange(NM)
    angle = 2 * np.pi * np.outer(np.arange(N), mode) / N
    forward = np.concatenate([np.cos(angle), -np.sin(angle)], 1) / np.sqrt(N)
    twice = np.where(mode == 0, 1.0, 2.0)[:, None] / np.sqrt(N)
    inverse = np.concatenate([twice * np.cos(angle.T), -twice * np.sin(angle.T)], 0)
    diagonal = np.zeros((4, M2, 4, N))
    for a in range(4):
        diagonal[a, :, a] = inverse
    step, half = np.arange(TILES // 8 * K0)[None] // K0, np.arange(P)[:, None] // E0
    tables = {
        "identity": np.eye(P),
        "offs": step * 1024 + half * 512,
        "iota": np.broadcast_to(np.arange(TILES // 8 * 2 * K0), (E0, TILES // 8 * 2 * K0)),
        "upper": np.triu(np.ones((E0, E0)), 1),
        "forward": forward,
        "inverse": diagonal.reshape(P, 4 * N),
        "iota8": np.broadcast_to(np.tile(np.arange(E1), 4), (P, 4 * E1)),
    }
    return {n: np.ascontiguousarray(a, dtype=np.float32) for n, a in tables.items()}


def kernel(**inputs):
    import concourse.bacc as bacc
    from concourse.bass_utils import run_bass_kernel_spmd

    arrays = {n: np.ascontiguousarray(a) for n, a in inputs.items() if n != "L1_conv_ff_b0"}
    arrays["L1_conv_ff_b0_t"] = np.ascontiguousarray(np.asarray(inputs["L1_conv_ff_b0"]).reshape(H1 // P, P).T)
    arrays.update(shape_constants())
    nc = bacc.Bacc("TRN2", target_bir_lowering=False, num_devices=1)
    dram = {n: nc.dram_tensor(n, a.shape, F32, kind="ExternalInput").ap() for n, a in arrays.items()}
    dram["x1"] = nc.dram_tensor("x1", (TOK, C), F32, kind="Internal").ap()
    for n in ("z1", "z2"):
        dram[n] = nc.dram_tensor(n, (2, NM, N, C), F32, kind="Internal").ap()
    dram["out"] = nc.dram_tensor("out", (1, N, N, C), F32, kind="ExternalOutput").ap()
    program(nc, dram)
    return run_bass_kernel_spmd(nc, [arrays], core_ids=[0]).results[0]["out"]
```

```python
from contextlib import ExitStack

import numpy as np

import concourse.bass as bass
from concourse import mybir

F32 = mybir.dt.float32
U32 = mybir.dt.uint32
ALU = mybir.AluOpType
ACT = mybir.ActivationFunctionType
AXX = mybir.AxisListType.X

P = 128
C = 128
N = 256
TOK = N * N
TILES = TOK // P
NH = 4
HD = 32
E0 = 64
K0 = 8
H0 = 512
NM = 16
M2 = 2 * NM
H1 = 512
E1 = 8
LOW = -3.0e38


class Core:

    def __init__(self, nc, ctx, dram):
        self.nc, self.ctx, self.d = nc, ctx, dram
        self.phase_sems, self.unprimed = [], []
        self.passed = nc.alloc_semaphore("passed")

    def sem(self, name, from_zero=False):
        handle = self.nc.alloc_semaphore(name)
        self.phase_sems.append(handle)
        if not from_zero:
            self.unprimed.append(handle)
        return handle

    def end_phase(self):
        self.nc.clear_and_free_semaphores(self.phase_sems)
        self.phase_sems, self.unprimed = [], []
        self.nc.all_engine_barrier()

    def prime(self, eng):
        for handle in self.unprimed:
            eng.sem_inc(handle, 1)
        self.unprimed = []

    def wait_alone(self, eng, sem, value):
        eng.wait_ge(sem, counted(value))
        eng.sem_inc(self.passed, 1)

    def sb(self, ctx, name, shape, dt=F32):
        return ctx.enter_context(self.nc.sbuf_tensor(name, shape, dt))

    def ps(self, ctx, name, shape, dt=F32):
        return ctx.enter_context(self.nc.psum_tensor(name, shape, dt))


def counted(value):
    return max(value, 0) + 1 if isinstance(value, int) else value + 1


def row_of(vector):
    return vector.rearrange("(a n) -> a n", a=1).broadcast_to([P, vector.shape[0]])


def load_constants(k):
    nc, d = k.nc, k.d
    k.ident = k.sb(k.ctx, "ident", [P, P])
    k.gamma = k.sb(k.ctx, "gamma", [C, 1])
    k.beta = k.sb(k.ctx, "beta", [C, 1])
    k.mean = k.sb(k.ctx, "mean", [P, TILES])
    k.rstd = k.sb(k.ctx, "rstd", [P, TILES])
    k.mhalf = k.sb(k.ctx, "mhalf", [P, 16])
    consts_in = k.sem("consts_in")
    half_set = k.sem("half_set")
    with nc.Block() as block:
        @block.sync
        def _(sp):
            k.prime(sp)
            sp.dma_start(k.ident[:], d["identity"]).then_inc(consts_in, 16)
            sp.dma_start(k.gamma[:], d["L0_conv_ln_gamma"].rearrange("(c a) -> c a", a=1)).then_inc(consts_in, 16)
            sp.dma_start(k.beta[:], d["L0_conv_ln_beta"].rearrange("(c a) -> c a", a=1)).then_inc(consts_in, 16)
            sp.wait_ge(consts_in, counted(48))

        @block.gpsimd
        def _(pool):
            nc.gpsimd.memset(k.mhalf[:], -0.5).then_inc(half_set, 1)
            pool.wait_ge(half_set, counted(1))


class Turn:

    def __init__(self, place, lap, of):
        self.place, self.lap, self.of = place, lap, of
        self.s, self.before = place % 2, lap * (of // 2) + place // 2

    def shift(self, by):
        return Turn((self.place + by) % self.of, self.lap + (self.place + by) // self.of, self.of)

    @property
    def index(self):
        return self.lap * self.of + self.place


def run_steps(eng, step, first, head, tail, last, of=2):
    for i in range(first, head):
        step(Turn(i % of, i // of, of), i)
    with eng.Fori(0, (tail - head) // of) as r:
        for place in range(of):
            step(Turn(place, r + head // of, of), None)
    for i in range(tail, last):
        step(Turn(i % of, i // of, of), i)


def bias_pass(k, bias):
    nc, d = k.nc, k.d
    G = 8
    STEPS = TILES // G
    ON_DVE = 4
    LAP = 4
    with ExitStack() as ctx:
        xin = k.sb(ctx, "b_xin", [P, 4, G, C])
        xn = k.sb(ctx, "b_xn", [P, 2, G, C])
        zt = k.sb(ctx, "b_zt", [C, 2, G, P])
        wb = k.sb(ctx, "b_wb", [C, 32])
        stats = k.sb(ctx, "b_stats", [P, 2, G, 6])
        mv = k.sb(ctx, "b_mv", [P, 2, G, 2])
        var, rstd, nmean, shift = (k.sb(ctx, "b_" + n, [P, 2, G]) for n in ("var", "rstd", "nmean", "shift"))
        bias_t = k.sb(ctx, "b_bias_t", [2 * 32, 2, G // 2 * P])
        ps_t = k.ps(ctx, "b_ps_t", [C, 2, G, P])
        ps_b = k.ps(ctx, "b_ps_b", [P, 2, 512])
        wb_in, wb_zero, bias_in = k.sem("b_wb_in"), k.sem("b_wb_zero"), k.sem("b_bias_in")
        stored = [k.sem(f"b_stored{s}") for s in range(2)]
        x_in = [k.sem(f"b_x_in{s}") for s in range(4)]
        stats_done, mv_done, var_done, mean_kept, rstd_done, shift_done, rstd_kept = (k.sem("b_" + n) for n in (
            "stats_done", "mv_done", "var_done", "mean_kept", "rstd_done", "shift_done", "rstd_kept"))
        xn_dve, xn_act, t_done, zt_done, b_done, b_kept = (k.sem("b_" + n) for n in (
            "xn_dve", "xn_act", "t_done", "zt_done", "b_done", "b_kept"))
        x_v = d["x"].rearrange("a i k c -> (a i k) c").rearrange("(n t p) c -> n p t c", t=G, p=P)

        bias_v = d["bias"].rearrange("h j c -> h (j c)").rearrange("h (n a q) -> n a h q", a=2, q=G // 2 * P)

        def exists(i, by):
            return i is None or 0 <= i + by < STEPS

        def sp_step(step, i, sp):
            if exists(i, 4):
                L = step.shift(4)
                k.wait_alone(sp, xn_dve, L.index - 3)
                k.wait_alone(sp, xn_act, L.index - 3)
                sp.dma_start(xin[:, L.place], x_v[L.index]).then_inc(x_in[L.place], 16)
            if exists(i, 0):
                O = step
                k.wait_alone(sp, b_kept, O.index + 1)
                for half in range(2):
                    sp.dma_start(bias_v[O.index, half], bias_t[half * 32:half * 32 + NH, O.s]).then_inc(stored[O.s], 16)

        def pool_step(step, i, pool):
            if exists(i, 3):
                A = step.shift(3)
                pool.wait_ge(xn_act, counted(A.index - 1))
                pool.wait_ge(var_done, counted(A.index + 1))
                nc.gpsimd.tensor_tensor(rstd[:, A.s], var[:, A.s], k.mhalf[:, 0:G], ALU.pow).then_inc(rstd_done, 1)
                pool.wait_ge(rstd_done, counted(A.index + 1))
                nc.gpsimd.tensor_tensor(shift[:, A.s], nmean[:, A.s], rstd[:, A.s], ALU.mult).then_inc(shift_done, 1)

        def dve_step(step, i, dve):
            B, A = step.shift(2), step.shift(3)
            if exists(i, 3):
                dve.wait_ge(x_in[A.place], counted(A.lap * 16 + 16))
                for t in range(G):
                    ins = nc.vector.bn_stats(stats[:, A.s, t], xin[:, A.place, t])
                ins.then_inc(stats_done, 1)
            if exists(i, 2):
                dve.wait_ge(rstd_done, counted(B.index + 1))
                dve.wait_ge(t_done, counted(B.index - 1))
                for t in range(ON_DVE):
                    ins = nc.vector.tensor_scalar(xn[:, B.s, t], xin[:, B.place, t], mv[:, B.s, t, 0:1],
                                                  rstd[:, B.s, t:t + 1], ALU.subtract, ALU.mult)
                ins.then_inc(xn_dve, 1)
                nc.vector.tensor_copy(k.rstd[:, bass.ds(B.index * G, G)], rstd[:, B.s]).then_inc(rstd_kept, 1)
            if exists(i, 3):
                k.wait_alone(dve, stats_done, A.index + 1)
                for t in range(G):
                    ins = nc.vector.bn_aggr(mv[:, A.s, t], stats[:, A.s, t])
                ins.then_inc(mv_done, 1)
                dve.wait_ge(mv_done, counted(A.index + 1))
                nc.vector.tensor_scalar(nmean[:, A.s], mv[:, A.s, :, 0], -1.0, None, ALU.mult)
                nc.vector.tensor_scalar(var[:, A.s], mv[:, A.s, :, 1], 1.0 + 1e-5, 1e-11, ALU.mult, ALU.add)\
                    .then_inc(var_done, 1)
                nc.vector.tensor_copy(k.mean[:, bass.ds(A.index * G, G)], mv[:, A.s, :, 0]).then_inc(mean_kept, 1)

        def act_step(step, i, act):
            O, M, B = step, step.shift(1), step.shift(2)
            if exists(i, 2):
                act.wait_ge(shift_done, counted(B.index + 1))
                act.wait_ge(t_done, counted(B.index - 1))
                for t in range(ON_DVE, G):
                    ins = nc.scalar.activation(xn[:, B.s, t], xin[:, B.place, t], ACT.Identity,
                                               bias=shift[:, B.s, t:t + 1], scale=rstd[:, B.s, t:t + 1])
                ins.then_inc(xn_act, 1)
            if exists(i, 0):
                act.wait_ge(b_done, counted(O.index + 1))
                act.wait_ge(stored[O.s], counted(O.before * 32))
                nc.scalar.copy(bias_t[:, O.s], ps_b[0:2 * 32, O.s]).then_inc(b_kept, 1)
            if exists(i, 1):
                act.wait_ge(t_done, counted(M.index + 1))
                act.wait_ge(b_done, counted(M.index - 1))
                for half in range(2):
                    a, b = half * G // 2, (half + 1) * G // 2
                    nc.scalar.activation(zt[:, M.s, a:b], ps_t[:, M.s, a:b], ACT.Identity, bias=k.beta[:, 0:1],
                                         scale=k.gamma[:, 0:1]).then_inc(zt_done, 1)

        def pe_step(step, i, pe):
            M, B = step.shift(1), step.shift(2)
            if exists(i, 2):
                pe.wait_ge(xn_dve, counted(B.index + 1))
                pe.wait_ge(xn_act, counted(B.index + 1))
                pe.wait_ge(zt_done, counted((B.index - 1) * 2))
                for t in range(G):
                    ins = nc.tensor.transpose(ps_t[:, B.s, t], xn[:, B.s, t], k.ident[:])
                ins.then_inc(t_done, 1)
            if exists(i, 1):
                pe.wait_ge(zt_done, counted(M.index * 2 + 2))
                pe.wait_ge(b_kept, counted(M.index - 1))
                for half in range(2):
                    ins = nc.tensor.matmul(ps_b[half * 32:(half + 1) * 32, M.s], wb[:],
                                           zt[:, M.s, half * G // 2:(half + 1) * G // 2], start=True, stop=True)
                ins.then_inc(b_done, 1)

        run = lambda eng, f: run_steps(eng, lambda step, i: f(step, i, eng), -4, 0, STEPS - LAP, STEPS, LAP)
        with nc.Block() as block:
            @block.sync
            def _(sp):
                k.prime(sp)
                sp.wait_ge(wb_zero, counted(1))
                sp.dma_start(wb[:, 0:NH], d["L0_conv_Wb"]).then_inc(wb_in, 16)
                run(sp, sp_step)
                for s in range(2):
                    sp.wait_ge(stored[s], counted(STEPS // 2 * 32))
                for h in range(NH):
                    sp.dma_start(bias[:, :, h], d["bias"][h].rearrange("(b p) c -> p b c", p=P)).then_inc(bias_in, 16)
                sp.wait_ge(bias_in, counted(16 * NH))

            @block.gpsimd
            def _(pool):
                nc.gpsimd.memset(wb[:], 0.0).then_inc(wb_zero, 1)
                run(pool, pool_step)

            @block.vector
            def _(dve):
                run(dve, dve_step)

            @block.tensor
            def _(pe):
                pe.wait_ge(wb_in, counted(16))
                run(pe, pe_step)

            @block.scalar
            def _(act):
                run(act, act_step)


def attention(k, bias):
    nc, d = k.nc, k.d
    SCALE = float(HD) ** -0.25
    B = 2
    with ExitStack() as ctx:
        sb = lambda name, shape: k.sb(ctx, "a_" + name, shape)
        wqk, wg, wv, wo = sb("wqk", [C, 2, C]), sb("wg", [C, C]), sb("wv", [C, C]), sb("wo", [C, C])
        bg, bg_half, bo = sb("bg", [C, 1]), sb("bg_half", [C, 1]), sb("bo", [P, C])
        xr, xn, xo = (sb(n, [P, 2, B, C]) for n in ("xr", "xn", "xo"))
        xb = sb("xb", [P, 4, B, C])
        v = sb("v", [P, 2, B * C])
        zt = sb("zt", [C, 2, N])
        qk = sb("qk", [C, 2, 2, N])
        keys = sb("keys", [C, 2, NH, N])
        g, gate, vals = (sb(n, [C, 2, N]) for n in ("g", "gate", "vals"))
        prob = sb("prob", [P, 2, NH, B, N])
        top, ntop, total, rden = (sb(n, [P, 2, NH, B]) for n in ("top", "ntop", "total", "rden"))
        share = sb("share", [P, 2, B, C])
        pt = sb("pt", [P, NH, B, N])
        ps_s = k.ps(ctx, "a_ps_s", [P, NH, B, N])
        ps_p = k.ps(ctx, "a_ps_p", [P, 2, B, N])
        ps_a = k.ps(ctx, "a_ps_a", [P, 2, N])
        ps_o = k.ps(ctx, "a_ps_o", [P, 2, N])

        pair = lambda name: [k.sem(f"a_{name}{s}") for s in range(2)]
        w_in, ready = k.sem("a_w_in"), k.sem("a_ready")
        x_in, stored = pair("x_in"), pair("stored")
        xn_done, keys_done, top_done, ntop_done, rden_done, pt_even, gate_done, vals_done, xo_done = map(
            pair, ("xn_done", "keys_done", "top_done", "ntop_done", "rden_done", "pt_even", "gate_done", "vals_done", "xo_done"))
        zt_done, qk_kept, tanh_done, v_kept, exp_done, pt_odd = map(
            pair, ("zt_done", "qk_kept", "tanh_done", "v_kept", "exp_done", "pt_odd"))
        t_done, qk_done, gv_done, s_done, pt_done, av_done, share_turned, y_done = map(
            pair, ("t_done", "qk_done", "gv_done", "s_done", "pt_done", "av_done", "share_turned", "y_done"))
        xb_done, share_done = map(pair, ("xb_done", "share_done"))

        x_v = d["x"].rearrange("a i (b p) c -> (a i) p b c", p=P)
        x1_v = d["x1"].rearrange("(i b p) c -> i p b c", b=B, p=P)

        def exists(i, by):
            return i is None or 0 <= i + by < N

        def head(h):
            return slice(h * HD, (h + 1) * HD)

        def sp_step(step, i, sp):
            if exists(i, 2):
                L = step.shift(2)
                k.wait_alone(sp, xn_done[L.s], L.before)
                k.wait_alone(sp, xb_done[L.s], L.before)
                sp.dma_start(xr[:, L.s], x_v[L.index]).then_inc(x_in[L.s], 16)
            if exists(i, -3):
                row = step.shift(-3)
                k.wait_alone(sp, xo_done[row.s], row.before + 1)
                sp.dma_start(x1_v[row.index], xo[:, row.s]).then_inc(stored[row.s], 16)

        def pool_step(step, i, pool):
            L, D = step.shift(2), step.shift(-1)
            if exists(i, -1):
                k.wait_alone(pool, rden_done[D.s], D.before + 1)
                k.wait_alone(pool, share_turned[D.s], D.before)
                nc.gpsimd.tensor_copy(share[:, D.s].rearrange("p b (h c) -> p b h c", h=NH),
                                      rden[:, D.s].rearrange("p h b -> p b h").unsqueeze(3).broadcast_to([P, B, NH, HD]))\
                    .then_inc(share_done[D.s], 1)
            if exists(i, 2):
                pool.wait_ge(x_in[L.s], counted(L.before * 16 + 16))
                pool.wait_ge(xo_done[L.s], counted(L.before - 1))
                nc.gpsimd.tensor_tensor(xb[:, L.place], xr[:, L.s], bo[:].unsqueeze(1).broadcast_to([P, B, C]),
                                        ALU.add).then_inc(xb_done[L.s], 1)

        def dve_step(step, i, dve):
            L, A, R, D, O = (step.shift(by) for by in (2, 1, 0, -1, -2))

            def turned(h):
                dve.wait_ge(pt_done[D.s], counted(D.before * 4 + (h + 1)))
                dve.wait_ge(av_done[1 - D.s], counted(D.shift(-1).before + 1))
                nc.vector.tensor_copy(pt[:, h], ps_p[:, 0]).then_inc(pt_even[D.s], 1)

            def scored(h):
                dve.wait_ge(s_done[R.s], counted(R.before * 4 + (h + 1)))
                k.wait_alone(dve, pt_done[R.s], R.before * 4)
                for b in range(B):
                    ins = nc.vector.tensor_tensor_reduce(prob[:, R.s, h, b], ps_s[:, h, b], bias[:, b, h], 1.0, LOW,
                                                         ALU.add, ALU.max, top[:, R.s, h, b:b + 1])
                ins.then_inc(top_done[R.s], 1)
                if h % 2:
                    dve.wait_ge(top_done[R.s], counted(R.before * 4 + (h + 1)))
                    nc.vector.tensor_scalar(ntop[:, R.s, h - 1:h + 1], top[:, R.s, h - 1:h + 1], -1.0, None, ALU.mult)\
                        .then_inc(ntop_done[R.s], 1)

            if exists(i, 0):
                scored(0)
                scored(1)
            if exists(i, -2):
                dve.wait_ge(y_done[O.s], counted(O.before + 1))
                dve.wait_ge(xb_done[O.s], counted(O.before + 1))
                dve.wait_ge(stored[O.s], counted(O.before * 16))
                nc.vector.scalar_tensor_tensor(xo[:, O.s].rearrange("p b c -> p (b c)"), ps_o[:, 0], 0.5,
                                               xb[:, O.place].rearrange("p b c -> p (b c)"), ALU.mult, ALU.add)\
                    .then_inc(xo_done[O.s], 1)
            if exists(i, -1):
                turned(0)
                dve.wait_ge(exp_done[D.s], counted(D.before * 4 + 4))
                dve.wait_ge(share_done[D.s], counted(D.before))
                nc.vector.reciprocal(rden[:, D.s], total[:, D.s]).then_inc(rden_done[D.s], 1)
            if exists(i, 0):
                scored(2)
            if exists(i, -1):
                turned(2)
            if exists(i, 0):
                scored(3)
            if exists(i, 2):
                dve.wait_ge(x_in[L.s], counted(L.before * 16 + 16))
                dve.wait_ge(t_done[L.s], counted(L.before))
                for b in range(B):
                    col = bass.ds(L.index * B + b, 1)
                    ins = nc.vector.tensor_scalar(xn[:, L.s, b], xr[:, L.s, b], k.mean[:, col], k.rstd[:, col],
                                                  ALU.subtract, ALU.mult)
                ins.then_inc(xn_done[L.s], 1)
            if exists(i, 1):
                dve.wait_ge(qk_kept[A.s], counted(A.before + 1))
                dve.wait_ge(s_done[A.s], counted(A.before * NH))
                for h in range(NH):
                    ins = nc.vector.tensor_copy(keys[head(h), A.s, h], qk[head(h), A.s, 1])
                ins.then_inc(keys_done[A.s], 1)
            if exists(i, -1):
                dve.wait_ge(share_turned[D.s], counted(D.before + 1))
                dve.wait_ge(tanh_done[D.s], counted(D.before + 1))
                dve.wait_ge(av_done[D.s], counted(D.before + 1))
                nc.vector.scalar_tensor_tensor(gate[:, D.s], g[:, D.s], 1.0, ps_o[:, 1], ALU.add, ALU.mult)\
                    .then_inc(gate_done[D.s], 1)
                dve.wait_ge(gate_done[D.s], counted(D.before + 1))
                dve.wait_ge(y_done[D.s], counted(D.before))
                nc.vector.tensor_tensor(vals[:, D.s], ps_o[:, 0], gate[:, D.s], ALU.mult).then_inc(vals_done[D.s], 1)

        def act_step(step, i, act):
            A, R, D = step.shift(1), step, step.shift(-1)

            def turned(h):
                act.wait_ge(pt_done[D.s], counted(D.before * 4 + (h + 1)))
                act.wait_ge(av_done[1 - D.s], counted(D.shift(-1).before + 1))
                nc.scalar.copy(pt[:, h], ps_p[:, 1]).then_inc(pt_odd[D.s], 1)

            def exps(row, h):
                act.wait_ge(ntop_done[row.s], counted(row.before * 2 + (h // 2 + 1)))
                act.wait_ge(rden_done[row.s], counted(row.before))
                for b in range(B):
                    ins = nc.scalar.activation(prob[:, row.s, h, b], prob[:, row.s, h, b], ACT.Exp,
                                               bias=ntop[:, row.s, h, b:b + 1], accum_out=total[:, row.s, h, b:b + 1])
                ins.then_inc(exp_done[row.s], 1)

            if exists(i, -1):
                exps(D, 2)
                exps(D, 3)
            if exists(i, 1):
                act.wait_ge(t_done[A.s], counted(A.before + 1))
                act.wait_ge(gv_done[A.s], counted(A.before))
                nc.scalar.activation(zt[:, A.s], ps_a[:, 0], ACT.Identity,
                                     bias=k.beta[:, 0:1], scale=k.gamma[:, 0:1]).then_inc(zt_done[A.s], 1)
            if exists(i, -1):
                turned(1)
                turned(3)
            if exists(i, 1):
                act.wait_ge(qk_done[A.s], counted(A.before + 1))
                act.wait_ge(s_done[A.s], counted(A.before * 4))
                act.wait_ge(keys_done[A.s], counted(A.before))
                nc.scalar.activation(qk[:, A.s], ps_a[:], ACT.Copy, scale=SCALE).then_inc(qk_kept[A.s], 1)
            if exists(i, 0):
                exps(R, 0)
            if exists(i, 1):
                act.wait_ge(gv_done[A.s], counted(A.before + 1))
                act.wait_ge(gate_done[A.s], counted(A.before))
                nc.scalar.activation(g[:, A.s], ps_a[:, 0], ACT.Tanh, bias=bg_half[:, 0:1], scale=0.5)\
                    .then_inc(tanh_done[A.s], 1)
                act.wait_ge(av_done[A.s], counted(A.before))
                nc.scalar.copy(v[:, A.s], ps_a[:, 1]).then_inc(v_kept[A.s], 1)
            if exists(i, 0):
                exps(R, 1)

        def pe_step(step, i, pe):
            A, R, D, O = (step.shift(by) for by in (1, 0, -1, -2))

            def turn(h):
                kept = pt_odd if h % 2 else pt_even
                pe.wait_ge(exp_done[D.s], counted(D.before * 4 + (h + 1)))
                if h < 2:
                    pe.wait_ge(kept[1 - D.s], counted((D.shift(-1).before + 1) * 2))
                else:
                    pe.wait_ge(kept[D.s], counted(D.before * 2 + 1))
                for kb in range(B):
                    for b in range(B):
                        ins = nc.tensor.transpose(ps_p[:, h % 2, kb, b * P:(b + 1) * P],
                                                  prob[:, D.s, h, b, kb * P:(kb + 1) * P], k.ident[:])
                ins.then_inc(pt_done[D.s], 1)

            def score(h):
                if h == 0:
                    pe.wait_ge(keys_done[R.s], counted(R.before + 1))
                pe.wait_ge(top_done[1 - R.s], counted(R.shift(-1).before * 4 + (h + 1)))
                for b in range(B):
                    ins = nc.tensor.matmul(ps_s[:, h, b], qk[:, R.s, 0, b * P:(b + 1) * P], keys[:, R.s, h],
                                           start=True, stop=True)
                ins.then_inc(s_done[R.s], 1)

            if exists(i, 0):
                score(0)
                score(1)
            if exists(i, 1):
                pe.wait_ge(xn_done[A.s], counted(A.before + 1))
                pe.wait_ge(v_kept[1 - A.s], counted(A.shift(-1).before + 1))
                for b in range(B):
                    ins = nc.tensor.transpose(ps_a[:, 0, b * P:(b + 1) * P], xn[:, A.s, b], k.ident[:])
                ins.then_inc(t_done[A.s], 1)
            if exists(i, -2):
                pe.wait_ge(vals_done[O.s], counted(O.before + 1))
                for b in range(B):
                    ins = nc.tensor.matmul(ps_o[:, 0, b * C:(b + 1) * C], vals[:, O.s, b * P:(b + 1) * P], wo[:],
                                           start=True, stop=True)
                ins.then_inc(y_done[O.s], 1)
            if exists(i, -1):
                turn(0)
                turn(1)
            if exists(i, 0):
                score(2)
            if exists(i, -1):
                turn(2)
            if exists(i, 0):
                score(3)
            if exists(i, -1):
                turn(3)
            if exists(i, 1):
                pe.wait_ge(zt_done[A.s], counted(A.before + 1))
                for a in range(2):
                    ins = nc.tensor.matmul(ps_a[:, a], wqk[:, a], zt[:, A.s], start=True, stop=True)
                ins.then_inc(qk_done[A.s], 1)
            if exists(i, -1):
                pe.wait_ge(xo_done[1 - D.s], counted(D.shift(-1).before + 1))
                pe.wait_ge(share_done[D.s], counted(D.before + 1))
                for b in range(B):
                    ins = nc.tensor.transpose(ps_o[:, 1, b * P:(b + 1) * P], share[:, D.s, b], k.ident[:])
                ins.then_inc(share_turned[D.s], 1)
                pe.wait_ge(pt_even[D.s], counted(D.before * 2 + 2))
                pe.wait_ge(pt_odd[D.s], counted(D.before * 2 + 2))
                pe.wait_ge(v_kept[D.s], counted(D.before + 1))
                for kb in range(B):
                    for h in range(NH):
                        ins = nc.tensor.matmul(ps_o[head(h), 0], v[:, D.s, kb * C + h * HD:kb * C + (h + 1) * HD],
                                               pt[:, h, kb], start=kb == 0, stop=kb == B - 1)
                ins.then_inc(av_done[D.s], 1)
            if exists(i, 1):
                pe.wait_ge(qk_kept[A.s], counted(A.before + 1))
                nc.tensor.matmul(ps_a[:, 0], wg[:], zt[:, A.s], start=True, stop=True)
                for b in range(B):
                    ins = nc.tensor.matmul(ps_a[:, 1, b * C:(b + 1) * C], zt[:, A.s, b * P:(b + 1) * P], wv[:],
                                           start=True, stop=True)
                ins.then_inc(gv_done[A.s], 1)

        run = lambda eng, f: run_steps(eng, lambda step, i: f(step, i, eng), -2, 4, N - 4, N + 3, 4)
        with nc.Block() as block:
            @block.sync
            def _(sp):
                k.prime(sp)
                for place, name in ((wqk[:, 0], "Wq"), (wqk[:, 1], "Wk"), (wg[:], "Wg"), (wv[:], "Wv"), (wo[:], "Wo")):
                    sp.dma_start(place, d["L0_conv_" + name]).then_inc(w_in, 16)
                sp.dma_start(bg[:], d["L0_conv_bg"].rearrange("(c a) -> c a", a=1)).then_inc(w_in, 16)
                sp.dma_start(bo[:], row_of(d["L0_conv_bo"])).then_inc(w_in, 16)
                run(sp, sp_step)
                for s in range(2):
                    sp.wait_ge(stored[s], counted(16 * N // 2))

            @block.gpsimd
            def _(pool):
                nc.gpsimd.memset(keys[:], 0.0).then_inc(ready, 1)
                pool.wait_ge(w_in, counted(16 * 7))
                pool.wait_ge(ready, counted(2))
                run(pool, pool_step)

            @block.vector
            def _(dve):
                dve.wait_ge(w_in, counted(16 * 7))
                nc.vector.tensor_scalar(bg_half[:], bg[:], 0.5, None, ALU.mult).then_inc(ready, 1)
                run(dve, dve_step)

            @block.scalar
            def _(act):
                act.wait_ge(ready, counted(2))
                run(act, act_step)

            @block.tensor
            def _(pe):
                pe.wait_ge(w_in, counted(16 * 7))
                run(pe, pe_step)


def gate_pass(k, kept_top, kept_at, kept_sum):
    nc, d = k.nc, k.d
    G = 8
    STEPS = TILES // G
    HALF = G // 2 * P
    ON_DVE = 4
    LAP = 4
    with ExitStack() as ctx:
        sb = lambda name, shape, dt=F32: k.sb(ctx, "g_" + name, shape, dt)
        xin, xn = sb("xin", [P, 4, G, C]), sb("xn", [P, 2, G, C])
        ut = sb("ut", [C, 2, G, P])
        stats, mv = sb("stats", [P, 2, G, 6]), sb("mv", [P, 2, G, 2])
        var, rstd, nmean, shift = (sb(n, [P, 2, G]) for n in ("var", "rstd", "nmean", "shift"))
        gate_in, gate_t, gate_b = sb("gate_in", [E0, C]), sb("gate_t", [C, E0]), sb("gate_b", [2 * E0, 1])
        logit, ex = sb("logit", [P, 2, HALF]), sb("ex", [P, HALF])
        best, at, nbest, esum = sb("best", [P, 2, K0]), sb("at", [P, 2, K0], U32), sb("nbest", [P, 2]), sb("esum", [P, 2])
        ps_t = k.ps(ctx, "g_ps_t", [C, 2, G, P])
        ps_l = k.ps(ctx, "g_ps_l", [P, 2, HALF])
        ps_g = k.ps(ctx, "g_ps_g", [C, 512])
        w_in, gate_turned, gate_kept = k.sem("g_w_in"), k.sem("g_gate_turned"), k.sem("g_gate_kept")
        x_in = [k.sem(f"g_x_in{s}") for s in range(4)]
        stats_done, mv_done, var_done, rstd_done, shift_done = (k.sem("g_" + n) for n in (
            "stats_done", "mv_done", "var_done", "rstd_done", "shift_done"))
        xn_dve, xn_act, t_done, ut_done, l_done, logit_done = (k.sem("g_" + n) for n in (
            "xn_dve", "xn_act", "t_done", "ut_done", "l_done", "logit_done"))
        best_done, nbest_done, at_done, esum_done, kept = (k.sem("g_" + n) for n in (
            "best_done", "nbest_done", "at_done", "esum_done", "kept"))
        x_v = d["x1"].rearrange("(n t p) c -> n p t c", t=G, p=P)

        def exists(i, by):
            return i is None or 0 <= i + by < STEPS

        def sp_step(step, i, sp):
            if exists(i, 5):
                L = step.shift(5)
                k.wait_alone(sp, xn_dve, L.index - 3)
                k.wait_alone(sp, xn_act, L.index - 3)
                sp.dma_start(xin[:, L.place], x_v[L.index]).then_inc(x_in[L.place], 16)

        def pool_step(step, i, pool):
            if exists(i, 4):
                A = step.shift(4)
                pool.wait_ge(xn_act, counted(A.index - 1))
                pool.wait_ge(var_done, counted(A.index + 1))
                nc.gpsimd.tensor_tensor(rstd[:, A.s], var[:, A.s], k.mhalf[:, 0:G], ALU.pow).then_inc(rstd_done, 1)
                pool.wait_ge(rstd_done, counted(A.index + 1))
                nc.gpsimd.tensor_tensor(shift[:, A.s], nmean[:, A.s], rstd[:, A.s], ALU.mult).then_inc(shift_done, 1)

        def dve_step(step, i, dve):
            O, S, B, A = step, step.shift(1), step.shift(3), step.shift(4)
            if exists(i, 4):
                dve.wait_ge(x_in[A.place], counted(A.lap * 16 + 16))
                for t in range(G):
                    ins = nc.vector.bn_stats(stats[:, A.s, t], xin[:, A.place, t])
                ins.then_inc(stats_done, 1)
            if exists(i, 3):
                dve.wait_ge(rstd_done, counted(B.index + 1))
                dve.wait_ge(t_done, counted(B.index - 1))
                for t in range(ON_DVE):
                    ins = nc.vector.tensor_scalar(xn[:, B.s, t], xin[:, B.place, t], mv[:, B.s, t, 0:1],
                                                  rstd[:, B.s, t:t + 1], ALU.subtract, ALU.mult)
                ins.then_inc(xn_dve, 1)
            if exists(i, 4):
                k.wait_alone(dve, stats_done, A.index + 1)
                for t in range(G):
                    ins = nc.vector.bn_aggr(mv[:, A.s, t], stats[:, A.s, t])
                ins.then_inc(mv_done, 1)
            if exists(i, 1):
                k.wait_alone(dve, kept, (S.index - 1) * 3)
                k.wait_alone(dve, logit_done, S.index + 1)
                nc.vector.max(best[:, S.s], logit[:, S.s]).then_inc(best_done, 1)
            if exists(i, 4):
                dve.wait_ge(mv_done, counted(A.index + 1))
                nc.vector.tensor_scalar(nmean[:, A.s], mv[:, A.s, :, 0], -1.0, None, ALU.mult)
                nc.vector.tensor_scalar(var[:, A.s], mv[:, A.s, :, 1], 1e-5, None, ALU.add).then_inc(var_done, 1)
            if exists(i, 1):
                dve.wait_ge(best_done, counted(S.index + 1))
                nc.vector.tensor_scalar(nbest[:, S.s:S.s + 1], best[:, S.s, 0:1], -1.0, None, ALU.mult)\
                    .then_inc(nbest_done, 1)
                nc.vector.max_index(at[:, S.s], best[:, S.s], logit[:, S.s]).then_inc(at_done, 1)
            if exists(i, 0):
                dve.wait_ge(at_done, counted(O.index + 1))
                nc.vector.tensor_copy(kept_top[:, bass.ds(O.index * K0, K0)], best[:, O.s]).then_inc(kept, 1)
                nc.vector.tensor_copy(kept_at[:, bass.ds(O.index * K0, K0)], at[:, O.s]).then_inc(kept, 1)
                dve.wait_ge(esum_done, counted(O.index + 1))
                nc.vector.tensor_copy(kept_sum[:, bass.ds(O.index, 1)], esum[:, O.s:O.s + 1]).then_inc(kept, 1)

        def act_step(step, i, act):
            S, M, B = step.shift(1), step.shift(2), step.shift(3)
            if exists(i, 2):
                act.wait_ge(t_done, counted(M.index + 1))
                act.wait_ge(l_done, counted(M.index - 1))
                for half in range(2):
                    a, b = half * G // 2, (half + 1) * G // 2
                    nc.scalar.copy(ut[:, M.s, a:b], ps_t[:, M.s, a:b]).then_inc(ut_done, 1)
            if exists(i, 3):
                act.wait_ge(shift_done, counted(B.index + 1))
                act.wait_ge(t_done, counted(B.index - 1))
                for t in range(ON_DVE, G):
                    ins = nc.scalar.activation(xn[:, B.s, t], xin[:, B.place, t], ACT.Identity,
                                               bias=shift[:, B.s, t:t + 1], scale=rstd[:, B.s, t:t + 1])
                ins.then_inc(xn_act, 1)
            if exists(i, 1):
                act.wait_ge(nbest_done, counted(S.index + 1))
                act.wait_ge(kept, counted((S.index - 1) * 3))
                nc.scalar.activation(ex[:], logit[:, S.s], ACT.Exp, bias=nbest[:, S.s:S.s + 1],
                                     accum_out=esum[:, S.s:S.s + 1]).then_inc(esum_done, 1)
            if exists(i, 2):
                act.wait_ge(l_done, counted(M.index + 1))
                act.wait_ge(at_done, counted(M.index - 1))
                nc.scalar.activation(logit[:, M.s], ps_l[:, M.s], ACT.Identity, bias=gate_b[:, 0:1])\
                    .then_inc(logit_done, 1)

        def pe_step(step, i, pe):
            M, B = step.shift(2), step.shift(3)
            if exists(i, 2):
                pe.wait_ge(ut_done, counted(M.index * 2 + 2))
                pe.wait_ge(logit_done, counted(M.index - 1))
                for half in range(2):
                    ins = nc.tensor.matmul(ps_l[half * E0:(half + 1) * E0, M.s], gate_t[:],
                                           ut[:, M.s, half * G // 2:(half + 1) * G // 2], start=True, stop=True)
                ins.then_inc(l_done, 1)
            if exists(i, 3):
                pe.wait_ge(xn_dve, counted(B.index + 1))
                pe.wait_ge(xn_act, counted(B.index + 1))
                pe.wait_ge(ut_done, counted((B.index - 1) * 2))
                for t in range(G):
                    ins = nc.tensor.transpose(ps_t[:, B.s, t], xn[:, B.s, t], k.ident[:])
                ins.then_inc(t_done, 1)

        run = lambda eng, f: run_steps(eng, lambda step, i: f(step, i, eng), -5, 0, STEPS - 2 * LAP, STEPS, LAP)
        with nc.Block() as block:
            @block.sync
            def _(sp):
                k.prime(sp)
                sp.dma_start(gate_in[:], d["L0_ffn_gate_w"]).then_inc(w_in, 16)
                for half in range(2):
                    sp.dma_start(gate_b[half * E0:(half + 1) * E0], d["L0_ffn_gate_b"].rearrange("(e a) -> e a", a=1))\
                        .then_inc(w_in, 16)
                run(sp, sp_step)

            @block.gpsimd
            def _(pool):
                run(pool, pool_step)

            @block.vector
            def _(dve):
                dve.wait_ge(gate_turned, counted(1))
                nc.vector.tensor_copy(gate_t[:], ps_g[:, 0:E0]).then_inc(gate_kept, 1)
                run(dve, dve_step)

            @block.tensor
            def _(pe):
                pe.wait_ge(w_in, counted(48))
                nc.tensor.transpose(ps_g[:, 0:E0], gate_in[:], k.ident[0:E0, 0:E0]).then_inc(gate_turned, 1)
                pe.wait_ge(gate_kept, counted(1))
                run(pe, pe_step)

            @block.scalar
            def _(act):
                run(act, act_step)


def experts(k, kept_top, kept_at, kept_sum):
    nc, d = k.nc, k.d
    STEPS = TILES // 8
    CAND = STEPS * 2 * K0
    HB = H0 // P
    W = 4
    with ExitStack() as ctx:
        sb = lambda name, shape, dt=F32: k.sb(ctx, "e_" + name, shape, dt)
        offs, iota, upper, ones = sb("offs", [P, STEPS * K0]), sb("iota", [E0, CAND]), sb("upper", [E0, E0]), sb("ones", [E0, 1])
        at_all = sb("at_all", [P, STEPS * K0])
        cand, cand_at = sb("cand", [E0, STEPS, 2, K0]), sb("cand_at", [E0, STEPS, 2, K0])
        sums = sb("sums", [E0, 2, STEPS])
        top, pos, posf, ntop = sb("top", [E0, K0]), sb("pos", [E0, K0], U32), sb("posf", [E0, K0]), sb("ntop", [E0, 1])
        junk = sb("junk", [E0, CAND])
        tok, tok_u, keep_u = sb("tok", [E0, K0]), sb("tok_u", [E0, K0], U32), sb("keep_u", [E0, K0], U32)
        esc, prod, tsum, tinv = sb("esc", [E0, 2, STEPS]), sb("prod", [E0, 2, STEPS]), sb("tsum", [E0, 1]), sb("tinv", [E0, 1])
        ptop, prob = sb("ptop", [E0, K0]), sb("prob", [E0, K0])
        x, u = sb("x", [E0, K0, C]), sb("u", [E0, K0, C])
        stats, mv, var, rstd = sb("stats", [E0, K0, 6]), sb("mv", [E0, K0, 2]), sb("var", [E0, K0]), sb("rstd", [E0, K0])
        pooled, pooled_t = sb("pooled", [E0, C]), sb("pooled_t", [C, E0])
        w1, w2 = sb("w1", [P, 2, W, H0]), sb("w2", [P, 2, W, HB, C])
        b1, b1_t, b2 = sb("b1", [E0, H0]), sb("b1_t", [P, HB, E0]), sb("b2", [E0, C])
        hb, hid = sb("hb", [P, HB, E0]), sb("hid", [P, HB, E0])
        o_t, o_e = sb("o_t", [C, E0]), sb("o_e", [E0, C])
        weighted = sb("weighted", [E0, K0, C])
        spread, others = sb("spread", [E0, K0, E0]), sb("others", [E0, K0, E0])
        same, earlier = sb("same", [E0, K0, K0, E0]), sb("earlier", [E0, K0, E0])
        count, skip = sb("count", [E0, K0]), sb("skip", [E0, K0])
        xnew = sb("xnew", [E0, K0, C])
        ps_h, ps_b1, ps_o = k.ps(ctx, "e_ps_h", [P, 512]), k.ps(ctx, "e_ps_b1", [P, HB, P]), k.ps(ctx, "e_ps_o", [P, 512])
        ps_m, ps_s = k.ps(ctx, "e_ps_m", [P, 512]), k.ps(ctx, "e_ps_s", [P, K0 * E0])
        ps_u = k.ps(ctx, "e_ps_u", [P, K0, C])
        names = """consts_in offs_done cand_in top_done pos_done posf_done tok_done tok_u_done ntop_done esc_done ptop_done
            prod_done tsum_done tinv_done prob_done x_in stats_done mv_done var_done rstd_done u_done pooled_acc
            pooled_turned pooled_kept b1_turned b1_kept h_all hb_done hid_done o_all o_kept o_turned oe_done
            weighted_done spread_done others_turned others_kept same_done u_all count_all skip_done keep_done
            xnew_done written""".split()
        S = {n: k.sem("e_" + n, from_zero=n in ("x_in", "written")) for n in names}
        pair = lambda name: [k.sem(f"e_{name}{s}") for s in range(2)]
        w1_in, w2_in, h_done, o_done = map(pair, ("w1_in", "w2_in", "h_done", "o_done"))
        col = lambda v, j: v[:, j:j + 1]
        x1_rows = d["x1"]

        with nc.Block() as block:
            @block.sync
            def _(sp):
                k.prime(sp)
                sp.dma_start(offs[:], d["offs"]).then_inc(S["consts_in"], 16)
                sp.dma_start(iota[:], d["iota"]).then_inc(S["consts_in"], 16)
                sp.dma_start(upper[:], d["upper"]).then_inc(S["consts_in"], 16)
                sp.dma_start(b1[:], d["L0_ffn_weight1"][:, C]).then_inc(S["consts_in"], 16)
                sp.dma_start(b2[:], d["L0_ffn_weight2"][:, H0]).then_inc(S["consts_in"], 16)
                for half in range(2):
                    rows = slice(half * E0, (half + 1) * E0)
                    sp.dma_start(cand[:, :, half], kept_top[rows].rearrange("e (n k) -> e n k", k=K0)).then_inc(S["cand_in"], 16)
                    sp.dma_start(sums[:, half], kept_sum[rows]).then_inc(S["cand_in"], 16)
                sp.wait_ge(S["offs_done"], counted(1))
                for half in range(2):
                    rows = slice(half * E0, (half + 1) * E0)
                    sp.dma_start(cand_at[:, :, half], at_all[rows].rearrange("e (n k) -> e n k", k=K0)).then_inc(S["cand_in"], 16)
                w1_v = d["L0_ffn_weight1"].rearrange("(n w) c h -> n c w h", w=W)
                w2_v = d["L0_ffn_weight2"].rearrange("(n w) h o -> n w h o", w=W)
                with sp.Fori(0, E0 // W // 2) as r:
                    for s in range(2):
                        sp.wait_ge(h_done[s], counted(r))
                        sp.dma_start(w1[:, s], w1_v[r * 2 + s][0:C]).then_inc(w1_in[s], 16)
                with sp.Fori(0, E0 // W // 2) as r:
                    for s in range(2):
                        sp.wait_ge(o_done[s], counted(r))
                        sp.dma_start(w2[:, s], w2_v[r * 2 + s][:, 0:H0].rearrange("w (p b) o -> p w b o", b=HB))\
                            .then_inc(w2_in[s], 16)

            @block.gpsimd
            def _(pool):
                pool.wait_ge(S["tok_u_done"], counted(1))
                for j in range(K0):
                    nc.gpsimd.indirect_dma_start(
                        out=x[:, j], out_offset=None, in_=x1_rows,
                        in_offset=bass.IndirectOffsetOnAxis(ap=col(tok_u, j), axis=0)).then_inc(S["x_in"], 16)
                pool.wait_ge(S["var_done"], counted(1))
                nc.gpsimd.tensor_tensor(rstd[:], var[:], k.mhalf[0:E0, 0:K0], ALU.pow).then_inc(S["rstd_done"], 1)
                pool.wait_ge(S["x_in"], 16 * K0)
                pool.wait_ge(S["keep_done"], counted(1))
                pool.wait_ge(S["xnew_done"], counted(K0))
                for j in range(K0):
                    nc.gpsimd.indirect_dma_start(
                        out=x1_rows, out_offset=bass.IndirectOffsetOnAxis(ap=col(keep_u, j), axis=0), in_=xnew[:, j],
                        in_offset=None, bounds_check=TOK - 1, oob_is_err=False).then_inc(S["written"], 16)
                pool.wait_ge(S["written"], 16 * K0)

            @block.vector
            def _(dve):
                dve.wait_ge(S["consts_in"], counted(80))
                nc.vector.memset(ones[:], 1.0)
                nc.vector.tensor_tensor(at_all[:], kept_at[:], offs[:], ALU.add).then_inc(S["offs_done"], 1)
                dve.wait_ge(S["cand_in"], counted(16 * 6))
                flat = cand[:].rearrange("e n a k -> e (n a k)")
                nc.vector.max(top[:], flat).then_inc(S["top_done"], 1)
                dve.wait_ge(S["top_done"], counted(1))
                nc.vector.tensor_scalar(ntop[:], top[:, 0:1], -1.0, None, ALU.mult).then_inc(S["ntop_done"], 1)
                nc.vector.max_index(pos[:], top[:], flat).then_inc(S["pos_done"], 1)
                dve.wait_ge(S["pos_done"], counted(1))
                nc.vector.tensor_copy(posf[:], pos[:]).then_inc(S["posf_done"], 1)
                dve.wait_ge(S["posf_done"], counted(1))
                for j in range(K0):
                    if j:
                        dve.wait_ge(S["tok_done"], counted(j))
                    nc.vector.scalar_tensor_tensor(junk[:], iota[:], col(posf, j), cand_at[:].rearrange("e n a k -> e (n a k)"),
                                                   ALU.is_equal, ALU.mult, accum_out=col(tok, j)).then_inc(S["tok_done"], 1)
                dve.wait_ge(S["tok_done"], counted(K0))
                nc.vector.tensor_copy(tok_u[:], tok[:]).then_inc(S["tok_u_done"], 1)
                dve.wait_ge(S["esc_done"], counted(1))
                nc.vector.tensor_tensor(prod[:], esc[:], sums[:], ALU.mult).then_inc(S["prod_done"], 1)
                dve.wait_ge(S["prod_done"], counted(1))
                nc.vector.tensor_reduce(tsum[:], prod[:].rearrange("e a n -> e (a n)"), AXX, ALU.add).then_inc(S["tsum_done"], 1)
                dve.wait_ge(S["tsum_done"], counted(1))
                nc.vector.reciprocal(tinv[:], tsum[:]).then_inc(S["tinv_done"], 1)
                dve.wait_ge(S["tinv_done"], counted(1))
                dve.wait_ge(S["ptop_done"], counted(1))
                nc.vector.tensor_scalar(prob[:], ptop[:], tinv[:, 0:1], None, ALU.mult).then_inc(S["prob_done"], 1)
                dve.wait_ge(S["x_in"], 16 * K0)
                for j in range(K0):
                    ins = nc.vector.bn_stats(stats[:, j], x[:, j])
                ins.then_inc(S["stats_done"], 1)
                dve.wait_ge(S["stats_done"], counted(1))
                for j in range(K0):
                    ins = nc.vector.bn_aggr(mv[:, j], stats[:, j])
                ins.then_inc(S["mv_done"], 1)
                dve.wait_ge(S["mv_done"], counted(1))
                nc.vector.tensor_scalar(var[:], mv[:, :, 1], 1e-5, None, ALU.add).then_inc(S["var_done"], 1)
                dve.wait_ge(S["rstd_done"], counted(1))
                for j in range(K0):
                    ins = nc.vector.tensor_scalar(u[:, j], x[:, j], mv[:, j, 0:1], col(rstd, j), ALU.subtract, ALU.mult)
                ins.then_inc(S["u_done"], 1)
                dve.wait_ge(S["u_done"], counted(1))
                dve.wait_ge(S["prob_done"], counted(1))
                for j in range(K0):
                    if j == 0:
                        nc.vector.tensor_scalar(pooled[:], u[:, 0], prob[:, 0:1], None, ALU.mult).then_inc(S["pooled_acc"], 1)
                        continue
                    dve.wait_ge(S["pooled_acc"], counted(j))
                    nc.vector.scalar_tensor_tensor(pooled[:], u[:, j], col(prob, j), pooled[:], ALU.mult, ALU.add)\
                        .then_inc(S["pooled_acc"], 1)
                dve.wait_ge(S["pooled_turned"], counted(1))
                nc.vector.tensor_copy(pooled_t[:], ps_m[:, 0:E0]).then_inc(S["pooled_kept"], 1)
                dve.wait_ge(S["b1_turned"], counted(1))
                nc.vector.tensor_copy(b1_t[:], ps_b1[:, :, 0:E0]).then_inc(S["b1_kept"], 1)
                for j in range(K0):
                    ins = nc.vector.tensor_copy(spread[:, j], col(tok, j).broadcast_to([E0, E0]))
                ins.then_inc(S["spread_done"], 1)
                dve.wait_ge(S["others_turned"], counted(1))
                nc.vector.tensor_copy(others[:].rearrange("e j f -> e (j f)"), ps_s[0:E0]).then_inc(S["others_kept"], 1)
                dve.wait_ge(S["others_kept"], counted(1))
                for j in range(K0):
                    ins = nc.vector.tensor_scalar(same[:, j], others[:], col(tok, j), None, ALU.is_equal)
                ins.then_inc(S["same_done"], 1)
                dve.wait_ge(S["same_done"], counted(1))
                for j in range(K0):
                    ins = nc.vector.tensor_tensor(earlier[:, j], same[:, j, j], upper[:], ALU.mult)
                ins.then_inc(S["same_done"], 1)
                dve.wait_ge(S["h_all"], counted(1))
                dve.wait_ge(S["b1_kept"], counted(1))
                nc.vector.tensor_tensor(hb[:], ps_h[:, 0:HB * E0].rearrange("p (b e) -> p b e", b=HB), b1_t[:], ALU.add)\
                    .then_inc(S["hb_done"], 1)
                dve.wait_ge(S["o_all"], counted(1))
                nc.vector.tensor_copy(o_t[:], ps_o[:, 0:E0]).then_inc(S["o_kept"], 1)
                dve.wait_ge(S["o_turned"], counted(1))
                nc.vector.tensor_tensor(o_e[:], ps_m[0:E0, C:2 * C], b2[:], ALU.add).then_inc(S["oe_done"], 1)
                dve.wait_ge(S["oe_done"], counted(1))
                for j in range(K0):
                    ins = nc.vector.tensor_scalar(weighted[:, j], o_e[:], col(prob, j), None, ALU.mult)
                ins.then_inc(S["weighted_done"], 1)
                dve.wait_ge(S["u_all"], counted(K0))
                for j in range(K0):
                    nc.vector.tensor_tensor(xnew[:, j], ps_u[0:E0, j], x[:, j], ALU.add).then_inc(S["xnew_done"], 1)
                dve.wait_ge(S["count_all"], counted(1))
                nc.vector.tensor_scalar(skip[:], ps_m[0:E0, 2 * C:2 * C + K0], 0.5, float(2 * TOK), ALU.is_gt, ALU.mult)\
                    .then_inc(S["skip_done"], 1)
                dve.wait_ge(S["skip_done"], counted(1))
                nc.vector.tensor_tensor(keep_u[:], skip[:], tok[:], ALU.add).then_inc(S["keep_done"], 1)

            @block.scalar
            def _(act):
                act.wait_ge(S["ntop_done"], counted(1))
                nc.scalar.activation(esc[:], cand[:, :, :, 0].rearrange("e n a -> e a n"), ACT.Exp, bias=ntop[:, 0:1]).then_inc(S["esc_done"], 1)
                nc.scalar.activation(ptop[:], top[:], ACT.Exp, bias=ntop[:, 0:1]).then_inc(S["ptop_done"], 1)
                act.wait_ge(S["hb_done"], counted(1))
                nc.scalar.activation(hid[:], hb[:], ACT.Gelu).then_inc(S["hid_done"], 1)

            @block.tensor
            def _(pe):
                pe.wait_ge(S["consts_in"], counted(80))
                for b in range(HB):
                    ins = nc.tensor.transpose(ps_b1[:, b, 0:E0], b1[:].rearrange("e (p b) -> e b p", b=HB)[:, b],
                                              k.ident[0:E0, 0:E0])
                ins.then_inc(S["b1_turned"], 1)
                pe.wait_ge(S["pooled_acc"], counted(K0))
                nc.tensor.transpose(ps_m[:, 0:E0], pooled[:], k.ident[0:E0, 0:E0]).then_inc(S["pooled_turned"], 1)
                pe.wait_ge(S["spread_done"], counted(1))
                for j in range(K0):
                    ins = nc.tensor.transpose(ps_s[0:E0, j * E0:(j + 1) * E0], spread[:, j], k.ident[0:E0, 0:E0])
                ins.then_inc(S["others_turned"], 1)
                pe.wait_ge(S["pooled_kept"], counted(1))
                with pe.Fori(0, E0 // W // 2) as r:
                    for s in range(2):
                        pe.wait_ge(w1_in[s], counted(r * 16 + 16))
                        for w in range(W):
                            e = r * (2 * W) + (s * W + w)
                            for b in range(HB):
                                ins = nc.tensor.matmul(ps_h[:, bass.ds(e + b * E0, 1)],
                                                       w1[:, s, w].rearrange("c (p b) -> c b p", b=HB)[:, b],
                                                       pooled_t[:, bass.ds(e, 1)], start=True, stop=True)
                        ins.then_inc(h_done[s], 1)
                nc.tensor.drain().then_inc(S["h_all"], 1)
                pe.wait_ge(S["hid_done"], counted(1))
                with pe.Fori(0, E0 // W // 2) as r:
                    for s in range(2):
                        pe.wait_ge(w2_in[s], counted(r * 16 + 16))
                        for w in range(W):
                            e = r * (2 * W) + (s * W + w)
                            for b in range(HB):
                                ins = nc.tensor.matmul(ps_o[:, bass.ds(e, 1)], w2[:, s, w, b], hid[:, b, bass.ds(e, 1)],
                                                       start=b == 0, stop=b == HB - 1)
                        ins.then_inc(o_done[s], 1)
                nc.tensor.drain().then_inc(S["o_all"], 1)
                pe.wait_ge(S["o_kept"], counted(1))
                nc.tensor.transpose(ps_m[0:E0, C:2 * C], o_t[:], k.ident[:]).then_inc(S["o_turned"], 1)
                pe.wait_ge(S["weighted_done"], counted(1))
                pe.wait_ge(S["same_done"], counted(2))
                for j in range(K0):
                    for f in range(K0):
                        ins = nc.tensor.matmul(ps_u[0:E0, j], same[:, f, j], weighted[:, f], start=f == 0, stop=f == K0 - 1)
                    ins.then_inc(S["u_all"], 1)
                pe.wait_ge(S["oe_done"], counted(1))
                for j in range(K0):
                    for f in range(j + 1):
                        ins = nc.tensor.matmul(ps_m[0:E0, 2 * C + j:2 * C + j + 1], same[:, f, j] if f < j else earlier[:, j],
                                               ones[:], start=f == 0, stop=f == j)
                ins.then_inc(S["count_all"], 1)


def transform(k, along_rows, mean_t, rstd_t, shift_t, modes):
    nc, d = k.nc, k.d
    G, LINES = 8, 4
    U = 4
    LAP = 2 * U
    STEPS = N // LINES
    ON_DVE = 3 if along_rows else 5
    tag = "r_" if along_rows else "c_"
    with ExitStack() as ctx:
        sb = lambda name, shape, dt=F32: k.sb(ctx, tag + name, shape, dt)
        xin, xn = sb("xin", [P, 4, G, C]), sb("xn", [P, 2, G, C])
        stats, mv = sb("stats", [P, 2, G, 6]), sb("mv", [P, 2, G, 2])
        var, rstd, nmean, shift = (sb(n, [P, 2, G]) for n in ("var", "rstd", "nmean", "shift"))
        basis = sb("basis", [P, 2, M2])
        by_mode = sb("by_mode", [P, LINES, C])
        ps_m = k.ps(ctx, tag + "ps_m", [P, 2, LINES, C])
        ps_t = k.ps(ctx, tag + "ps_t", [C, LINES, P])
        basis_in, m_kept, m_turned, modes_kept = (k.sem(tag + n) for n in ("basis_in", "m_kept", "m_turned", "modes_kept"))
        x_in = [k.sem(f"{tag}x_in{s}") for s in range(4)]
        stats_done, mv_done, var_done, rstd_done, shift_done, kept, xn_dve, xn_act, m_done = (k.sem(tag + n) for n in (
            "stats_done", "mv_done", "var_done", "rstd_done", "shift_done", "kept", "xn_dve", "xn_act", "m_done"))
        if along_rows:
            x_v = d["x1"].rearrange("(n t p) c -> n p t c", t=G, p=P)
        else:
            x_v = d["x1"].rearrange("(b p n w) c -> n p b (w c)", b=2, p=P, w=LINES)

        def exists(i, by):
            return i is None or 0 <= i + by < STEPS

        def bank_before(step, i, by):
            last = step.shift(2 - by)
            if last.place % U == U - 1 and exists(i, 2 - by):
                return last.place // U, last.lap * 2 + last.place // U
            return None, None

        def slot(turn):
            return turn.place % 4

        def sp_step(step, i, sp):
            if exists(i, 5):
                L = step.shift(5)
                k.wait_alone(sp, xn_dve, L.index - 3)
                k.wait_alone(sp, xn_act, L.index - 3)
                dst = xin[:, slot(L)] if along_rows else xin[:, slot(L)].rearrange("p (b w) c -> p b (w c)", b=2)
                sp.dma_start(dst, x_v[L.index]).then_inc(x_in[slot(L)], 16)

        def pool_step(step, i, pool):
            if exists(i, 4):
                A = step.shift(4)
                pool.wait_ge(xn_act, counted(A.index - 1))
                pool.wait_ge(var_done, counted(A.index + 1))
                nc.gpsimd.tensor_tensor(rstd[:, A.s], var[:, A.s], k.mhalf[:, 0:G], ALU.pow).then_inc(rstd_done, 1)
                pool.wait_ge(rstd_done, counted(A.index + 1))
                nc.gpsimd.tensor_tensor(shift[:, A.s], nmean[:, A.s], rstd[:, A.s], ALU.mult).then_inc(shift_done, 1)

        def statistics_of(B, t):
            if along_rows:
                return mv[:, B.s, t, 0:1], rstd[:, B.s, t:t + 1], shift[:, B.s, t:t + 1]
            line = bass.ds(B.index * LINES + t % LINES, 1)
            return tuple(what[:, t // LINES, line] for what in (mean_t, rstd_t, shift_t))

        def dve_step(step, i, dve):
            B, A = step.shift(3), step.shift(4)
            if exists(i, 4):
                dve.wait_ge(x_in[slot(A)], counted((A.lap * 2 + A.place // 4) * 16 + 16))
                if along_rows:
                    for t in range(G):
                        ins = nc.vector.bn_stats(stats[:, A.s, t], xin[:, slot(A), t])
                    ins.then_inc(stats_done, 1)
            if exists(i, 3):
                if along_rows:
                    dve.wait_ge(rstd_done, counted(B.index + 1))
                dve.wait_ge(m_done, counted(B.index - 1))
                for t in range(ON_DVE):
                    mean, scale, _ = statistics_of(B, t)
                    ins = nc.vector.tensor_scalar(xn[:, B.s, t], xin[:, slot(B), t], mean, scale, ALU.subtract, ALU.mult)
                ins.then_inc(xn_dve, 1)
                if along_rows:
                    nc.vector.tensor_copy(k.rstd[:, bass.ds(B.index * G, G)], rstd[:, B.s]).then_inc(kept, 1)
            if exists(i, 4) and along_rows:
                k.wait_alone(dve, stats_done, A.index + 1)
                for t in range(G):
                    ins = nc.vector.bn_aggr(mv[:, A.s, t], stats[:, A.s, t])
                ins.then_inc(mv_done, 1)
                dve.wait_ge(mv_done, counted(A.index + 1))
                nc.vector.tensor_scalar(nmean[:, A.s], mv[:, A.s, :, 0], -1.0, None, ALU.mult)
                nc.vector.tensor_scalar(var[:, A.s], mv[:, A.s, :, 1], 1e-6, None, ALU.add).then_inc(var_done, 1)
                nc.vector.tensor_copy(k.mean[:, bass.ds(A.index * G, G)], mv[:, A.s, :, 0])

        def act_step(step, i, act):
            if exists(i, 3):
                B = step.shift(3)
                if along_rows:
                    act.wait_ge(shift_done, counted(B.index + 1))
                else:
                    act.wait_ge(x_in[slot(B)], counted((B.lap * 2 + B.place // 4) * 16 + 16))
                act.wait_ge(m_done, counted(B.index - 1))
                for t in range(ON_DVE, G):
                    _, scale, bias = statistics_of(B, t)
                    ins = nc.scalar.activation(xn[:, B.s, t], xin[:, slot(B), t], ACT.Identity, bias=bias, scale=scale)
                ins.then_inc(xn_act, 1)
            bank, n = bank_before(step, i, 1)
            if bank is not None:
                act.wait_ge(m_done, counted((n + 1) * U))
                act.wait_ge(m_turned, counted(n))
                nc.scalar.copy(by_mode[:], ps_m[:, bank]).then_inc(m_kept, 1)
            bank, n = bank_before(step, i, 2)
            if bank is not None:
                k.wait_alone(act, m_turned, n + 1)
                nc.scalar.copy(modes[:, bass.ds(n * (U * LINES), U * LINES)].rearrange("c (g w) m -> c w g m", w=LINES),
                               ps_t[:].rearrange("c w (g m) -> c w g m", m=M2)).then_inc(modes_kept, 1)

        def pe_step(step, i, pe):
            if exists(i, 2):
                M = step.shift(2)
                g, bank, n = M.place % U, M.place // U, M.lap * 2 + M.place // U
                pe.wait_ge(xn_dve, counted(M.index + 1))
                pe.wait_ge(xn_act, counted(M.index + 1))
                if g == 0:
                    pe.wait_ge(m_kept, counted(n - 1))
                order = "p (w b) c -> p b w c" if along_rows else "p (b w) c -> p b w c"
                for b in range(2):
                    ins = nc.tensor.matmul(ps_m[g * M2:(g + 1) * M2, bank], basis[:, b],
                                           xn[:, M.s].rearrange(order, b=2)[:, b], start=b == 0, stop=b == 1)
                ins.then_inc(m_done, 1)
            bank, n = bank_before(step, i, 1)
            if bank is not None:
                pe.wait_ge(m_kept, counted(n + 1))
                pe.wait_ge(modes_kept, counted(n))
                for w in range(LINES):
                    ins = nc.tensor.transpose(ps_t[:, w], by_mode[:, w], k.ident[:])
                ins.then_inc(m_turned, 1)

        run = lambda eng, f: run_steps(eng, lambda step, i: f(step, i, eng), -5, 0, STEPS - LAP, STEPS, LAP)
        with nc.Block() as block:
            @block.sync
            def _(sp):
                k.prime(sp)
                sp.dma_start(basis[:], d["forward"].rearrange("(b p) m -> p b m", p=P)).then_inc(basis_in, 16)
                run(sp, sp_step)

            @block.gpsimd
            def _(pool):
                if along_rows:
                    run(pool, pool_step)

            @block.vector
            def _(dve):
                run(dve, dve_step)

            @block.scalar
            def _(act):
                run(act, act_step)

            @block.tensor
            def _(pe):
                pe.wait_ge(basis_in, counted(16))
                run(pe, pe_step)


def turn_statistics(k, mean_t, rstd_t, shift_t):
    nc = k.nc
    with ExitStack() as ctx:
        ps = k.ps(ctx, "u_ps", [P, 2, 2, N])
        turned, kept, shifted = k.sem("u_turned"), k.sem("u_kept"), k.sem("u_shifted")
        with nc.Block() as block:
            @block.tensor
            def _(pe):
                k.prime(pe)
                for i, what in enumerate((k.mean, k.rstd)):
                    for xb in range(2):
                        for yb in range(2):
                            ins = nc.tensor.transpose(
                                ps[:, i, xb, yb * P:(yb + 1) * P],
                                what[:].rearrange("p (x b) -> p b x", b=2)[:, yb, xb * P:(xb + 1) * P], k.ident[:])
                    ins.then_inc(turned, 1)

            @block.vector
            def _(dve):
                for i, to in enumerate((mean_t, rstd_t)):
                    dve.wait_ge(turned, counted(i + 1))
                    nc.vector.tensor_copy(to[:], ps[:, i]).then_inc(kept, 1)
                dve.wait_ge(kept, counted(2))
                nc.vector.scalar_tensor_tensor(shift_t[:], mean_t[:], -1.0, rstd_t[:], ALU.mult, ALU.mult)\
                    .then_inc(shifted, 1)


def mix_modes(k, modes, weight, mixed):
    nc, d = k.nc, k.d
    tag = "m" + weight[-1] + "_"
    with ExitStack() as ctx:
        w = k.sb(ctx, tag + "w", [C, C, NM, 2])
        ww = k.sb(ctx, tag + "ww", [C, NM, 3, C])
        z = k.sb(ctx, tag + "z", [P, 2, 2, NM, C])
        ps = k.ps(ctx, tag + "ps", [P, 4, 512])
        w_in, ww_done, mixed_done, kept_a, kept_v, written = (
            k.sem(tag + n) for n in ("w_in", "ww_done", "mixed", "kept_a", "kept_v", "written"))
        with nc.Block() as block:
            @block.sync
            def _(sp):
                k.prime(sp)
                sp.dma_start(w[:], d[weight]).then_inc(w_in, 16)
                for lb in range(2):
                    sp.wait_ge(kept_a, counted((lb + 1) * NM // 2))
                    sp.wait_ge(kept_v, counted((lb + 1) * NM // 2))
                    for part in range(2):
                        sp.dma_start(mixed[part, :, lb * P:(lb + 1) * P].rearrange("m l o -> l m o"), z[:, lb, part])\
                            .then_inc(written, 16)
                sp.wait_ge(written, counted(16 * 4))

            @block.vector
            def _(dve):
                dve.wait_ge(w_in, counted(16))
                for m in range(NM):
                    nc.vector.tensor_scalar(ww[:, m, 0], w[:, :, m, 1], -1.0, None, ALU.mult)
                    nc.vector.tensor_copy(ww[:, m, 1:3], w[:, :, m].rearrange("i o a -> i a o")).then_inc(ww_done, 1)
                for n in range(0, 2 * NM, 2):
                    lb, m = n // NM, n % NM
                    dve.wait_ge(mixed_done, counted(n + 1))
                    nc.vector.tensor_copy(z[:, lb, :, m], ps[:, n % 4, 0:2 * C].rearrange("p (a o) -> p a o", a=2))\
                        .then_inc(kept_v, 1)

            @block.scalar
            def _(act):
                for n in range(1, 2 * NM, 2):
                    lb, m = n // NM, n % NM
                    act.wait_ge(mixed_done, counted(n + 1))
                    nc.scalar.copy(z[:, lb, :, m], ps[:, n % 4, 0:2 * C].rearrange("p (a o) -> p a o", a=2))\
                        .then_inc(kept_a, 1)

            @block.tensor
            def _(pe):
                for n in range(2 * NM):
                    lb, m = n // NM, n % NM
                    pe.wait_ge(ww_done, counted(m + 1))
                    if n >= 4:
                        pe.wait_ge(kept_a if n % 2 else kept_v, counted(n // 2 - 1))
                    lines = slice(lb * P, (lb + 1) * P)
                    nc.tensor.matmul(ps[:, n % 4, 0:2 * C], modes[:, lines, m], ww[:, m, 1:3], start=True, stop=False)
                    nc.tensor.matmul(ps[:, n % 4, 0:2 * C], modes[:, lines, NM + m], ww[:, m, 0:2], start=False, stop=True)\
                        .then_inc(mixed_done, 1)


def spectra(k):
    nc, d = k.nc, k.d
    with ExitStack() as ctx:
        modes = k.sb(ctx, "f_modes", [C, N, M2])
        mean_t, rstd_t, shift_t = (k.sb(ctx, "f_" + n, [P, 2, N]) for n in ("mean_t", "rstd_t", "shift_t"))
        transform(k, True, mean_t, rstd_t, shift_t, modes)
        k.end_phase()
        turn_statistics(k, mean_t, rstd_t, shift_t)
        k.end_phase()
        mix_modes(k, modes, "L1_conv_w1", d["z1"])
        k.end_phase()
        transform(k, False, mean_t, rstd_t, shift_t, modes)
        k.end_phase()
        mix_modes(k, modes, "L1_conv_w2", d["z2"])
        k.end_phase()


def layer1(k):
    nc, d = k.nc, k.d
    BX, BY, T = 16, 32, 4
    U = N // BY
    LAPS = N // BX
    BLOCKS = U * LAPS
    HB = H1 // P
    Q4 = T * P
    EH = E1 // 2
    ADDS = 1 + T * EH
    LOADS = 22
    with ExitStack() as ctx:
        sb = lambda name, shape, dt=F32: k.sb(ctx, "l_" + name, shape, dt)
        z1_next, z1 = sb("z1_next", [P, BX // 4, C]), sb("z1", [P, BX // 4, C])
        z2 = sb("z2", [P, N // 4, C])
        basis, basis_x = sb("basis", [P, 4, N]), sb("basis_x", [P, 4, BX])
        w0, b0, w1, b1 = sb("w0", [C, HB, P]), sb("b0", [P, HB]), sb("w1", [P, HB, C]), sb("b1", [P, C])
        ln_g, ln_b = sb("ln_g", [P, C]), sb("ln_b", [P, C])
        router, router_b = sb("router", [C, 32]), sb("router_b", [P, 1])
        we, eb = sb("we", [C, E1, C]), sb("eb", [P, T, C])
        iota = sb("iota", [P, T, E1])
        ht, hid = sb("ht", [C, 2, Q4]), sb("hid", [P, 2, HB, Q4])
        x2, xb, h2, x3, acc, out = (sb(n, [P, 2, T, C]) for n in ("x2", "xb", "h2", "x3", "acc", "out"))
        u, ut = sb("u", [P, T, C]), sb("ut", [C, 4, Q4])
        stats, mv, var, rstd = sb("stats", [P, T, 6]), sb("mv", [P, 2, T, 2]), sb("var", [P, 2, T]), sb("rstd", [P, 2, T])
        stats3, mv3, var3, rstd3 = sb("stats3", [P, T, 6]), sb("mv3", [P, 2, T, 2]), sb("var3", [P, 2, T]), sb("rstd3", [P, 2, T])
        logit_t, logit = sb("logit_t", [P, P]), sb("logit", [P, T, E1])
        top, at, atf = sb("top", [P, T, 8]), sb("at", [P, T, 8], U32), sb("atf", [P, T, 2])
        diff, ratio, den = sb("diff", [P, T]), sb("ratio", [P, T]), sb("den", [P, T])
        share = sb("share", [P, 2, T])
        pick, picked = sb("pick", [P, 2, T, E1]), sb("picked", [P, 2, T, E1])
        weight, weight_t = sb("weight", [P, 2, T, 32]), sb("weight_t", [P, P])
        scaled4, pairs = sb("scaled4", [P, 2, T, EH, C]), sb("pairs", [P, T, 2, C])
        quads = sb("quads", [P, T, C])
        ps_h, ps_f, ps_g = k.ps(ctx, "l_ps_h", [C, Q4]), k.ps(ctx, "l_ps_f", [P, 2, Q4]), k.ps(ctx, "l_ps_g", [P, T, C])
        ps_t, ps_e, ps_x = k.ps(ctx, "l_ps_t", [P, 512]), k.ps(ctx, "l_ps_e", [P, 2, 512]), k.ps(ctx, "l_ps_x", [P, T, C])

        sems = lambda *names: [k.sem("l_" + n) for n in names]
        w_in, zeroed, z1_in = sems("w_in", "zeroed", "z1_in")
        x_in, stored = sems("x_in0", "x_in1"), sems("stored0", "stored1")
        i_done, f_done, g_done, t_done, rl_done, rt_done, e_done, wt_done, x_done = sems(
            "i_done", "f_done", "g_done", "t_done", "rl_done", "rt_done", "e_done", "wt_done", "x_done")
        ht_done, relu_done, ut_done, rl_kept, ratio_done, wt_kept, scaled4_done = sems(
            "ht_done", "relu_done", "ut_done", "rl_kept", "ratio_done", "wt_kept", "scaled4_done")
        h2_done, stats_done, mv_done, var_done, scaled, x3_done = sems(
            "h2_done", "stats_done", "mv_done", "var_done", "scaled", "x3_done")
        stats3_done, mv3_done, var3_done, u_done, rt_kept, top_done, at_done, atf_done, diff_done = sems(
            "stats3_done", "mv3_done", "var3_done", "u_done", "rt_kept", "top_done", "at_done", "atf_done", "diff_done")
        share_done, pick_done, w_done, acc_done = sems("share_done", "pick_done", "w_done", "acc_done")
        z1_done, rstd_done, rstd3_done, xb_done, pairs_done, quads_done, out_done = sems(
            "z1_done", "rstd_done", "rstd3_done", "xb_done", "pairs_done", "quads_done", "out_done")

        grid = "(X t a Y y) c -> X Y a y t c"
        x2_v = d["x1"].rearrange(grid, X=LAPS, t=T, a=4, Y=U, y=BY)
        out_v = d["out"].rearrange("o x y c -> (o x y) c").rearrange(grid, X=LAPS, t=T, a=4, Y=U, y=BY)
        z1_v = d["z1"].rearrange("r m (X q a) o -> X a (r m) q o", X=LAPS, a=4)
        z2_v = d["z2"].rearrange("r m (q a) o -> a (r m) q o", a=4)

        def exists(i, by):
            return i is None or 0 <= i + by < BLOCKS

        def quarter(a):
            return slice(a * 32, (a + 1) * 32)

        def load_z1(sp, lap):
            for a in range(4):
                sp.dma_start(z1_next[quarter(a)], z1_v[lap, a]).then_inc(z1_in, 16)

        def sp_step(step, i, sp):
            O, F, G = step, step.shift(4), step.shift(5)
            if G.place == 6 and exists(i, 5 + U):
                k.wait_alone(sp, z1_done, G.lap * 2 + 2)
                load_z1(sp, G.lap + 1)
            if exists(i, 4):
                k.wait_alone(sp, xb_done, F.index - 1)
                for a in range(4):
                    sp.dma_start(x2[quarter(a), F.s], x2_v[F.lap, F.place, a]).then_inc(x_in[F.s], 16)
            if exists(i, 0):
                k.wait_alone(sp, out_done, O.index + 1)
                for a in range(4):
                    sp.dma_start(out_v[O.lap, O.place, a], out[quarter(a), O.s]).then_inc(stored[O.s], 16)

        def pool_step(step, i, pool):
            O, R, F, G = step, step.shift(3), step.shift(4), step.shift(5)
            if exists(i, 5) and G.place == 0:
                k.wait_alone(pool, z1_in, G.lap * 64 + 64)
                k.wait_alone(pool, i_done, G.index)
                nc.gpsimd.tensor_copy(z1[:], z1_next[:]).then_inc(z1_done, 1)
                nc.gpsimd.tensor_copy(basis_x[:], basis[:, :, bass.ds(G.lap * BX, BX)]).then_inc(z1_done, 1)
            if exists(i, 3):
                pool.wait_ge(var_done, counted(R.index + 1))
                nc.gpsimd.tensor_tensor(rstd[:, R.s], var[:, R.s], k.mhalf[:, 0:T], ALU.pow).then_inc(rstd_done, 1)
            if exists(i, 0):
                pool.wait_ge(scaled4_done, counted((O.index + 1) * T * EH))
                nc.gpsimd.tensor_tensor(pairs[:], scaled4[:, O.s, :, 0:2], scaled4[:, O.s, :, 2:4], ALU.add)\
                    .then_inc(pairs_done, 1)
                pool.wait_ge(pairs_done, counted(O.index + 1))
                nc.gpsimd.tensor_tensor(quads[:], pairs[:, :, 0], pairs[:, :, 1], ALU.add).then_inc(quads_done, 1)
            if exists(i, 3):
                pool.wait_ge(var3_done, counted(R.index + 1))
                nc.gpsimd.tensor_tensor(rstd3[:, R.s], var3[:, R.s], k.mhalf[:, 0:T], ALU.pow).then_inc(rstd3_done, 1)
            if exists(i, 0):
                pool.wait_ge(quads_done, counted(O.index + 1))
                pool.wait_ge(acc_done, counted((O.index + 1) * ADDS))
                pool.wait_ge(stored[O.s], counted(O.before * 64))
                nc.gpsimd.tensor_tensor(out[:, O.s], quads[:], acc[:, O.s], ALU.add).then_inc(out_done, 1)
            if exists(i, 4):
                pool.wait_ge(x_in[F.s], counted(F.before * 64 + 64))
                pool.wait_ge(x3_done, counted((F.index - 1) * T))
                nc.gpsimd.tensor_tensor(xb[:, F.s], x2[:, F.s], ln_b[:].unsqueeze(1).broadcast_to([P, T, C]), ALU.add)\
                    .then_inc(xb_done, 1)

        def dve_step(step, i, dve):
            E, Q, R = step.shift(1), step.shift(2), step.shift(3)

            def add_experts(t):
                if not exists(i, 1):
                    return
                dve.wait_ge(e_done, counted(E.index * (2 * T) + 2 * t + 1))
                for e in range(EH):
                    dve.wait_ge(acc_done, counted(E.index * ADDS + (t * EH + e if e else 0) + 1))
                    nc.vector.scalar_tensor_tensor(
                        acc[:, E.s, t], ps_e[:, 0, e * C:(e + 1) * C], weight[:, E.s, t, e:e + 1],
                        acc[:, E.s, t], ALU.mult, ALU.add).then_inc(acc_done, 1)

            if exists(i, 3):
                dve.wait_ge(g_done, counted(R.index + 1))
                nc.vector.tensor_tensor(h2[:, R.s], ps_g[:], b1[:].unsqueeze(1).broadcast_to([P, T, C]), ALU.add)\
                    .then_inc(h2_done, 1)
                k.wait_alone(dve, h2_done, R.index + 1)
                for t in range(T):
                    ins = nc.vector.bn_stats(stats[:, t], h2[:, R.s, t])
                ins.then_inc(stats_done, 1)
                k.wait_alone(dve, stats_done, R.index + 1)
                for t in range(T):
                    ins = nc.vector.bn_aggr(mv[:, R.s, t], stats[:, t])
                ins.then_inc(mv_done, 1)
                dve.wait_ge(mv_done, counted(R.index + 1))
                nc.vector.tensor_scalar(var[:, R.s], mv[:, R.s, :, 1], 1e-5, None, ALU.add).then_inc(var_done, 1)
                for t in range(T):
                    ins = nc.vector.scalar_tensor_tensor(h2[:, R.s, t], h2[:, R.s, t], mv[:, R.s, t, 0:1], ln_g[:],
                                                         ALU.subtract, ALU.mult)
                ins.then_inc(scaled, 1)
            if exists(i, 1):
                dve.wait_ge(x_done, counted(E.index + 1))
                dve.wait_ge(out_done, counted(E.index - 1))
                nc.vector.tensor_tensor(acc[:, E.s], ps_x[:], x3[:, E.s], ALU.add).then_inc(acc_done, 1)
            if exists(i, 2):
                dve.wait_ge(rt_done, counted(Q.index + 1))
                nc.vector.tensor_copy(logit[:], ps_t[:, P:2 * P].rearrange("p (t e) -> p t e", t=T)[:, :, 0:E1])\
                    .then_inc(rt_kept, 1)
            add_experts(0)
            if exists(i, 2):
                k.wait_alone(dve, rt_kept, Q.index + 1)
                for t in range(T):
                    ins = nc.vector.max(top[:, t], logit[:, t])
                ins.then_inc(top_done, 1)
            if exists(i, 3):
                dve.wait_ge(scaled, counted(R.index + 1))
                dve.wait_ge(rstd_done, counted(R.index + 1))
                dve.wait_ge(xb_done, counted(R.index + 1))
                for t in range(T):
                    nc.vector.scalar_tensor_tensor(x3[:, R.s, t], h2[:, R.s, t], rstd[:, R.s, t:t + 1], xb[:, R.s, t],
                                                   ALU.mult, ALU.add).then_inc(x3_done, 1)
            if exists(i, 2):
                dve.wait_ge(top_done, counted(Q.index + 1))
                nc.vector.tensor_tensor(diff[:], top[:, :, 1], top[:, :, 0], ALU.subtract).then_inc(diff_done, 1)
                for t in range(T):
                    ins = nc.vector.max_index(at[:, t], top[:, t], logit[:, t])
                ins.then_inc(at_done, 1)
            add_experts(1)
            if exists(i, 3):
                k.wait_alone(dve, x3_done, R.index * T + T)
                for t in range(T):
                    ins = nc.vector.bn_stats(stats3[:, t], x3[:, R.s, t])
                ins.then_inc(stats3_done, 1)
            if exists(i, 2):
                dve.wait_ge(ratio_done, counted(Q.index + 1))
                nc.vector.tensor_scalar(den[:], ratio[:], 1.0, None, ALU.add).then_inc(share_done, 1)
                dve.wait_ge(at_done, counted(Q.index + 1))
                nc.vector.tensor_copy(atf[:], at[:, :, 0:2]).then_inc(atf_done, 1)
            if exists(i, 3):
                k.wait_alone(dve, stats3_done, R.index + 1)
                for t in range(T):
                    ins = nc.vector.bn_aggr(mv3[:, R.s, t], stats3[:, t])
                ins.then_inc(mv3_done, 1)
            if exists(i, 2):
                dve.wait_ge(share_done, counted(Q.index * 3 + 1))
                nc.vector.reciprocal(share[:, 0], den[:]).then_inc(share_done, 1)
            add_experts(2)
            if exists(i, 3):
                dve.wait_ge(mv3_done, counted(R.index + 1))
                nc.vector.tensor_scalar(var3[:, R.s], mv3[:, R.s, :, 1], 1e-5, None, ALU.add).then_inc(var3_done, 1)
            if exists(i, 2):
                dve.wait_ge(share_done, counted(Q.index * 3 + 2))
                nc.vector.tensor_tensor(share[:, 1], ratio[:], share[:, 0], ALU.mult).then_inc(share_done, 1)
            if exists(i, 3):
                dve.wait_ge(rstd3_done, counted(R.index + 1))
                dve.wait_ge(t_done, counted(R.index))
                for t in range(T):
                    ins = nc.vector.tensor_scalar(u[:, t], x3[:, R.s, t], mv3[:, R.s, t, 0:1], rstd3[:, R.s, t:t + 1],
                                                  ALU.subtract, ALU.mult)
                ins.then_inc(u_done, 1)
            add_experts(3)
            if exists(i, 2):
                dve.wait_ge(atf_done, counted(Q.index + 1))
                for j in range(2):
                    ins = nc.vector.tensor_tensor(pick[:, j], iota[:], atf[:, :, j:j + 1].broadcast_to([P, T, E1]),
                                                  ALU.is_equal)
                ins.then_inc(pick_done, 1)
                dve.wait_ge(share_done, counted(Q.index * 3 + 3))
                dve.wait_ge(pick_done, counted(Q.index * 2 + 1))
                for j in range(2):
                    ins = nc.vector.tensor_tensor(picked[:, j], pick[:, j],
                                                  share[:, j].unsqueeze(2).broadcast_to([P, T, E1]), ALU.mult)
                ins.then_inc(pick_done, 1)
                dve.wait_ge(pick_done, counted(Q.index * 2 + 2))
                dve.wait_ge(wt_done, counted(Q.index - 1))
                dve.wait_ge(scaled4_done, counted((Q.index - 1) * T * EH))
                nc.vector.tensor_tensor(weight[:, Q.s, :, 0:E1], picked[:, 0], picked[:, 1], ALU.add).then_inc(w_done, 1)

        def act_step(step, i, act):
            E, Q, R, F, G = (step.shift(by) for by in (1, 2, 3, 4, 5))

            def relu(hb):
                if exists(i, 4):
                    act.wait_ge(f_done, counted(F.index * HB + hb + 1))
                    act.wait_ge(g_done, counted(F.index - 1))
                    nc.scalar.activation(hid[:, F.s, hb], ps_f[:, hb % 2], ACT.Relu, bias=b0[:, hb:hb + 1])\
                        .then_inc(relu_done, 1)

            def scale_experts(t):
                if exists(i, 1):
                    act.wait_ge(e_done, counted(E.index * (2 * T) + 2 * t + 2))
                    act.wait_ge(pairs_done, counted(E.index - 1))
                    for e in range(EH):
                        nc.scalar.activation(scaled4[:, E.s, t, e], ps_e[:, 1, e * C:(e + 1) * C], ACT.Copy,
                                             scale=weight[:, E.s, t, EH + e:EH + e + 1]).then_inc(scaled4_done, 1)

            relu(0)
            scale_experts(0)
            relu(1)
            if exists(i, 2):
                act.wait_ge(diff_done, counted(Q.index + 1))
                nc.scalar.activation(ratio[:], diff[:], ACT.Exp).then_inc(ratio_done, 1)
            if exists(i, 5):
                act.wait_ge(i_done, counted(G.index + 1))
                act.wait_ge(f_done, counted((G.index - 1) * HB))
                nc.scalar.copy(ht[:, G.s], ps_h[:]).then_inc(ht_done, 1)
            scale_experts(1)
            relu(2)
            scale_experts(2)
            relu(3)
            scale_experts(3)
            if exists(i, 3):
                act.wait_ge(t_done, counted(R.index + 1))
                nc.scalar.copy(ut[:, R.place % 4], ps_t[:]).then_inc(ut_done, 1)
            if exists(i, 3):
                act.wait_ge(rl_done, counted(R.index + 1))
                nc.scalar.activation(logit_t[:], ps_t[:, 0:P], ACT.Identity, bias=router_b[:, 0:1]).then_inc(rl_kept, 1)
            if exists(i, 2):
                act.wait_ge(wt_done, counted(Q.index + 1))
                nc.scalar.copy(weight_t[:], ps_x[:, 0]).then_inc(wt_kept, 1)

        def pe_step(step, i, pe):
            E, Q, R, F, G = (step.shift(by) for by in (1, 2, 3, 4, 5))

            def first(hb):
                if exists(i, 4):
                    if hb == 0:
                        pe.wait_ge(ht_done, counted(F.index + 1))
                    pe.wait_ge(relu_done, counted(F.index * HB + hb - 1))
                    nc.tensor.matmul(ps_f[:, hb % 2], w0[:, hb], ht[:, F.s], start=True, stop=True).then_inc(f_done, 1)

            def second(tiles):
                if exists(i, 4):
                    if tiles[0] == 0:
                        pe.wait_ge(relu_done, counted(F.index * HB + HB))
                        pe.wait_ge(h2_done, counted(F.index))
                    for t in tiles:
                        for hb in range(HB):
                            ins = nc.tensor.matmul(ps_g[:, t], hid[:, F.s, hb, t * P:(t + 1) * P], w1[:, hb],
                                                   start=hb == 0, stop=hb == HB - 1)
                    if tiles[-1] == T - 1:
                        ins.then_inc(g_done, 1)

            def experts_of(t):
                if exists(i, 1):
                    tokens = ut[:, E.place % 4, t * P:(t + 1) * P]
                    if t:
                        pe.wait_ge(acc_done, counted(E.index * ADDS + 1 + t * EH))
                    else:
                        pe.wait_ge(acc_done, counted(E.index * ADDS))
                    nc.tensor.matmul(ps_e[:, 0], tokens, we[:, 0:EH], start=True, stop=True).then_inc(e_done, 1)
                    pe.wait_ge(scaled4_done, counted(E.index * (T * EH) + t * EH))
                    nc.tensor.matmul(ps_e[:, 1], tokens, we[:, EH:E1], start=True, stop=True).then_inc(e_done, 1)

            experts_of(0)
            first(0)
            if exists(i, 2):
                pe.wait_ge(rl_kept, counted(Q.index + 1))
                nc.tensor.transpose(ps_t[:, P:2 * P], logit_t[:], k.ident[:]).then_inc(rt_done, 1)
            if exists(i, 1):
                pe.wait_ge(wt_kept, counted(E.index + 1))
                for t in range(T):
                    ins = nc.tensor.matmul(ps_x[:, t], weight_t[:], eb[:, t], start=True, stop=True)
                ins.then_inc(x_done, 1)
            first(1)
            if exists(i, 5):
                if G.place == 0:
                    pe.wait_ge(z1_done, counted(G.lap * 2 + 2))
                pe.wait_ge(ht_done, counted(G.index))
                for q in range(BX // 4):
                    nc.tensor.matmul(ps_h[:, q * 4 * BY:(q + 1) * 4 * BY], z1[:, q],
                                     basis[:, :, G.place * BY:(G.place + 1) * BY], start=q == 0, stop=False,
                                     skip_group_check=True)
                by_column = ps_h[:].rearrange("c (x q a) -> c q a x", x=BX, a=4)
                for q in range(BY // 4):
                    ins = nc.tensor.matmul(by_column[:, q], z2[:, G.place * (BY // 4) + q], basis_x[:], start=False,
                                           stop=q == BY // 4 - 1, skip_group_check=True)
                ins.then_inc(i_done, 1)
            experts_of(1)
            first(2)
            experts_of(2)
            first(3)
            experts_of(3)
            second((0, 1))
            if exists(i, 3):
                pe.wait_ge(u_done, counted(R.index + 1))
                pe.wait_ge(rt_kept, counted(R.index))
                for t in range(T):
                    ins = nc.tensor.transpose(ps_t[:, t * P:(t + 1) * P], u[:, t], k.ident[:])
                ins.then_inc(t_done, 1)
            second((2, 3))
            if exists(i, 3):
                pe.wait_ge(ut_done, counted(R.index + 1))
                for t in range(T):
                    ins = nc.tensor.matmul(ps_t[quarter(t), 0:P], router[:], ut[:, R.place % 4, t * P:(t + 1) * P],
                                           start=True, stop=True)
                ins.then_inc(rl_done, 1)
            if exists(i, 2):
                pe.wait_ge(w_done, counted(Q.index + 1))
                pe.wait_ge(acc_done, counted(E.index * ADDS + 1))
                nc.tensor.transpose(ps_x[:, 0], weight[:, Q.s].rearrange("p t e -> p (t e)"), k.ident[:])\
                    .then_inc(wt_done, 1)

        run = lambda eng, f: run_steps(eng, lambda step, i: f(step, i, eng), -5, 0, BLOCKS - U, BLOCKS, U)
        with nc.Block() as block:
            @block.sync
            def _(sp):
                k.prime(sp)
                def load(place, array):
                    loads.append(1)
                    sp.dma_start(place, array).then_inc(w_in, 16)

                loads = []
                sp.wait_ge(zeroed, counted(2))
                load(basis[:], d["inverse"].rearrange("p (a n) -> p a n", a=4))
                for a in range(4):
                    load(z2[quarter(a)], z2_v[a])
                load(w0[:].rearrange("c b h -> c (b h)"), d["L1_conv_ff_w0"])
                load(b0[:], d["L1_conv_ff_b0_t"])
                load(w1[:], d["L1_conv_ff_w1"].rearrange("(b h) o -> h b o", b=HB))
                load(b1[:], row_of(d["L1_conv_ff_b1"]))
                load(ln_g[:], row_of(d["L1_conv_ln_g"]))
                load(ln_b[:], row_of(d["L1_conv_ln_b"]))
                load(router[:, 0:E1], d["L1_ffn_router_w"])
                load(we[:], d["L1_ffn_expert_w"].rearrange("e c o -> c e o"))
                load(iota[:], d["iota8"].rearrange("p (t e) -> p t e", t=T))
                for t in range(T):
                    rows = slice(32 * t, 32 * t + E1)
                    load(router_b[rows], d["L1_ffn_router_b"].rearrange("(e a) -> e a", a=1))
                    load(eb[rows, t], d["L1_ffn_expert_b"])
                assert len(loads) == LOADS
                load_z1(sp, 0)
                run(sp, sp_step)
                for s in range(2):
                    sp.wait_ge(stored[s], counted(64 * BLOCKS // 2))

            @block.gpsimd
            def _(pool):
                pool.wait_ge(w_in, counted(16 * LOADS))
                run(pool, pool_step)

            @block.vector
            def _(dve):
                nc.vector.memset(router[:], 0.0)
                nc.vector.memset(router_b[:], 0.0)
                nc.vector.memset(eb[:], 0.0).then_inc(zeroed, 1)
                nc.vector.memset(weight[:], 0.0).then_inc(zeroed, 1)
                dve.wait_ge(w_in, counted(16 * LOADS))
                dve.wait_ge(zeroed, counted(2))
                run(dve, dve_step)

            @block.scalar
            def _(act):
                act.wait_ge(w_in, counted(16 * LOADS))
                run(act, act_step)

            @block.tensor
            def _(pe):
                pe.wait_ge(w_in, counted(16 * LOADS))
                run(pe, pe_step)


def program(nc, dram):
    with ExitStack() as ctx:
        k = Core(nc, ctx, dram)
        load_constants(k)
        k.end_phase()
        with ExitStack() as part:
            bias = k.sb(part, "bias", [P, 2, NH, N])
            bias_pass(k, bias)
            k.end_phase()
            attention(k, bias)
            k.end_phase()
        with ExitStack() as part:
            kept_top = k.sb(part, "kept_top", [P, TILES // 8 * K0])
            kept_at = k.sb(part, "kept_at", [P, TILES // 8 * K0], U32)
            kept_sum = k.sb(part, "kept_sum", [P, TILES // 8])
            gate_pass(k, kept_top, kept_at, kept_sum)
            k.end_phase()
            experts(k, kept_top, kept_at, kept_sum)
            k.end_phase()
        spectra(k)
        layer1(k)


def shape_constants():
    mode = np.arange(NM)
    angle = 2 * np.pi * np.outer(np.arange(N), mode) / N
    forward = np.concatenate([np.cos(angle), -np.sin(angle)], 1) / np.sqrt(N)
    twice = np.where(mode == 0, 1.0, 2.0)[:, None] / np.sqrt(N)
    inverse = np.concatenate([twice * np.cos(angle.T), -twice * np.sin(angle.T)], 0)
    diagonal = np.zeros((4, M2, 4, N))
    for a in range(4):
        diagonal[a, :, a] = inverse
    step, half = np.arange(TILES // 8 * K0)[None] // K0, np.arange(P)[:, None] // E0
    tables = {
        "identity": np.eye(P),
        "offs": step * 1024 + half * 512,
        "iota": np.broadcast_to(np.arange(TILES // 8 * 2 * K0), (E0, TILES // 8 * 2 * K0)),
        "upper": np.triu(np.ones((E0, E0)), 1),
        "forward": forward,
        "inverse": diagonal.reshape(P, 4 * N),
        "iota8": np.broadcast_to(np.tile(np.arange(E1), 4), (P, 4 * E1)),
    }
    return {n: np.ascontiguousarray(a, dtype=np.float32) for n, a in tables.items()}


def kernel(**inputs):
    import concourse.bacc as bacc
    from concourse.bass_utils import run_bass_kernel_spmd

    arrays = {n: np.ascontiguousarray(a) for n, a in inputs.items() if n != "L1_conv_ff_b0"}
    arrays["L1_conv_ff_b0_t"] = np.ascontiguousarray(np.asarray(inputs["L1_conv_ff_b0"]).reshape(H1 // P, P).T)
    arrays.update(shape_constants())
    nc = bacc.Bacc("TRN2", target_bir_lowering=False, num_devices=1)
    dram = {n: nc.dram_tensor(n, a.shape, F32, kind="ExternalInput").ap() for n, a in arrays.items()}
    dram["x1"] = nc.dram_tensor("x1", (TOK, C), F32, kind="Internal").ap()
    dram["bias"] = nc.dram_tensor("bias_rows", (NH, N, N), F32, kind="Internal").ap()
    for n in ("z1", "z2"):
        dram[n] = nc.dram_tensor(n, (2, NM, N, C), F32, kind="Internal").ap()
    dram["out"] = nc.dram_tensor("out", (1, N, N, C), F32, kind="ExternalOutput").ap()
    program(nc, dram)
    return run_bass_kernel_spmd(nc, [arrays], core_ids=[0]).results[0]["out"]
```
